# Optimizing a Trainium2 kernel written in Bass

```python
import numpy as np
import jax
import jax.numpy as jnp

def _softmax(x, axis=-1):
    return jax.nn.softmax(x, axis=axis)

def _gelu(x):
    return jax.nn.gelu(x, approximate=True)

def _silu(x):
    return jax.nn.silu(x)

def _sigmoid(x):
    return jax.nn.sigmoid(x)

def _layernorm(x, axis=-1, eps=1e-05):
    m = jnp.mean(x, axis=axis, keepdims=True)
    v = jnp.var(x, axis=axis, keepdims=True)
    return (x - m) / jnp.sqrt(v + eps)

def _scatter_add(tgt, idx, src, axis=0):
    return tgt.at[idx].add(src)

def _segment_sum(src, seg, n):
    return jax.ops.segment_sum(src, seg, n)
kernel_name = 'mk_vit_tower_cls_d2_tok_img1024_r4_97586e'

def setup_inputs(seed: int=0):
    np.random.seed(seed)
    _w = jnp.asarray

    def _rec_inputs():
        import jax
        import jax.numpy as jnp
        _rk = jax.random.key(seed)
        x = -0.000392918 + 0.999932 * jax.random.normal(jax.random.fold_in(_rk, 1), (8, 256, 256, 1), jnp.float32)
        cls_tok = 0.02 * jax.random.normal(jax.random.fold_in(_rk, 5), (1, 1, 256), jnp.float32)
        return (x, cls_tok)
    x, cls_tok = _rec_inputs()

    def _L0_tok_setup():
        import jax, jax.numpy as jnp
        import numpy as np
        INV_SQRT2 = 0.7071067811865476
        LEVEL = 3

        def _split(x, axis):
            ax = axis % x.ndim
            sl0 = [slice(None)] * x.ndim
            sl0[ax] = slice(0, None, 2)
            sl1 = [slice(None)] * x.ndim
            sl1[ax] = slice(1, None, 2)
            x0, x1 = (x[tuple(sl0)], x[tuple(sl1)])
            return ((x0 + x1) * INV_SQRT2, (x0 - x1) * INV_SQRT2)

        def _merge(lo, hi, axis):
            ax = axis % lo.ndim
            e = (lo + hi) * INV_SQRT2
            o = (lo - hi) * INV_SQRT2
            s = jnp.stack([e, o], axis=ax + 1)
            shape = list(lo.shape)
            shape[ax] *= 2
            return s.reshape(shape)

        def _dwt2(x):
            lo, hi = _split(x, -1)
            a, h = _split(lo, -2)
            v, d = _split(hi, -2)
            return (a, h, v, d)

        def _idwt2(a, h, v, d):
            lo = _merge(a, h, -2)
            hi = _merge(v, d, -2)
            return _merge(lo, hi, -1)
        key = jax.random.key(seed)
        ks = jax.random.split(key, 8)
        B, H, W = (16, 256, 256)
        x = jax.random.normal(ks[0], (B, H, W, 1), dtype=jnp.float32)
        na = H // 8 * (W // 8)
        n2 = H // 4 * (W // 4)
        n1 = H // 2 * (W // 2)
        scale = 0.02
        Wa = jax.random.normal(ks[1], (na, 1), dtype=jnp.float32) * scale
        ba = jnp.zeros((1,), jnp.float32)
        Wd1 = jax.random.normal(ks[2], (3 * na, 3), dtype=jnp.float32) * scale
        bd1 = jnp.zeros((3,), jnp.float32)
        Wd2 = jax.random.normal(ks[3], (3 * n2, 3), dtype=jnp.float32) * scale
        bd2 = jnp.zeros((3,), jnp.float32)
        Wd3 = jax.random.normal(ks[4], (3 * n1, 3), dtype=jnp.float32) * scale
        bd3 = jnp.zeros((3,), jnp.float32)
        return {'x': x, 'Wa': Wa, 'ba': ba, 'Wd1': Wd1, 'bd1': bd1, 'Wd2': Wd2, 'bd2': bd2, 'Wd3': Wd3, 'bd3': bd3}
    _L0_tok_all = _L0_tok_setup()
    _L0_tok_in = {k: v for k, v in _L0_tok_all.items() if k in ('Wa', 'ba', 'Wd1', 'bd1', 'Wd2', 'bd2', 'Wd3', 'bd3')}
    del _L0_tok_all

    def _L0_attn_setup():
        import math
        import jax, jax.numpy as jnp
        import numpy as np
        N_HEAD = 16

        def _rope_cos_sin(l, head_dim):
            scale = jnp.arange(0, head_dim, 2, dtype=jnp.float32)[:head_dim // 2]
            freqs = 1.0 / 10000.0 ** scale
            angles = jnp.arange(l, dtype=jnp.float32)[:, None] * freqs[None, :]
            return (jnp.cos(angles), jnp.sin(angles))

        def _rope_apply(x, cos, sin):
            b, l, h, hd = x.shape
            xp = x.astype(jnp.float32).reshape(b, l, h, hd // 2, 2)
            xr, xi = (xp[..., 0], xp[..., 1])
            c = cos[None, :, None, :]
            s = sin[None, :, None, :]
            out_r = xr * c - xi * s
            out_i = xr * s + xi * c
            out = jnp.stack([out_r, out_i], axis=-1).reshape(b, l, h, hd)
            return out.astype(x.dtype)
        key = jax.random.key(seed)
        ks = jax.random.split(key, 9)
        b, l, d = (2, 512, 256)
        sc = 1.0 / math.sqrt(d)
        inp = {'x': jax.random.normal(ks[0], (b, l, d), dtype=jnp.float32), 'Wq': jax.random.normal(ks[1], (d, d), dtype=jnp.float32) * sc, 'bq': jnp.zeros((d,), dtype=jnp.float32), 'Wk': jax.random.normal(ks[2], (d, d), dtype=jnp.float32) * sc, 'bk': jnp.zeros((d,), dtype=jnp.float32), 'Wv': jax.random.normal(ks[3], (d, d), dtype=jnp.float32) * sc, 'bv': jnp.zeros((d,), dtype=jnp.float32), 'Wo': jax.random.normal(ks[4], (d, d), dtype=jnp.float32) * sc, 'bo': jnp.zeros((d,), dtype=jnp.float32)}
        return inp
    _L0_attn_all = _L0_attn_setup()
    _L0_attn_in = {k: v for k, v in _L0_attn_all.items() if k in ('Wq', 'bq', 'Wk', 'bk', 'Wv', 'bv', 'Wo', 'bo')}
    del _L0_attn_all

    def _L0_ffn_setup():
        import jax, jax.numpy as jnp
        import numpy as np
        CAPACITY_FACTOR = 1.25
        key = jax.random.key(seed)
        k1, k2, k3, k4 = jax.random.split(key, 4)
        B, T, D, F, E = (4, 1024, 256, 1024, 8)
        s = 0.02
        return {'x': jax.random.normal(k1, (B, T, D), dtype=jnp.float32), 'wg': jax.random.normal(k2, (D, E), dtype=jnp.float32) * s, 'W1': jax.random.normal(k3, (E, D, F), dtype=jnp.float32) * s, 'b1': jnp.zeros((E, F), dtype=jnp.float32), 'W2': jax.random.normal(k4, (E, F, D), dtype=jnp.float32) * s, 'b2': jnp.zeros((E, D), dtype=jnp.float32)}
    _L0_ffn_all = _L0_ffn_setup()
    _L0_ffn_in = {k: v for k, v in _L0_ffn_all.items() if k in ('wg', 'W1', 'b1', 'W2', 'b2')}
    del _L0_ffn_all

    def _L1_attn_setup():
        import math
        import jax, jax.numpy as jnp
        import numpy as np
        NUM_BUCKETS = 32
        MAX_DISTANCE = 128
        HEADS = 8
        DIM_HEAD = 64

        def _relative_position_bucket(rel_pos, num_buckets=NUM_BUCKETS, max_distance=MAX_DISTANCE):
            n = jnp.maximum(-rel_pos, 0)
            max_exact = num_buckets // 2
            is_small = n < max_exact
            val_if_large = max_exact + (jnp.log(jnp.maximum(n, 1).astype(jnp.float32) / max_exact) / math.log(max_distance / max_exact) * (num_buckets - max_exact)).astype(jnp.int32)
            val_if_large = jnp.minimum(val_if_large, num_buckets - 1)
            return jnp.where(is_small, n, val_if_large)
        key = jax.random.key(seed)
        ks = jax.random.split(key, 5)
        b, n, dim = (2, 512, 256)
        inner = HEADS * DIM_HEAD
        return {'x': jax.random.normal(ks[0], (b, n, dim), dtype=jnp.float32), 'Wq': jax.random.normal(ks[1], (dim, inner), dtype=jnp.float32) * dim ** (-0.5), 'Wkv': jax.random.normal(ks[2], (dim, 2 * inner), dtype=jnp.float32) * dim ** (-0.5), 'Wo': jax.random.normal(ks[3], (inner, dim), dtype=jnp.float32) * inner ** (-0.5), 'bo': jnp.zeros((dim,), dtype=jnp.float32), 'rel_emb': jax.random.normal(ks[4], (NUM_BUCKETS, HEADS), dtype=jnp.float32) * 0.02}
    _L1_attn_all = _L1_attn_setup()
    _L1_attn_in = {k: v for k, v in _L1_attn_all.items() if k in ('Wq', 'Wkv', 'Wo', 'bo', 'rel_emb')}
    del _L1_attn_all

    def _L1_ffn_setup():
        import jax, jax.numpy as jnp
        import numpy as np
        MANT_BITS = 8
        _PWL_X = jnp.linspace(-4.0, 4.0, 33, dtype=jnp.float32)
        _PWL_Y = 0.5 * _PWL_X * (1.0 + jax.lax.erf(_PWL_X / jnp.sqrt(jnp.float32(2.0))))

        def float2fix(x, mantissa_bits):
            s = jnp.float32(2.0 ** mantissa_bits)
            q = jnp.round(x * s) / s
            return x + jax.lax.stop_gradient(q - x)

        def pwlin_gelu_basic(x, mantissa_bits_in, mantissa_bits_out):
            xq = float2fix(x, mantissa_bits_in)
            y = jnp.interp(xq, _PWL_X, _PWL_Y)
            y = jnp.where(xq > 4.0, xq, jnp.where(xq < -4.0, jnp.float32(0.0), y))
            return float2fix(y, mantissa_bits_out)
        key = jax.random.key(seed)
        k_x, k_w1, k_b1, k_w2, k_b2 = jax.random.split(key, 5)
        dim, ff_dim = (256, 1024)
        B, S = (32, 128)
        sc1 = 1.0 / np.sqrt(dim)
        sc2 = 1.0 / np.sqrt(ff_dim)
        return {'x': jax.random.normal(k_x, (B, S, dim), dtype=jnp.float32), 'w1': jax.random.uniform(k_w1, (dim, ff_dim), jnp.float32, -sc1, sc1), 'b1': jax.random.uniform(k_b1, (ff_dim,), jnp.float32, -sc1, sc1), 'w2': jax.random.uniform(k_w2, (ff_dim, dim), jnp.float32, -sc2, sc2), 'b2': jax.random.uniform(k_b2, (dim,), jnp.float32, -sc2, sc2)}
    _L1_ffn_all = _L1_ffn_setup()
    _L1_ffn_in = {k: v for k, v in _L1_ffn_all.items() if k in ('w1', 'b1', 'w2', 'b2')}
    del _L1_ffn_all
    return {'x': x, 'cls_tok': cls_tok, 'L0_tok_Wa': _L0_tok_in['Wa'], 'L0_tok_ba': _L0_tok_in['ba'], 'L0_tok_Wd1': _L0_tok_in['Wd1'], 'L0_tok_bd1': _L0_tok_in['bd1'], 'L0_tok_Wd2': _L0_tok_in['Wd2'], 'L0_tok_bd2': _L0_tok_in['bd2'], 'L0_tok_Wd3': _L0_tok_in['Wd3'], 'L0_tok_bd3': _L0_tok_in['bd3'], 'L0_attn_Wq': _L0_attn_in['Wq'], 'L0_attn_bq': _L0_attn_in['bq'], 'L0_attn_Wk': _L0_attn_in['Wk'], 'L0_attn_bk': _L0_attn_in['bk'], 'L0_attn_Wv': _L0_attn_in['Wv'], 'L0_attn_bv': _L0_attn_in['bv'], 'L0_attn_Wo': _L0_attn_in['Wo'], 'L0_attn_bo': _L0_attn_in['bo'], 'L0_ffn_wg': _L0_ffn_in['wg'], 'L0_ffn_W1': _L0_ffn_in['W1'], 'L0_ffn_b1': _L0_ffn_in['b1'], 'L0_ffn_W2': _L0_ffn_in['W2'], 'L0_ffn_b2': _L0_ffn_in['b2'], 'L1_attn_Wq': _L1_attn_in['Wq'], 'L1_attn_Wkv': _L1_attn_in['Wkv'], 'L1_attn_Wo': _L1_attn_in['Wo'], 'L1_attn_bo': _L1_attn_in['bo'], 'L1_attn_rel_emb': _L1_attn_in['rel_emb'], 'L1_ffn_w1': _L1_ffn_in['w1'], 'L1_ffn_b1': _L1_ffn_in['b1'], 'L1_ffn_w2': _L1_ffn_in['w2'], 'L1_ffn_b2': _L1_ffn_in['b2']}

def reference(x, cls_tok, L0_tok_Wa, L0_tok_ba, L0_tok_Wd1, L0_tok_bd1, L0_tok_Wd2, L0_tok_bd2, L0_tok_Wd3, L0_tok_bd3, L0_attn_Wq, L0_attn_bq, L0_attn_Wk, L0_attn_bk, L0_attn_Wv, L0_attn_bv, L0_attn_Wo, L0_attn_bo, L0_ffn_wg, L0_ffn_W1, L0_ffn_b1, L0_ffn_W2, L0_ffn_b2, L1_attn_Wq, L1_attn_Wkv, L1_attn_Wo, L1_attn_bo, L1_attn_rel_emb, L1_ffn_w1, L1_ffn_b1, L1_ffn_w2, L1_ffn_b2):
    import jax
    import jax.numpy as jnp

    def _L0_tok_ref(x, Wa, ba, Wd1, bd1, Wd2, bd2, Wd3, bd3):
        import jax, jax.numpy as jnp
        import numpy as np
        INV_SQRT2 = 0.7071067811865476
        LEVEL = 3

        def _split(x, axis):
            ax = axis % x.ndim
            sl0 = [slice(None)] * x.ndim
            sl0[ax] = slice(0, None, 2)
            sl1 = [slice(None)] * x.ndim
            sl1[ax] = slice(1, None, 2)
            x0, x1 = (x[tuple(sl0)], x[tuple(sl1)])
            return ((x0 + x1) * INV_SQRT2, (x0 - x1) * INV_SQRT2)

        def _merge(lo, hi, axis):
            ax = axis % lo.ndim
            e = (lo + hi) * INV_SQRT2
            o = (lo - hi) * INV_SQRT2
            s = jnp.stack([e, o], axis=ax + 1)
            shape = list(lo.shape)
            shape[ax] *= 2
            return s.reshape(shape)

        def _dwt2(x):
            lo, hi = _split(x, -1)
            a, h = _split(lo, -2)
            v, d = _split(hi, -2)
            return (a, h, v, d)

        def _idwt2(a, h, v, d):
            lo = _merge(a, h, -2)
            hi = _merge(v, d, -2)
            return _merge(lo, hi, -1)
        img = x[..., 0]
        B = img.shape[0]
        details = []
        cur = img
        for _ in range(LEVEL):
            cur, h, v, d = _dwt2(cur)
            details.append((h, v, d))
        aw = jax.nn.sigmoid(cur.reshape(B, -1) @ Wa + ba)
        rec = cur * aw[:, :, None]
        det_params = [(Wd1, bd1), (Wd2, bd2), (Wd3, bd3)]
        for (h, v, d), (Wd, bd) in zip(reversed(details), det_params):
            flat = jnp.stack([h, v, d], axis=1).reshape(B, -1)
            w = jax.nn.softmax(flat @ Wd + bd, axis=-1)
            rec = _idwt2(rec, h * w[:, 0, None, None], v * w[:, 1, None, None], d * w[:, 2, None, None])
        return rec

    def _L0_attn_ref(x, Wq, bq, Wk, bk, Wv, bv, Wo, bo):
        import math
        import jax, jax.numpy as jnp
        import numpy as np
        N_HEAD = 16

        def _rope_cos_sin(l, head_dim):
            scale = jnp.arange(0, head_dim, 2, dtype=jnp.float32)[:head_dim // 2]
            freqs = 1.0 / 10000.0 ** scale
            angles = jnp.arange(l, dtype=jnp.float32)[:, None] * freqs[None, :]
            return (jnp.cos(angles), jnp.sin(angles))

        def _rope_apply(x, cos, sin):
            b, l, h, hd = x.shape
            xp = x.astype(jnp.float32).reshape(b, l, h, hd // 2, 2)
            xr, xi = (xp[..., 0], xp[..., 1])
            c = cos[None, :, None, :]
            s = sin[None, :, None, :]
            out_r = xr * c - xi * s
            out_i = xr * s + xi * c
            out = jnp.stack([out_r, out_i], axis=-1).reshape(b, l, h, hd)
            return out.astype(x.dtype)
        b, l, d = x.shape
        h = N_HEAD
        hd = d // h
        q = (x @ Wq + bq).reshape(b, l, h, hd)
        k = (x @ Wk + bk).reshape(b, l, h, hd)
        v = (x @ Wv + bv).reshape(b, l, h, hd)
        cos, sin = _rope_cos_sin(l, hd)
        q = _rope_apply(q, cos, sin)
        k = _rope_apply(k, cos, sin)
        score = jnp.einsum('blhd,bmhd->bhlm', q, k) / math.sqrt(hd)
        ctx = jnp.einsum('bhlm,bmhd->blhd', score, v).reshape(b, l, d)
        return ctx @ Wo + bo

    def _L0_ffn_ref(x, wg, W1, b1, W2, b2):
        import jax, jax.numpy as jnp
        import numpy as np
        CAPACITY_FACTOR = 1.25
        B, T, D = x.shape
        E = wg.shape[1]
        N = B * T
        capacity = int(N / E * CAPACITY_FACTOR) + 1
        xf = x.reshape(N, D)
        logits = xf @ wg
        scores = jax.nn.softmax(logits, axis=-1)
        top1 = jnp.argmax(scores, axis=-1)
        combine_w = jnp.take_along_axis(scores, top1[:, None], axis=1)[:, 0]
        oh = jax.nn.one_hot(top1, E, dtype=jnp.int32)
        rank = jnp.take_along_axis(jnp.cumsum(oh, axis=0), top1[:, None], axis=1)[:, 0] - 1
        valid = rank < capacity
        trash = E * capacity
        slot = jnp.where(valid, top1 * capacity + rank, trash)
        buf = jnp.zeros((E * capacity + 1, D), dtype=x.dtype).at[slot].set(xf)
        eb = buf[:E * capacity].reshape(E, capacity, D)
        h = jax.nn.gelu(jnp.einsum('ecd,edf->ecf', eb, W1) + b1[:, None, :], approximate=False)
        y = jnp.einsum('ecf,efd->ecd', h, W2) + b2[:, None, :]
        yf = y.reshape(E * capacity, D)
        gathered = yf[jnp.minimum(slot, E * capacity - 1)]
        out_flat = jnp.where(valid[:, None], gathered, 0.0) * combine_w[:, None]
        return out_flat.reshape(B, T, D)

    def _L1_attn_ref(x, Wq, Wkv, Wo, bo, rel_emb):
        import math
        import jax, jax.numpy as jnp
        import numpy as np
        NUM_BUCKETS = 32
        MAX_DISTANCE = 128
        HEADS = 8
        DIM_HEAD = 64

        def _relative_position_bucket(rel_pos, num_buckets=NUM_BUCKETS, max_distance=MAX_DISTANCE):
            n = jnp.maximum(-rel_pos, 0)
            max_exact = num_buckets // 2
            is_small = n < max_exact
            val_if_large = max_exact + (jnp.log(jnp.maximum(n, 1).astype(jnp.float32) / max_exact) / math.log(max_distance / max_exact) * (num_buckets - max_exact)).astype(jnp.int32)
            val_if_large = jnp.minimum(val_if_large, num_buckets - 1)
            return jnp.where(is_small, n, val_if_large)
        b, n, dim = x.shape
        h, d = (HEADS, DIM_HEAD)
        scale = d ** (-0.5)
        bias_scale = d ** 0.5
        q = x @ Wq
        kv = x @ Wkv
        k, v = jnp.split(kv, 2, axis=-1)

        def to_heads(t):
            return t.reshape(b, n, h, d).transpose(0, 2, 1, 3)
        q, k, v = (to_heads(q) * scale, to_heads(k), to_heads(v))
        sim = jnp.einsum('bhid,bhjd->bhij', q, k)
        pos = jnp.arange(n)
        rel_pos = pos[None, :] - pos[:, None]
        buckets = _relative_position_bucket(rel_pos)
        bias = rel_emb[buckets]
        bias = bias.transpose(2, 0, 1)[None] * bias_scale
        sim = sim + bias
        causal_mask = jnp.triu(jnp.ones((n, n), dtype=bool), k=1)
        sim = jnp.where(causal_mask, -jnp.finfo(sim.dtype).max, sim)
        attn = jax.nn.softmax(sim, axis=-1)
        out = jnp.einsum('bhij,bhjd->bhid', attn, v)
        out = out.transpose(0, 2, 1, 3).reshape(b, n, h * d)
        return out @ Wo + bo

    def _L1_ffn_ref(x, w1, b1, w2, b2):
        import jax, jax.numpy as jnp
        import numpy as np
        MANT_BITS = 8
        _PWL_X = jnp.linspace(-4.0, 4.0, 33, dtype=jnp.float32)
        _PWL_Y = 0.5 * _PWL_X * (1.0 + jax.lax.erf(_PWL_X / jnp.sqrt(jnp.float32(2.0))))

        def float2fix(x, mantissa_bits):
            s = jnp.float32(2.0 ** mantissa_bits)
            q = jnp.round(x * s) / s
            return x + jax.lax.stop_gradient(q - x)

        def pwlin_gelu_basic(x, mantissa_bits_in, mantissa_bits_out):
            xq = float2fix(x, mantissa_bits_in)
            y = jnp.interp(xq, _PWL_X, _PWL_Y)
            y = jnp.where(xq > 4.0, xq, jnp.where(xq < -4.0, jnp.float32(0.0), y))
            return float2fix(y, mantissa_bits_out)
        h = jnp.einsum('bsd,df->bsf', x, w1) + b1
        h = float2fix(h, MANT_BITS)
        h = pwlin_gelu_basic(h, MANT_BITS, MANT_BITS)
        h = float2fix(h, MANT_BITS)
        out = jnp.einsum('bsf,fd->bsd', h, w2) + b2
        return float2fix(out, MANT_BITS)
    h = _L0_tok_ref(x, L0_tok_Wa, L0_tok_ba, L0_tok_Wd1, L0_tok_bd1, L0_tok_Wd2, L0_tok_bd2, L0_tok_Wd3, L0_tok_bd3)
    h = jnp.concatenate([jnp.broadcast_to(cls_tok, (h.shape[0], 1, h.shape[2])), h], axis=1)
    h = h + _L0_attn_ref(_layernorm(h, axis=-1), L0_attn_Wq, L0_attn_bq, L0_attn_Wk, L0_attn_bk, L0_attn_Wv, L0_attn_bv, L0_attn_Wo, L0_attn_bo)
    h = h + _L0_ffn_ref(_layernorm(h, axis=-1), L0_ffn_wg, L0_ffn_W1, L0_ffn_b1, L0_ffn_W2, L0_ffn_b2)
    h = h + _L1_attn_ref(_layernorm(h, axis=-1), L1_attn_Wq, L1_attn_Wkv, L1_attn_Wo, L1_attn_bo, L1_attn_rel_emb)
    h = h + _L1_ffn_ref(_layernorm(h, axis=-1), L1_ffn_w1, L1_ffn_b1, L1_ffn_w2, L1_ffn_b2)
    return h

_drawn_inputs = setup_inputs


def setup_inputs(seed=0):
    import zlib

    import numpy as np

    out = dict(_drawn_inputs(seed))
    spreads = {'L0_tok_bd1': (0.0, 0.431),
     'L0_tok_bd2': (0.0, 0.469),
     'L0_tok_bd3': (0.0, 0.573),
     'L0_attn_bq': (0.0, 0.1),
     'L0_attn_bk': (0.0, 0.1),
     'L0_attn_bv': (0.0, 0.1),
     'L0_attn_bo': (0.0, 0.8),
     'L0_ffn_b1': (0.0, 0.8),
     'L0_ffn_b2': (0.0, 0.8),
     'L1_attn_bo': (0.0, 2.0)}
    factors = {'L0_ffn_wg': 8.0,
     'L0_ffn_W1': 8.0,
     'L0_ffn_W2': 8.0,
     'L1_attn_Wq': 7.728,
     'L1_attn_Wkv': 5.782,
     'L1_attn_Wo': 5.852,
     'L1_attn_rel_emb': 8.0,
     'L1_ffn_w1': 8.0,
     'L1_ffn_b1': 22.112,
     'L1_ffn_w2': 8.0,
     'L1_ffn_b2': 64.0}
    for name, (base, spread) in spreads.items():
        noise = np.random.default_rng([zlib.crc32(name.encode()), seed]).standard_normal(out[name].shape)
        drawn = base * np.exp(spread * noise) if base else spread * noise
        out[name] = jnp.asarray(drawn.astype(out[name].dtype))
    for name, factor in factors.items():
        out[name] = (out[name] * factor).astype(out[name].dtype)
    return out
```

```python
from contextlib import ExitStack

import numpy as np

import concourse.bass as bass
from concourse import mybir

ALU = mybir.AluOpType
ACT = mybir.ActivationFunctionType
AX = mybir.AxisListType
F32 = mybir.dt.float32
I32 = mybir.dt.int32
U32 = mybir.dt.uint32

P = 128
B = 8
ROWS = 256
D = 256
POS = ROWS + 1
KD = D // P
TPB = ROWS // P
NT = B * TPB
NTC = NT + 1
N_TOK = B * POS
EPS = 1e-5
HD0 = 16
E = 8
F = 1024
KF = F // P
CAP = int(N_TOK / E * 1.25) + 1
MT = 3
MR = -(-CAP // MT)
SLOTS = E * CAP
FAR = 1 << 20
H1 = 8
HD1 = 64
INNER = H1 * HD1
KI = INNER // P
BUCKETS = 32
SCOLS = (1 + P) + POS
MASKED = -1e30
ROUND = 49152.0

MATS = {}


def _columns(spec):
    at = 0
    for name, n in spec:
        MATS[name] = (at, n)
        at += n
    return at


N_MATS = _columns([("ident", P), ("flip", P), ("ones", P), ("tri", P), ("haar2", P), ("unhaar2", P), ("haar3", 64),
                   ("unhaar3", 64), ("blocks", KD * P), ("after", B * B), ("tri8", B), ("order", NTC * E),
                   ("first_slot", NTC * E), ("before", NT * E), ("is_cls", 1), ("neg_half", 2)])


def _shape_constants():
    f = np.float32
    m = np.zeros((P, N_MATS), f)

    def put(name, a):
        at, n = MATS[name]
        m[:a.shape[0], at:at + n] = a.reshape(a.shape[0], n)

    put("ident", np.eye(P))
    put("flip", np.eye(P)[::-1])
    put("ones", np.ones((P, P)))
    put("tri", np.triu(np.ones((P, P))))

    def haar(n):
        a = np.zeros((n, n))
        for i in range(n // 2):
            a[2 * i, i] = a[2 * i + 1, i] = a[2 * i, n // 2 + i] = 1
            a[2 * i + 1, n // 2 + i] = -1
        return a

    put("haar2", haar(P))
    put("unhaar2", 0.25 * haar(P).T)
    put("haar3", haar(64))
    put("unhaar3", 0.25 * haar(64).T)
    heads = np.arange(P) // HD0
    block = (heads[:, None] == heads[None, :]) / np.sqrt(HD0)
    put("blocks", np.concatenate([block] * KD, 1))
    after = np.zeros((P, B, B))
    for j in range(B):
        after[:, j, j + 1:] = 1
    put("after", after)
    put("tri8", np.triu(np.ones((B, B))))
    put("order", np.broadcast_to(np.arange(E, 0, -1), (P, NTC, E)))
    put("first_slot", np.broadcast_to(np.arange(E) * CAP - 1, (P, NTC, E)))
    before = np.zeros((B, NT, E))
    for b in range(B):
        before[b, b * TPB:] = 1
    put("before", before)
    put("is_cls", (np.arange(P) < B).astype(f)[:, None])
    put("neg_half", np.full((P, 2), -0.5))

    freqs = (f(1.0) / np.power(f(10000.0), np.arange(0, HD0, 2, dtype=f))).astype(f)
    angle = (np.arange(POS, dtype=f)[:, None] * freqs[None, :]).astype(f)[1:]
    cos = np.repeat(np.cos(angle), 2, axis=1).astype(f)
    sin = np.stack([-np.sin(angle), np.sin(angle)], -1).reshape(ROWS, HD0).astype(f)
    cos, sin = (np.tile(a, (1, D // HD0)) for a in (cos, sin))
    rope_t = np.stack([cos.T.reshape(KD, P, ROWS), sin.T.reshape(KD, P, ROWS)])
    rope_q = np.ascontiguousarray(rope_t.transpose(2, 0, 1, 3)).astype(f)
    rope_k = np.stack([cos.reshape(TPB, P, D), sin.reshape(TPB, P, D)])
    rope_k = np.ascontiguousarray(rope_k.transpose(2, 0, 1, 3)).astype(f)

    n = (ROWS - np.arange(2 * ROWS)).astype(np.int64)
    exact = BUCKETS // 2
    big = exact + (np.log(np.maximum(n, 1).astype(f) / exact) / np.log(128 / exact)
                   * (BUCKETS - exact)).astype(np.int32)
    bucket = np.where(n < exact, n, np.minimum(big, BUCKETS - 1))
    hot = np.zeros((BUCKETS + 1, 2 * ROWS), f)
    for v in range(2 * ROWS):
        hot[bucket[v] if n[v] >= 0 else BUCKETS, v] = 1
    far = np.full((1, H1), MASKED, f)
    return {"c_mats": m, "c_rope_q": rope_q, "c_rope_k": rope_k, "c_buckets": hot, "c_masked": far}


def rep(ap, axis, n):
    wide = ap.unsqueeze(axis)
    shape = list(wide.shape)
    shape[axis] = n
    return wide.broadcast_to(shape)


def vit_tower_kernel(nc, dram, out):
    ctx = ExitStack()
    with ctx:
        def sem(name):
            return ctx.enter_context(nc.semaphore(name))

        def sb(name, shape, dt=F32, scope=ctx):
            return scope.enter_context(nc.sbuf_tensor(name, shape, dt))

        early = []

        def early_sem(name):
            early.append(nc.alloc_semaphore(name=name))
            return early[-1]

        bank = [ctx.enter_context(nc.psum_tensor(f"bank{i}", [P, 512], F32)) for i in range(3)]
        kvbank = ctx.enter_context(nc.psum_tensor("kvbank", [P, 2, 512], F32))
        bank += [ctx.enter_context(nc.psum_tensor(f"bank{i}", [P, 512], F32)) for i in range(3, 6)]

        mats = sb("mats", [P, N_MATS])

        def mat(name, parts=P):
            at, n = MATS[name]
            return mats[0:parts, at:at + n]

        ident, ones = mat("ident"), mat("ones")

        hrow = sb("hrow", [P, NT, D])
        hcls = sb("hcls", [B, D])
        w1e = [sb(f"w1e{i}", [P, KD, F]) for i in range(2)]
        w2e = [sb(f"w2e{i}", [P, KF, D]) for i in range(2)]
        wq1 = sb("wq1", [P, KD, INNER])
        wkv1 = sb("wkv1", [P, KD, 2 * INNER])
        wo1 = sb("wo1", [P, KI, D])
        bo1 = sb("bo1", [P, D])
        toeplitz = sb("toeplitz", [P, H1, SCOLS])
        xrow = sb("xrow", [P, NT, D])
        xcls = sb("xcls", [B, D])
        to_slot = sb("to_slot", [P, NTC], U32)
        from_slot = sb("from_slot", [P, NTC], U32)
        weight = sb("weight", [P, NTC])

        buf = nc.dram_tensor("expert_in", [SLOTS + MT * MR - CAP, D], F32, kind="Internal").ap()
        ybuf = nc.dram_tensor("expert_out", [SLOTS, D], F32, kind="Internal").ap()
        bias_rev = nc.dram_tensor("bias_rev", [H1, 2 * ROWS], F32, kind="Internal").ap()

        mats_in = sem("mats_in")
        w1e_in = [sem(f"w1e_in{i}") for i in range(2)]
        w2e_in = [sem(f"w2e_in{i}") for i in range(2)]
        buf_zeroed = sem("buf_zeroed")
        l0_in = sem("l0_in")
        l1_in = sem("l1_in")
        out_stored = sem("out_stored")
        stored = 0

        def apart(eng):
            eng.wait_ge(mats_in, 16)

        def waits_apart(eng, *waits):
            waits = [(which, value if isinstance(value, int) else eng.to_reg(value)) for which, value in waits]
            if not all(isinstance(value, int) for _, value in waits):
                apart(eng)
            for which, value in waits:
                eng.wait_ge(which, value)

        def load_expert(eng, e):
            s = e % 2
            eng.dma_start(w1e[s][:, :, :], dram["L0_ffn_W1"][e].rearrange("(k p) f -> p k f", p=P)).then_inc(w1e_in[s], 16)
            eng.dma_start(w2e[s][:, :, :], dram["L0_ffn_W2"][e].rearrange("(k p) d -> p k d", p=P)).then_inc(w2e_in[s], 16)

        attn0 = ExitStack()
        wq0 = sb("wq0", [P, KD, D], scope=attn0)
        wqs0 = sb("wqs0", [P, KD, D], scope=attn0)
        wkv0 = sb("wkv0", [P, KD, 2 * D], scope=attn0)
        wo0 = sb("wo0", [P, KD, D], scope=attn0)
        wg = sb("wg", [P, KD, E], scope=attn0)
        ropeq = sb("ropeq", [P, 2, KD, ROWS], scope=attn0)
        ropek = sb("ropek", [P, 2, TPB, D], scope=attn0)
        bqm = sb("bqm", [P, KD], scope=attn0)
        bqs = sb("bqs", [P, KD], scope=attn0)
        bkv = sb("bkv", [P, 2 * D], scope=attn0)
        bo0 = sb("bo0", [P, D], scope=attn0)
        clsb = sb("clsb", [B, D], scope=attn0)
        emb = sb("emb", [BUCKETS + 1, H1], scope=attn0)
        hot = sb("hot", [BUCKETS + 1, 2 * ROWS], scope=attn0)
        bias = {n: early_sem("bias_" + n) for n in "emb_in emb brev_ps brev brev_out rev_in flip_ps flip_out".split()}

        tok = ExitStack()
        img = sb("img", [P, B, 2, D], scope=tok)
        lohi = sb("lohi", [P, B, 2, 2, P], scope=tok)
        a1 = sb("a1", [P, B, P], scope=tok)
        d1 = sb("d1", [P, B, 3, P], scope=tok)
        wd3 = sb("wd3", [P, 3, 3 * P], scope=tok)
        wd2 = sb("wd2", [P, 2, 64 * 3], scope=tok)
        wd1 = sb("wd1", [64, 2, 32 * 3], scope=tok)
        wa = sb("wa", [32, 32], scope=tok)
        tokb = sb("tokb", [P, 10], scope=tok)
        lh2 = sb("lh2", [P, 2, B, 64], scope=tok)
        c2 = sb("c2", [P, 2, B, 64], scope=tok)
        lh3 = sb("lh3", [64, 2, B, 32], scope=tok)
        c3 = sb("c3", [64, 2, B, 32], scope=tok)
        junk = sb("junk", [P, 2, 3, P], scope=tok)
        dots = sb("dots", [P, 80], scope=tok)
        lev = sb("lev", [P, 4, 3 * B * 3], scope=tok)
        red = sb("red", [P, 3, 3 * B], scope=tok)
        asig = sb("asig", [P, 3, B], scope=tok)
        f1 = sb("f1", [P, 2, B, 3], scope=tok)
        f2 = sb("f2", [P, 2, B], scope=tok)
        f3 = sb("f3", [64, 2, B], scope=tok)

        names = ("img_in tok_w_in tok_zero lo_done a1_done d1_done lh2_done c2_ps c2_done lh3_done c3_ps c3_done dots_done "
                 "dots_ps logit_done exp_done w_step w_done scaled un3_ps un3_done a2_done un2_ps un2_done a1_new "
                 "rows_done merged").split()
        s = {n: early_sem("t_" + n) for n in names}
        with nc.Block() as block:
            @block.sync
            def _(sp):
                for c in range(2):
                    b0, b1 = 4 * c, 4 * c + 4
                    sp.dma_start(img[:, b0:b1, :, :], dram["x"][b0:b1].rearrange("b (p r) w o -> p b r (w o)", r=2)).then_inc(s["img_in"], 16)
                    if c == 0:
                        sp.dma_start(mats[:, :], dram["c_mats"]).then_inc(mats_in, 16)
                sp.dma_start(wd3[:, :, :], dram["L0_tok_Wd3"].rearrange("(c i j) k -> i c (j k)", c=3, i=P)).then_inc(s["tok_w_in"], 16)
                v2 = dram["L0_tok_Wd2"].rearrange("(c i j) k -> c i (j k)", c=3, i=64)
                v1 = dram["L0_tok_Wd1"].rearrange("(c i j) k -> c i (j k)", c=3, i=32)
                for w, v, n in ((wd2, v2, 64), (wd1, v1, 32)):
                    sp.dma_start(w[n:2 * n, 0, :], v[0]).then_inc(s["tok_w_in"], 16)
                    sp.dma_start(w[0:n, 1, :], v[1]).then_inc(s["tok_w_in"], 16)
                    sp.dma_start(w[n:2 * n, 1, :], v[2]).then_inc(s["tok_w_in"], 16)
                sp.dma_start(wa[:, :], dram["L0_tok_Wa"].rearrange("(i j) o -> i (j o)", i=32)).then_inc(s["tok_w_in"], 16)
                for i, n in enumerate(("L0_tok_bd3", "L0_tok_bd2", "L0_tok_bd1")):
                    sp.dma_start(tokb[:, 3 * i:3 * i + 3], dram[n].partition_broadcast(P)).then_inc(s["tok_w_in"], 16)
                sp.dma_start(tokb[:, 9:10], dram["L0_tok_ba"].partition_broadcast(P)).then_inc(s["tok_w_in"], 16)
                sp.dma_start(wq0[:, :, :], dram["L0_attn_Wq"].rearrange("(k p) n -> p k n", p=P)).then_inc(l0_in, 16)
                sp.dma_start(wkv0[:, :, 0:D], dram["L0_attn_Wk"].rearrange("(k p) n -> p k n", p=P)).then_inc(l0_in, 16)
                sp.dma_start(wkv0[:, :, D:2 * D], dram["L0_attn_Wv"].rearrange("(k p) n -> p k n", p=P)).then_inc(l0_in, 16)
                sp.dma_start(wo0[:, :, :], dram["L0_attn_Wo"].rearrange("(k p) n -> p k n", p=P)).then_inc(l0_in, 16)
                sp.dma_start(wg[:, :, :], dram["L0_ffn_wg"].rearrange("(k p) n -> p k n", p=P)).then_inc(l0_in, 16)
                sp.dma_start(ropeq[:, :, :, :], dram["c_rope_q"]).then_inc(l0_in, 16)
                sp.dma_start(ropek[:, :, :, :], dram["c_rope_k"]).then_inc(l0_in, 16)
                with nc.allow_non_contiguous_dma(reason="one bias per partition"):
                    sp.dma_start(bqm[:, :], dram["L0_attn_bq"].rearrange("(m p) -> p m", p=P)).then_inc(l0_in, 16)
                    for r in range(2):
                        sp.dma_start(bqs[r:P:2, :], dram["L0_attn_bq"].rearrange("(m q r) -> r q m", m=KD, r=2)[1 - r]).then_inc(l0_in, 16)
                sp.dma_start(bkv[:, 0:D], dram["L0_attn_bk"].partition_broadcast(P)).then_inc(l0_in, 16)
                sp.dma_start(bkv[:, D:2 * D], dram["L0_attn_bv"].partition_broadcast(P)).then_inc(l0_in, 16)
                sp.dma_start(bo0[:, :], dram["L0_attn_bo"].partition_broadcast(P)).then_inc(l0_in, 16)
                sp.dma_start(clsb[:, :], dram["cls_tok"].rearrange("a b d -> (a b d)").partition_broadcast(B)).then_inc(l0_in, 16)
                sp.dma_start(emb[0:BUCKETS, :], dram["L1_attn_rel_emb"]).then_inc(bias["emb_in"], 16)
                sp.dma_start(emb[BUCKETS:BUCKETS + 1, :], dram["c_masked"]).then_inc(bias["emb_in"], 16)
                sp.dma_start(hot[:, :], dram["c_buckets"]).then_inc(bias["emb_in"], 16)
                sp.wait_ge(s["merged"], 4)
                for half in range(TPB):
                    for r in range(2):
                        sp.dma_start(hrow[r:P:2, half:NT:TPB, :], img[64 * half:64 * half + 64, :, r, :]).then_inc(s["rows_done"], 16)
                sp.wait_ge(s["rows_done"], 16 * 4)

            @block.gpsimd
            def _(pool):
                for c in range(2):
                    pool.wait_ge(s["img_in"], 16 * 2)
                    nc.gpsimd.tensor_tensor(lohi[:, 4 * c:4 * c + 4, 1, :, :], img[:, 4 * c:4 * c + 4, :, 0::2],
                                            img[:, 4 * c:4 * c + 4, :, 1::2], ALU.subtract).then_inc(s["lo_done"], 1)

            @block.vector
            def _(dve):
                nc.vector.memset(dots[:, :], 0.0).then_inc(s["tok_zero"], 1)
                nc.vector.memset(wd2[0:64, 0, :], 0.0).then_inc(s["tok_zero"], 1)
                nc.vector.memset(wd1[0:32, 0, :], 0.0).then_inc(s["tok_zero"], 1)
                dve.wait_ge(s["img_in"], 16 * 2)
                for c in range(2):
                    nc.vector.tensor_tensor(lohi[:, 4 * c:4 * c + 4, 0, :, :], img[:, 4 * c:4 * c + 4, :, 0::2],
                                            img[:, 4 * c:4 * c + 4, :, 1::2], ALU.add).then_inc(s["lo_done"], 1)
                dve.wait_ge(s["lo_done"], 4)
                nc.vector.tensor_tensor(a1[:, :, :], lohi[:, :, 0, 0, :], lohi[:, :, 0, 1, :], ALU.add).then_inc(s["a1_done"], 1)
                nc.vector.tensor_tensor(d1[:, :, 0, :], lohi[:, :, 0, 0, :], lohi[:, :, 0, 1, :], ALU.subtract).then_inc(s["d1_done"], 1)
                nc.vector.tensor_tensor(d1[:, :, 1, :], lohi[:, :, 1, 0, :], lohi[:, :, 1, 1, :], ALU.add).then_inc(s["d1_done"], 1)
                nc.vector.tensor_tensor(d1[:, :, 2, :], lohi[:, :, 1, 0, :], lohi[:, :, 1, 1, :], ALU.subtract).then_inc(s["d1_done"], 1)
                dve.wait_ge(s["a1_done"], 1)
                nc.vector.tensor_tensor(lh2[:, 0, :, :], a1[:, :, 0::2], a1[:, :, 1::2], ALU.add).then_inc(s["lh2_done"], 1)
                nc.vector.tensor_tensor(lh2[:, 1, :, :], a1[:, :, 0::2], a1[:, :, 1::2], ALU.subtract).then_inc(s["lh2_done"], 1)
                dve.wait_ge(s["tok_w_in"], 16 * 12)
                dve.wait_ge(s["tok_zero"], 3)
                dve.wait_ge(s["d1_done"], 3)
                n_dots = 0

                def products():
                    nonlocal n_dots
                    n_dots += 1
                    if n_dots > 2:
                        dve.wait_ge(s["dots_done"], n_dots - 2)
                    return junk[:, n_dots % 2, :, :]

                w3v = wd3[:, :, :].rearrange("p c (j k) -> p c j k", k=3)
                for b in range(B):
                    for k in range(3):
                        nc.vector.tensor_tensor_reduce(products(), d1[:, b, :, :], w3v[:, :, :, k], 1.0, 0.0, ALU.mult,
                                                       ALU.add, dots[:, 3 * b + k:3 * b + k + 1]).then_inc(s["dots_done"], 1)
                dve.wait_ge(s["c2_done"], 2)
                nc.vector.tensor_tensor(lh3[:, 0, :, :], c2[0:64, 0, :, 0::2], c2[0:64, 0, :, 1::2], ALU.add).then_inc(s["lh3_done"], 1)
                nc.vector.tensor_tensor(lh3[:, 1, :, :], c2[0:64, 0, :, 0::2], c2[0:64, 0, :, 1::2], ALU.subtract).then_inc(s["lh3_done"], 1)
                w2v = wd2[:, :, :].rearrange("p c (j k) -> p c j k", k=3)
                for b in range(B):
                    for k in range(3):
                        nc.vector.tensor_tensor_reduce(products()[:, 0:2, 0:64], c2[:, :, b, :], w2v[:, :, :, k], 1.0, 0.0, ALU.mult,
                                                       ALU.add, dots[:, 24 + 3 * b + k:24 + 3 * b + k + 1]).then_inc(s["dots_done"], 1)
                dve.wait_ge(s["c3_done"], 1)
                w1v = wd1[:, :, :].rearrange("p c (j k) -> p c j k", k=3)
                for b in range(B):
                    for k in range(3):
                        nc.vector.tensor_tensor_reduce(products()[0:64, 0:2, 0:32], c3[:, :, b, :], w1v[:, :, :, k], 1.0, 0.0, ALU.mult,
                                                       ALU.add, dots[0:64, 48 + 3 * b + k:48 + 3 * b + k + 1]).then_inc(s["dots_done"], 1)
                    nc.vector.tensor_tensor_reduce(products()[0:32, 0, 0:32], c3[0:32, 0, b, :], wa[:, :], 1.0, 0.0, ALU.mult,
                                                   ALU.add, dots[0:32, 72 + b:73 + b]).then_inc(s["dots_done"], 1)
                dve.wait_ge(s["dots_ps"], 1)
                for i in range(3):
                    nc.vector.scalar_tensor_tensor(lev[:, 0, 24 * i:24 * i + 24].rearrange("p (b k) -> p b k", k=3),
                                                   bank[1][:, 24 * i:24 * i + 24].rearrange("p (b k) -> p b k", k=3),
                                                   0.5 ** (i + 1), rep(tokb[:, 3 * i:3 * i + 3], 1, B), ALU.mult,
                                                   ALU.add).then_inc(s["w_step"], 1)
                nc.vector.tensor_scalar(asig[:, 0, :], bank[1][:, 72:80], 0.125, tokb[:, 9:10], ALU.mult, ALU.add).then_inc(s["w_step"], 1)
                dve.wait_ge(s["w_step"], 4)
                z = lev[:, 0, :].rearrange("p (n k) -> p n k", k=3)
                nc.vector.tensor_reduce(red[:, 0, :], z, AX.X, ALU.max).then_inc(s["w_step"], 1)
                dve.wait_ge(s["w_step"], 5)
                nc.vector.tensor_tensor(lev[:, 1, :].rearrange("p (n k) -> p n k", k=3), z, rep(red[:, 0, :], 2, 3), ALU.subtract).then_inc(s["logit_done"], 1)
                dve.wait_ge(s["exp_done"], 2)
                ez = lev[:, 2, :].rearrange("p (n k) -> p n k", k=3)
                nc.vector.tensor_reduce(red[:, 1, :], ez, AX.X, ALU.add).then_inc(s["w_step"], 1)
                nc.vector.tensor_scalar(asig[:, 2, :], asig[:, 1, :], 1.0, None, ALU.add).then_inc(s["w_step"], 1)
                dve.wait_ge(s["w_step"], 7)
                nc.vector.reciprocal(red[:, 2, :], red[:, 1, :]).then_inc(s["w_step"], 1)
                nc.vector.reciprocal(asig[:, 0, :], asig[:, 2, :]).then_inc(s["w_step"], 1)
                dve.wait_ge(s["w_step"], 9)
                nc.vector.tensor_tensor(lev[:, 3, :].rearrange("p (n k) -> p n k", k=3), ez, rep(red[:, 2, :], 2, 3), ALU.mult).then_inc(s["w_step"], 1)
                dve.wait_ge(s["w_step"], 10)
                wv = lev[:, 3, :].rearrange("p (l b k) -> p l k b", l=3, k=3)
                nc.vector.tensor_copy(f3[0:32, 0, :], asig[0:32, 0, :]).then_inc(s["w_done"], 1)
                nc.vector.tensor_copy(f3[0:32, 1, :], wv[0:32, 2, 1, :]).then_inc(s["w_done"], 1)
                nc.vector.tensor_copy(f3[32:64, :, :], wv[32:64, 2, 0::2, :]).then_inc(s["w_done"], 1)
                nc.vector.memset(f2[0:64, 0, :], 1.0).then_inc(s["w_done"], 1)
                nc.vector.tensor_copy(f2[0:64, 1, :], wv[0:64, 1, 1, :]).then_inc(s["w_done"], 1)
                nc.vector.tensor_copy(f2[64:P, :, :], wv[64:P, 1, 0::2, :]).then_inc(s["w_done"], 1)
                nc.vector.tensor_scalar(f1[:, 0, :, :], lev[:, 3, 0:24].rearrange("p (b k) -> p b k", k=3), 0.25, None, ALU.mult).then_inc(s["w_done"], 1)
                dve.wait_ge(s["w_done"], 7)
                nc.vector.tensor_tensor(c3[:, :, :, :], c3[:, :, :, :], rep(f3[:, :, :], 3, 32), ALU.mult).then_inc(s["scaled"], 1)
                for k in range(3):
                    nc.vector.tensor_tensor(d1[:, :, k, :], d1[:, :, k, :], rep(f1[:, 0, :, k], 2, P), ALU.mult).then_inc(s["scaled"], 1)
                dve.wait_ge(s["un3_done"], 1)
                u3 = lh3
                nc.vector.tensor_tensor(c2[0:64, 0, :, 0::2], u3[:, 0, :, :], u3[:, 1, :, :], ALU.add).then_inc(s["a2_done"], 1)
                nc.vector.tensor_tensor(c2[0:64, 0, :, 1::2], u3[:, 0, :, :], u3[:, 1, :, :], ALU.subtract).then_inc(s["a2_done"], 1)
                dve.wait_ge(s["a2_done"], 2)
                nc.vector.tensor_tensor(c2[:, :, :, :], c2[:, :, :, :], rep(f2[:, :, :], 3, 64), ALU.mult).then_inc(s["scaled"], 1)
                dve.wait_ge(s["scaled"], 5)
                nc.vector.tensor_tensor(lohi[:, :, 1, 0, :], d1[:, :, 1, :], d1[:, :, 2, :], ALU.add).then_inc(s["a1_new"], 1)
                nc.vector.tensor_tensor(lohi[:, :, 1, 1, :], d1[:, :, 1, :], d1[:, :, 2, :], ALU.subtract).then_inc(s["a1_new"], 1)
                dve.wait_ge(s["un2_done"], 2)
                nc.vector.tensor_tensor(a1[:, :, 0::2], lh2[:, 0, :, :], lh2[:, 1, :, :], ALU.add).then_inc(s["a1_new"], 1)
                nc.vector.tensor_tensor(a1[:, :, 1::2], lh2[:, 0, :, :], lh2[:, 1, :, :], ALU.subtract).then_inc(s["a1_new"], 1)
                dve.wait_ge(s["a1_new"], 4)
                nc.vector.tensor_tensor(lohi[:, :, 0, 0, :], a1[:, :, :], d1[:, :, 0, :], ALU.add).then_inc(s["a1_new"], 1)
                nc.vector.tensor_tensor(lohi[:, :, 0, 1, :], a1[:, :, :], d1[:, :, 0, :], ALU.subtract).then_inc(s["a1_new"], 1)
                dve.wait_ge(s["a1_new"], 6)
                for c in range(2):
                    q = slice(4 * c, 4 * c + 4)
                    nc.vector.tensor_tensor(img[:, q, :, 0::2], lohi[:, q, 0, :, :], lohi[:, q, 1, :, :], ALU.add).then_inc(s["merged"], 1)
                    nc.vector.tensor_tensor(img[:, q, :, 1::2], lohi[:, q, 0, :, :], lohi[:, q, 1, :, :], ALU.subtract).then_inc(s["merged"], 1)

            @block.tensor
            def _(pe):
                pe.wait_ge(mats_in, 16)
                for g in range(2):
                    pe.wait_ge(s["lh2_done"], g + 1)
                    nc.tensor.matmul(kvbank[:, g, :], mat("haar2"), lh2[:, g, :, :], start=True, stop=True).then_inc(s["c2_ps"], 1)
                pe.wait_ge(s["lh3_done"], 2)
                nc.tensor.matmul(bank[0][0:64, :], mat("haar3", 64), lh3[:, :, :, :], start=True, stop=True).then_inc(s["c3_ps"], 1)
                pe.wait_ge(s["dots_done"], 24 + 24 + 32)
                nc.tensor.matmul(bank[1][:, 0:80], ones, dots[:, :], start=True, stop=True).then_inc(s["dots_ps"], 1)
                pe.wait_ge(s["scaled"], 1)
                nc.tensor.matmul(bank[0][0:64, :], mat("unhaar3", 64), c3[:, :, :, :], start=True, stop=True).then_inc(s["un3_ps"], 1)
                pe.wait_ge(s["scaled"], 5)
                for g in range(2):
                    nc.tensor.matmul(kvbank[:, g, :], mat("unhaar2"), c2[:, g, :, :], start=True, stop=True).then_inc(s["un2_ps"], 1)

            @block.scalar
            def _(act):
                for g in range(2):
                    act.wait_ge(s["c2_ps"], g + 1)
                    nc.scalar.copy(c2[:, g, :, :], kvbank[:, g, :].rearrange("p (b j) -> p b j", b=B)).then_inc(s["c2_done"], 1)
                act.wait_ge(s["c3_ps"], 1)
                nc.scalar.copy(c3[:, :, :, :].rearrange("p c b j -> p (c b j)"), bank[0][0:64, :]).then_inc(s["c3_done"], 1)
                act.wait_ge(s["logit_done"], 1)
                nc.scalar.activation(lev[:, 2, :], lev[:, 1, :], ACT.Exp).then_inc(s["exp_done"], 1)
                nc.scalar.activation(asig[:, 1, :], asig[:, 0, :], ACT.Exp, scale=-1.0).then_inc(s["exp_done"], 1)
                act.wait_ge(s["un3_ps"], 1)
                nc.scalar.copy(lh3[:, :, :, :].rearrange("p c b j -> p (c b j)"), bank[0][0:64, :]).then_inc(s["un3_done"], 1)
                for g in range(2):
                    act.wait_ge(s["un2_ps"], g + 1)
                    nc.scalar.mul(lh2[:, g, :, :].rearrange("p b j -> p (b j)"), kvbank[:, g, :], 0.25).then_inc(s["un2_done"], 1)
        tok.close()
        brev = sb("brev", [H1, 2 * ROWS], scope=attn0)
        hankel = sb("hankel", [P, H1, SCOLS], scope=attn0)
        scope = ExitStack()
        stat0 = sb("stat0", [P, NT, 6], scope=scope)
        mv0 = sb("mv0", [P, NT, 2], scope=scope)
        var0 = sb("var0", [P, NT], scope=scope)
        rstd0 = sb("rstd0", [P, NT], scope=scope)
        nh16 = sb("nh16", [P, NT], scope=scope)
        statc = sb("statc", [B, 6], scope=scope)
        mvc = sb("mvc", [B, 2], scope=scope)
        varc = sb("varc", [B, 1], scope=scope)
        rstdc = sb("rstdc", [B, 1], scope=scope)
        xc0 = sb("xc0", [B, D], scope=scope)
        xct0 = sb("xct0", [P, KD, B], scope=scope)
        qc0 = sb("qc0", [P, KD, B], scope=scope)
        kvc = sb("kvc", [1, 2 * D], scope=scope)
        xn0 = [sb(f"xn0_{i}", [P, TPB, D], scope=scope) for i in range(2)]
        xt0 = [sb(f"xt0_{i}", [P, KD, ROWS], scope=scope) for i in range(2)]
        t1 = sb("t1", [P, KD, ROWS], scope=scope)
        t2 = sb("t2", [P, KD, ROWS], scope=scope)
        qt0 = [sb(f"qt0_{i}", [P, KD, ROWS], scope=scope) for i in range(2)]
        kvb = [sb(f"kvb_{i}", [P, TPB, 2 * D], scope=scope) for i in range(2)]
        kt1 = sb("kt1", [P, TPB, D], scope=scope)
        kt2 = sb("kt2", [P, TPB, D], scope=scope)
        kr = sb("kr", [P, TPB, D], scope=scope)
        vtkm = sb("vtkm", [P, KD, P], scope=scope)
        gs = sb("gs", [P, KD, D], scope=scope)
        xn1 = [sb(f"xn1_{i}", [P, TPB, D], scope=scope) for i in range(2)]
        zrow = sb("zrow", [P, 2, D], scope=scope)
        x1t = sb("x1t", [P, KD, ROWS], scope=scope)
        stat1 = sb("stat1", [P, TPB, 6], scope=scope)
        mv1 = sb("mv1", [P, TPB, 2], scope=scope)
        var1 = sb("var1", [P, TPB], scope=scope)
        rstd1 = sb("rstd1", [P, TPB], scope=scope)
        clsrow = sb("clsrow", [1, B, D], scope=scope)
        clsatt = sb("clsatt", [B, D], scope=scope)
        logits = sb("logits", [P, NTC, E], scope=scope)

        names = ("stat0 aggr0 var0 rstd0 swapped xc0 xct_ps xct qc_ps qc kvc_ps kvc xn_ready xt_ps xt_ready q_ps q_used "
                 "kv_ps kvb_ready kt1 kt2 qr_ready kr_ready vtk_ps vtk_ready g_ps g_ready out_ps hb_done h_done cls_copied "
                 "stat1 aggr1 var1 rstd1 xn1_ready x1t_ps x1t_ready lg_ps lg_done nh xrow_done cls_ps").split()
        s = {n: early_sem("a_" + n) for n in names}
        l0_all = 16 * 14

        def per_image(eng, body):
            body(0, 0, True, False)
            with eng.Fori(0, B // 2 - 1) as pair:
                body(pair * 2 + 1, 1, False, False)
                body(pair * 2 + 2, 0, False, False)
            body(B - 1, (B - 1) % 2, False, True)

        def tiles(b):
            return bass.ds(b * TPB, TPB)

        with nc.Block() as block:
            @block.sync
            def _(sp):
                for e in range(2):
                    load_expert(sp, e)
                for src, dst in (("L1_attn_Wq", wq1), ("L1_attn_Wkv", wkv1), ("L1_attn_Wo", wo1)):
                    sp.dma_start(dst[:, :, :], dram[src].rearrange("(k p) n -> p k n", p=P)).then_inc(l1_in, 16)
                sp.dma_start(bo1[:, :], dram["L1_attn_bo"].partition_broadcast(P)).then_inc(l1_in, 16)
                sp.wait_ge(bias["brev"], 1)
                sp.dma_start(bias_rev, brev[:, :]).then_inc(bias["brev_out"], 16)
                sp.wait_ge(bias["brev_out"], 16)
                for t in range(TPB):
                    n, at = 1 + P * (t + 1), (1 + P) * t
                    rows = bass.AP(tensor=bias_rev.tensor, offset=ROWS - P * t - P, ap=[[1, P], [2 * ROWS, H1], [1, n]])
                    sp.dma_start(hankel[:, :, at:at + n], rows).then_inc(bias["rev_in"], 16)
                sp.wait_ge(s["nh"], 1)
                for c in range(0, buf.shape[0], 256):
                    n = min(256, buf.shape[0] - c)
                    sp.dma_start(buf[c:c + n, :], zrow[0:n // 2, :, :]).then_inc(buf_zeroed, 16)
                sp.wait_ge(buf_zeroed, 16 * -(-buf.shape[0] // 256))

            @block.gpsimd
            def _(pool):
                nc.gpsimd.memset(zrow[:, :, :], 0.0).then_inc(s["nh"], 1)
                nc.gpsimd.memset(logits[:, :, :], 0.0).then_inc(s["nh"], 1)
                nc.gpsimd.memset(nh16[:, :], -0.5).then_inc(s["nh"], 1)
                pool.wait_ge(l0_in, l0_all)
                nc.gpsimd.tensor_copy(wqs0[:, :, 0::2], wq0[:, :, 1::2]).then_inc(s["swapped"], 1)
                nc.gpsimd.tensor_copy(wqs0[:, :, 1::2], wq0[:, :, 0::2]).then_inc(s["swapped"], 1)
                pool.wait_ge(s["aggr0"], NT + 1)
                nc.gpsimd.tensor_scalar(var0[:, :], mv0[:, :, 1], EPS, None, ALU.add).then_inc(s["var0"], 1)
                nc.gpsimd.tensor_scalar(varc[:, :], mvc[:, 1:2], EPS, None, ALU.add).then_inc(s["var0"], 1)
                pool.wait_ge(s["var0"], 2)
                pool.wait_ge(s["nh"], 3)
                nc.gpsimd.tensor_tensor(rstd0[:, :], var0[:, :], nh16[:, :], ALU.pow).then_inc(s["rstd0"], 1)
                nc.gpsimd.tensor_tensor(rstdc[:, :], varc[:, :], nh16[0:B, 0:1], ALU.pow).then_inc(s["rstd0"], 1)

                def turn_qk(b, slot, first):
                    pool.wait_ge(s["q_used"], b + 1)
                    if not first:
                        pool.wait_ge(s["out_ps"], b)
                    nc.gpsimd.tensor_tensor(qt0[slot][:, :, :], t1[:, :, :], t2[:, :, :], ALU.add).then_inc(s["qr_ready"], 1)
                    pool.wait_ge(s["kvb_ready"], b + 1)
                    if not first:
                        pool.wait_ge(s["kr_ready"], b)
                    nc.gpsimd.tensor_tensor(kt1[:, :, :], kvb[slot][:, :, 0:D], ropek[:, 0, :, :], ALU.mult).then_inc(s["kt1"], 1)
                    pool.wait_ge(s["kt1"], b + 1)
                    pool.wait_ge(s["kt2"], 2 * b + 2)
                    if not first:
                        pool.wait_ge(s["vtk_ps"], b + 1)
                    nc.gpsimd.tensor_tensor(kr[:, :, :], kt1[:, :, :], kt2[:, :, :], ALU.add).then_inc(s["kr_ready"], 1)

                def deviations(b):
                    waits_apart(pool, (s["aggr1"], 2 * b + 2))
                    nc.gpsimd.tensor_scalar(var1[:, :], mv1[:, :, 1], EPS, None, ALU.add).then_inc(s["var1"], 1)
                    pool.wait_ge(s["var1"], b + 1)
                    nc.gpsimd.tensor_tensor(rstd1[:, :], var1[:, :], nh16[:, 0:TPB], ALU.pow).then_inc(s["rstd1"], 1)

                def keep_rows(b, slot):
                    pool.wait_ge(s["xn1_ready"], b + 1)
                    nc.gpsimd.tensor_copy(xrow[:, tiles(b), :], xn1[slot][:, :, :]).then_inc(s["xrow_done"], 1)

                turn_qk(0, 0, True)

                def image(b, slot, first, last):
                    if not first:
                        deviations(b - 1)
                    pool.wait_ge(s["xn_ready"], b + 1)
                    nc.gpsimd.tensor_tensor(hrow[:, tiles(b), :], hrow[:, tiles(b), :], rep(bo0[:, :], 1, TPB), ALU.add).then_inc(s["hb_done"], 1)
                    if not last:
                        turn_qk(b + 1, 1 - slot, False)
                    if not first:
                        keep_rows(b - 1, 1 - slot)

                pool.sem_inc(s["xrow_done"], 1)
                per_image(pool, image)
                deviations(B - 1)
                keep_rows(B - 1, (B - 1) % 2)

            @block.vector
            def _(dve):
                dve.wait_ge(bias["emb_in"], 16 * 3)
                nc.vector.tensor_scalar(emb[0:BUCKETS, :], emb[0:BUCKETS, :], 64.0, None, ALU.mult).then_inc(bias["emb"], 1)
                for t in range(NT):
                    nc.vector.bn_stats(stat0[:, t, :], hrow[:, t, :]).then_inc(s["stat0"], 1)
                dve.wait_ge(bias["brev_ps"], 1)
                nc.vector.tensor_copy(brev[:, :], bank[1][0:H1, :]).then_inc(bias["brev"], 1)
                dve.wait_ge(l0_in, l0_all)
                nc.vector.bn_stats(statc[:, :], clsb[:, :]).then_inc(s["stat0"], 1)
                for t in range(NT):
                    dve.wait_ge(s["stat0"], t + 1)
                    nc.vector.bn_aggr(mv0[:, t, :], stat0[:, t, :]).then_inc(s["aggr0"], 1)
                dve.wait_ge(s["stat0"], NT + 1)
                nc.vector.bn_aggr(mvc[:, :], statc[:, :]).then_inc(s["aggr0"], 1)
                dve.wait_ge(s["rstd0"], 2)
                dve.wait_ge(s["aggr0"], NT + 1)
                nc.vector.tensor_scalar(xc0[:, :], clsb[:, :], mvc[:, 0:1], rstdc[:, 0:1], ALU.subtract, ALU.mult).then_inc(s["xc0"], 1)

                def norm0(b, slot):
                    for t in range(TPB):
                        at = bass.ds(b * TPB + t, 1)
                        ins = nc.vector.tensor_scalar(xn0[slot][:, t, :], hrow[:, at, :].rearrange("p o d -> p (o d)"),
                                                      mv0[:, at, 0:1].rearrange("p o d -> p (o d)"), rstd0[:, at], ALU.subtract, ALU.mult)
                    ins.then_inc(s["xn_ready"], 1)

                norm0(0, 0)
                dve.wait_ge(s["qc_ps"], 1)
                for m in range(KD):
                    nc.vector.tensor_scalar(qc0[:, m, :], bank[4][:, B * m:B * m + B], bqm[:, m:m + 1], None, ALU.add).then_inc(s["qc"], 1)
                dve.wait_ge(s["kvc_ps"], 1)
                nc.vector.tensor_tensor(kvc[:, :], bank[5][0:1, :], bkv[0:1, :], ALU.add).then_inc(s["kvc"], 1)

                def rotate(b, slot, first):
                    dve.wait_ge(s["q_ps"], b + 1)
                    if not first:
                        dve.wait_ge(s["qr_ready"], b)
                    for m in range(KD):
                        cols = slice(ROWS * m, ROWS * m + ROWS)
                        nc.vector.scalar_tensor_tensor(t1[:, m, :], bank[1][:, cols], bqm[:, m:m + 1], ropeq[:, 0, m, :], ALU.add, ALU.mult)
                        ins = nc.vector.scalar_tensor_tensor(t2[:, m, :], bank[2][:, cols], bqs[:, m:m + 1], ropeq[:, 1, m, :], ALU.add, ALU.mult)
                    ins.then_inc(s["q_used"], 1)
                    dve.wait_ge(s["kv_ps"], b + 1)
                    if not first:
                        dve.wait_ge(s["vtk_ps"], b)
                        dve.wait_ge(s["kr_ready"], b)
                    nc.vector.tensor_tensor(kvb[slot][:, :, :], kvbank[:, :, :], rep(bkv[:, :], 1, TPB), ALU.add).then_inc(s["kvb_ready"], 1)
                    dve.wait_ge(s["kvb_ready"], b + 1)
                    nc.vector.tensor_tensor(kt2[:, :, 0::2], kvb[slot][:, :, 1:D:2], ropek[:, 1, :, 0::2], ALU.mult).then_inc(s["kt2"], 1)
                    nc.vector.tensor_tensor(kt2[:, :, 1::2], kvb[slot][:, :, 0:D:2], ropek[:, 1, :, 1::2], ALU.mult).then_inc(s["kt2"], 1)

                def residual(b, slot):
                    dve.wait_ge(s["out_ps"], b + 2)
                    dve.wait_ge(s["hb_done"], b + 1)
                    nc.vector.tensor_tensor(hrow[:, tiles(b), :], bank[5][:, :].rearrange("p (t d) -> p t d", t=TPB),
                                            hrow[:, tiles(b), :], ALU.add).then_inc(s["h_done"], 1)
                    waits_apart(dve, (s["h_done"], b + 1))
                    for t in range(TPB):
                        ins = nc.vector.bn_stats(stat1[:, t, :], hrow[:, bass.ds(b * TPB + t, 1), :].rearrange("p o d -> p (o d)"))
                    ins.then_inc(s["stat1"], 1)
                    waits_apart(dve, (s["stat1"], b + 1))
                    for t in range(TPB):
                        nc.vector.bn_aggr(mv1[:, t, :], stat1[:, t, :]).then_inc(s["aggr1"], 1)
                    dve.wait_ge(s["rstd1"], b + 1)
                    dve.wait_ge(s["x1t_ps"], b + 1)
                    dve.wait_ge(s["xrow_done"], b + 1)
                    dve.wait_ge(s["aggr1"], 2 * b + 2)
                    for t in range(TPB):
                        at = bass.ds(b * TPB + t, 1)
                        ins = nc.vector.tensor_scalar(xn1[slot][:, t, :], hrow[:, at, :].rearrange("p o d -> p (o d)"),
                                                      mv1[:, t, 0:1], rstd1[:, t:t + 1], ALU.subtract, ALU.mult)
                    ins.then_inc(s["xn1_ready"], 1)

                rotate(0, 0, True)

                def image(b, slot, first, last):
                    if not last:
                        if not first:
                            dve.wait_ge(s["xt_ps"], b)
                        norm0(b + 1, 1 - slot)
                    dve.wait_ge(s["vtk_ps"], b + 2)
                    if not first:
                        dve.wait_ge(s["g_ps"], b)
                    nc.vector.tensor_tensor(vtkm[:, :, :], bank[3][:, 0:D].rearrange("p (g n) -> p g n", g=KD),
                                            mat("blocks").rearrange("p (g n) -> p g n", g=KD), ALU.mult).then_inc(s["vtk_ready"], 1)
                    if not first:
                        residual(b - 1, 1 - slot)
                    if not last:
                        rotate(b + 1, 1 - slot, False)

                per_image(dve, image)
                residual(B - 1, (B - 1) % 2)

            @block.scalar
            def _(act):
                act.wait_ge(s["xct_ps"], 1)
                nc.scalar.copy(xct0[:, :, :], bank[3][:, 0:KD * B].rearrange("p (k b) -> p k b", k=KD)).then_inc(s["xct"], 1)

                def evac_xt(b, slot, early):
                    act.wait_ge(s["xt_ps"], b + 1)
                    if not early:
                        act.wait_ge(s["kv_ps"], b - 1)
                    nc.scalar.copy(xt0[slot][:, :, :], bank[0][:, :].rearrange("p (k n) -> p k n", k=KD)).then_inc(s["xt_ready"], 1)

                def evac_expert_rows(b):
                    act.wait_ge(s["x1t_ps"], b + 2)
                    nc.scalar.copy(x1t[:, :, :], bank[0][:, :].rearrange("p (k n) -> p k n", k=KD)).then_inc(s["x1t_ready"], 1)
                    act.wait_ge(s["lg_ps"], b + 1)
                    nc.scalar.copy(logits[:, tiles(b), :], bank[0][:, 0:TPB * E].rearrange("p (t e) -> p t e", t=TPB)).then_inc(s["lg_done"], 1)

                evac_xt(0, 0, True)
                act.wait_ge(s["nh"], 3)

                def image(b, slot, first, last):
                    if not last:
                        evac_xt(b + 1, 1 - slot, first)
                    act.wait_ge(s["g_ps"], b + 1)
                    if not first:
                        act.wait_ge(s["out_ps"], b + 1)
                    nc.scalar.copy(gs[:, :, :], bank[4][:, :].rearrange("p (g n) -> p g n", g=KD)).then_inc(s["g_ready"], 1)
                    if not first:
                        evac_expert_rows(b - 1)
                    act.wait_ge(s["cls_ps"], b + 1)
                    nc.scalar.copy(clsrow[0:1, bass.ds(b, 1), :].rearrange("p o d -> p (o d)"), bank[3][0:1, D:2 * D]).then_inc(s["cls_copied"], 1)

                per_image(act, image)
                evac_expert_rows(B - 1)

            @block.tensor
            def _(pe):
                pe.sem_inc(s["out_ps"], 1)
                pe.sem_inc(s["vtk_ps"], 1)
                pe.sem_inc(s["x1t_ps"], 1)
                pe.sem_inc(s["lg_done"], 1)
                pe.wait_ge(mats_in, 16)
                pe.wait_ge(l0_in, l0_all)
                pe.wait_ge(bias["emb"], 1)
                nc.tensor.matmul(bank[1][0:H1, :], emb[:, :], hot[:, :], start=True, stop=True).then_inc(bias["brev_ps"], 1)
                pe.wait_ge(s["xc0"], 1)
                for k in range(KD):
                    ins = nc.tensor.transpose(bank[3][:, B * k:B * k + B], xc0[:, P * k:P * k + P], mat("ident", B)[:, 0:B])
                ins.then_inc(s["xct_ps"], 1)
                pe.wait_ge(s["xct"], 1)
                for m in range(KD):
                    for k in range(KD):
                        ins = nc.tensor.matmul(bank[4][:, B * m:B * m + B], wq0[:, k, P * m:P * m + P], xct0[:, k, :], start=(k == 0), stop=(k == KD - 1))
                ins.then_inc(s["qc_ps"], 1)
                for k in range(KD):
                    ins = nc.tensor.matmul(bank[5][0:1, :], xct0[:, k, 0:1], wkv0[:, k, :], start=(k == 0), stop=(k == KD - 1))
                ins.then_inc(s["kvc_ps"], 1)

                def turn(src, done):
                    for k in range(KD):
                        for t in range(TPB):
                            ins = nc.tensor.transpose(bank[0][:, ROWS * k + P * t:ROWS * k + P * t + P], src(t)[:, P * k:P * k + P], ident)
                    ins.then_inc(done, 1)

                def expert_rows_t(b, slot):
                    pe.wait_ge(s["xn1_ready"], b + 1)
                    for k in range(KD):
                        for t in range(TPB):
                            ins = nc.tensor.transpose(bank[0][:, ROWS * k + P * t:ROWS * k + P * t + P], xn1[slot][:, t, P * k:P * k + P], ident)
                    ins.then_inc(s["x1t_ps"], 1)

                def logits_of(b):
                    pe.wait_ge(s["x1t_ready"], b + 1)
                    for t in range(TPB):
                        for k in range(KD):
                            ins = nc.tensor.matmul(bank[0][:, E * t:E * t + E], x1t[:, k, P * t:P * t + P], wg[:, k, :], start=(k == 0), stop=(k == KD - 1))
                    ins.then_inc(s["lg_ps"], 1)

                pe.wait_ge(s["xn_ready"], 1)
                turn(lambda t: xn0[0][:, t, :], s["xt_ps"])
                pe.wait_ge(s["swapped"], 2)
                pe.wait_ge(s["qc"], 2)
                pe.wait_ge(s["kvc"], 1)
                pe.wait_ge(bias["brev"], 1)

                def project_q(b, slot):
                    pe.wait_ge(s["xt_ready"], b + 1)
                    for w, o in ((wq0, bank[1]), (wqs0, bank[2])):
                        for m in range(KD):
                            for k in range(KD):
                                ins = nc.tensor.matmul(o[:, ROWS * m:ROWS * m + ROWS], w[:, k, P * m:P * m + P], xt0[slot][:, k, :],
                                                       start=(k == 0), stop=(k == KD - 1))
                    ins.then_inc(s["q_ps"], 1)

                def project_kv(b, slot):
                    for t in range(TPB):
                        for k in range(KD):
                            ins = nc.tensor.matmul(kvbank[:, t, :], xt0[slot][:, k, P * t:P * t + P], wkv0[:, k, :], start=(k == 0), stop=(k == KD - 1))
                    ins.then_inc(s["kv_ps"], 1)

                project_q(0, 0)
                project_kv(0, 0)

                def image(b, slot, first, last):
                    pe.wait_ge(s["kr_ready"], b + 1)
                    if not first:
                        pe.wait_ge(s["vtk_ready"], b)
                        pe.wait_ge(s["cls_copied"], b)
                    for g in range(KD):
                        for t in range(TPB):
                            nc.tensor.matmul(bank[3][:, P * g:P * g + P], kvb[slot][:, t, D + P * g:D + P * g + P], kr[:, t, P * g:P * g + P],
                                             start=(t == 0), stop=False)
                        ins = nc.tensor.matmul(bank[3][:, P * g:P * g + P], kvc[0:1, D + P * g:D + P * g + P], kvc[0:1, P * g:P * g + P],
                                               start=False, stop=True)
                    ins.then_inc(s["vtk_ps"], 1)
                    if not first:
                        pe.wait_ge(s["lg_done"], b)
                    if not last:
                        pe.wait_ge(s["xn_ready"], b + 2)
                        turn(lambda t: xn0[1 - slot][:, t, :], s["xt_ps"])
                    pe.wait_ge(s["vtk_ready"], b + 1)
                    if not first:
                        pe.wait_ge(s["g_ready"], b)
                    for g in range(KD):
                        ins = nc.tensor.matmul(bank[4][:, D * g:D * g + D], vtkm[:, g, :], wo0[:, g, :], start=True, stop=True)
                    ins.then_inc(s["g_ps"], 1)
                    if not last:
                        pe.wait_ge(s["q_used"], b + 1)
                        project_q(b + 1, 1 - slot)
                    if not first:
                        expert_rows_t(b - 1, 1 - slot)
                    if not last:
                        pe.wait_ge(s["kvb_ready"], b + 1)
                        project_kv(b + 1, 1 - slot)
                    if not first:
                        logits_of(b - 1)
                    pe.wait_ge(s["g_ready"], b + 1)
                    pe.wait_ge(s["qr_ready"], b + 1)
                    if not first:
                        pe.wait_ge(s["h_done"], b)
                    for g in range(KD):
                        ins = nc.tensor.matmul(bank[3][0:1, D:2 * D], qc0[:, g, 0:1], gs[:, g, :], start=(g == 0), stop=(g == KD - 1))
                    ins.then_inc(s["cls_ps"], 1)
                    for t in range(TPB):
                        for g in range(KD):
                            ins = nc.tensor.matmul(bank[5][:, D * t:D * t + D], qt0[slot][:, g, P * t:P * t + P], gs[:, g, :],
                                                   start=(g == 0), stop=(g == KD - 1))
                    ins.then_inc(s["out_ps"], 1)

                per_image(pe, image)
                pe.wait_ge(s["lg_done"], B)
                expert_rows_t(B - 1, (B - 1) % 2)
                logits_of(B - 1)

        names = ("cls_in hcb hcls stat aggr var rstd xcls xct_ps xct lg_ps lg mx cw_d cw_e best_d oh_w best oh cls_m rank_ps "
                 "rk_zero rk step idx scattered").split()
        s = {n: early_sem("r_" + n) for n in names}
        hcb = sb("hcb", [B, D], scope=scope)
        x1ct = sb("x1ct", [P, KD, B], scope=scope)
        route = sb("route", [P, 6, NTC], scope=scope)
        oh = sb("oh", [P, NTC, E], scope=scope)
        wt = sb("wt", [P, NTC, E], scope=scope)
        wt2 = sb("wt2", [P, NTC, E], scope=scope)
        rk = sb("rk", [P, NTC, E], scope=scope)
        ohcm = sb("ohcm", [B, NT, E], scope=scope)
        with nc.Block() as block:
            @block.sync
            def _(sp):
                for b in range(B):
                    sp.dma_start(clsatt[b:b + 1, :], clsrow[0:1, b, :]).then_inc(s["cls_in"], 16)
                sp.wait_ge(s["cls_in"], 16 * B)

            @block.gpsimd
            def _(pool):
                nc.gpsimd.tensor_tensor(hcb[:, :], clsb[:, :], bo0[0:B, :], ALU.add).then_inc(s["hcb"], 1)
                pool.wait_ge(s["aggr"], 1)
                nc.gpsimd.tensor_scalar(varc[:, :], mvc[:, 1:2], EPS, None, ALU.add).then_inc(s["var"], 1)
                pool.wait_ge(s["var"], 1)
                nc.gpsimd.tensor_tensor(rstdc[:, :], varc[:, :], nh16[0:B, 0:1], ALU.pow).then_inc(s["rstd"], 1)
                pool.wait_ge(s["idx"], 3)
                for t in range(NT):
                    nc.gpsimd.indirect_dma_start(buf[0:SLOTS, :], bass.IndirectOffsetOnAxis(to_slot[:, t:t + 1], 0), xrow[:, t, :], None,
                                                 bounds_check=SLOTS - 1, oob_is_err=False).then_inc(s["scattered"], 16)
                nc.gpsimd.indirect_dma_start(buf[0:SLOTS, :], bass.IndirectOffsetOnAxis(to_slot[0:B, NT:NTC], 0), xcls[:, :], None,
                                             bounds_check=SLOTS - 1, oob_is_err=False).then_inc(s["scattered"], 16)
                pool.wait_ge(s["scattered"], 16 * NTC)

            @block.vector
            def _(dve):
                dve.wait_ge(s["cls_in"], 16 * B)
                dve.wait_ge(s["hcb"], 1)
                nc.vector.tensor_tensor(hcls[:, :], clsatt[:, :], hcb[:, :], ALU.add).then_inc(s["hcls"], 1)
                dve.wait_ge(s["hcls"], 1)
                nc.vector.bn_stats(statc[:, :], hcls[:, :]).then_inc(s["stat"], 1)
                dve.wait_ge(s["stat"], 1)
                nc.vector.bn_aggr(mvc[:, :], statc[:, :]).then_inc(s["aggr"], 1)
                nc.vector.memset(rk[:, :, :], 0.0).then_inc(s["rk_zero"], 1)
                dve.wait_ge(s["rstd"], 1)
                dve.wait_ge(s["aggr"], 1)
                nc.vector.tensor_scalar(xcls[:, :], hcls[:, :], mvc[:, 0:1], rstdc[:, 0:1], ALU.subtract, ALU.mult).then_inc(s["xcls"], 1)
                dve.wait_ge(s["lg"], 1)
                lg = logits[:, :, :]
                mx, total, prob, rank, slot, valid = (route[:, i, :] for i in range(6))
                nc.vector.tensor_reduce(mx, lg, AX.X, ALU.max).then_inc(s["mx"], 1)
                dve.wait_ge(s["mx"], 1)
                nc.vector.tensor_tensor(wt[:, :, :], lg, rep(mx, 2, E), ALU.subtract).then_inc(s["cw_d"], 1)
                nc.vector.tensor_tensor(oh[:, :, :], lg, rep(mx, 2, E), ALU.is_equal).then_inc(s["best_d"], 1)
                dve.wait_ge(s["best_d"], 1)
                nc.vector.tensor_tensor(wt2[:, :, :], oh[:, :, :], mat("order").rearrange("p (t e) -> p t e", e=E), ALU.mult).then_inc(s["oh_w"], 1)
                dve.wait_ge(s["oh_w"], 1)
                nc.vector.tensor_reduce(rank, wt2[:, :, :], AX.X, ALU.max).then_inc(s["best"], 1)
                dve.wait_ge(s["best"], 1)
                nc.vector.tensor_tensor(oh[:, :, :], wt2[:, :, :], rep(rank, 2, E), ALU.is_equal).then_inc(s["oh"], 1)
                dve.wait_ge(s["oh"], 1)
                nc.vector.tensor_tensor(ohcm[:, :, :], rep(oh[0:B, NT, :], 1, NT), mat("before", B).rearrange("p (t e) -> p t e", e=E), ALU.mult).then_inc(s["cls_m"], 1)
                dve.wait_ge(s["cw_e"], 1)
                nc.vector.tensor_reduce(total, wt[:, :, :], AX.X, ALU.add).then_inc(s["step"], 1)
                dve.wait_ge(s["step"], 1)
                nc.vector.reciprocal(prob, total).then_inc(s["step"], 1)
                dve.wait_ge(s["rank_ps"], 2)
                dve.wait_ge(s["rk_zero"], 1)
                nc.vector.tensor_copy(rk[:, 0:NT, :], bank[2][:, 0:NT * E].rearrange("p (t e) -> p t e", e=E)).then_inc(s["rk"], 1)
                nc.vector.tensor_copy(rk[0:B, NT, :], bank[3][0:B, 0:E]).then_inc(s["rk"], 1)
                dve.wait_ge(s["rk"], 2)
                nc.vector.tensor_tensor(wt2[:, :, :], rk[:, :, :], oh[:, :, :], ALU.mult).then_inc(s["step"], 1)
                nc.vector.tensor_tensor(rk[:, :, :], rk[:, :, :], mat("first_slot").rearrange("p (t e) -> p t e", e=E), ALU.add).then_inc(s["step"], 1)
                dve.wait_ge(s["step"], 4)
                nc.vector.tensor_reduce(rank, wt2[:, :, :], AX.X, ALU.add).then_inc(s["step"], 1)
                nc.vector.tensor_tensor(rk[:, :, :], rk[:, :, :], oh[:, :, :], ALU.mult).then_inc(s["step"], 1)
                dve.wait_ge(s["step"], 6)
                nc.vector.tensor_reduce(slot, rk[:, :, :], AX.X, ALU.add).then_inc(s["step"], 1)
                nc.vector.tensor_scalar(valid, rank, float(CAP), None, ALU.is_le).then_inc(s["step"], 1)
                dve.wait_ge(s["step"], 8)
                nc.vector.tensor_tensor(weight[:, :], prob, valid, ALU.mult).then_inc(s["idx"], 1)
                nc.vector.tensor_scalar(from_slot[:, :], slot, float(SLOTS - 1), 0.0, ALU.min, ALU.max).then_inc(s["idx"], 1)
                nc.vector.tensor_scalar(mx, valid, -float(FAR), float(FAR), ALU.mult, ALU.add).then_inc(s["step"], 1)
                dve.wait_ge(s["step"], 9)
                nc.vector.tensor_tensor(total, mx, slot, ALU.add).then_inc(s["step"], 1)
                dve.wait_ge(s["step"], 10)
                nc.vector.tensor_scalar(to_slot[:, :], total, 0.0, None, ALU.max).then_inc(s["idx"], 1)

            @block.scalar
            def _(act):
                for h in range(H1):
                    act.wait_ge(bias["flip_ps"], h + 1)
                    nc.scalar.copy(toeplitz[:, h, :], bank[4 + h % 2][:, 0:SCOLS]).then_inc(bias["flip_out"], 1)
                act.wait_ge(s["xct_ps"], 1)
                nc.scalar.copy(x1ct[:, :, :], bank[0][:, 0:KD * B].rearrange("p (k b) -> p k b", k=KD)).then_inc(s["xct"], 1)
                act.wait_ge(s["lg_ps"], 1)
                nc.scalar.copy(logits[0:B, NT, :], bank[1][0:B, 0:E]).then_inc(s["lg"], 1)
                act.wait_ge(s["cw_d"], 1)
                nc.scalar.activation(wt[:, :, :], wt[:, :, :], ACT.Exp).then_inc(s["cw_e"], 1)

            @block.tensor
            def _(pe):
                pe.wait_ge(bias["rev_in"], 16 * TPB)
                for h in range(H1):
                    if h >= 2:
                        pe.wait_ge(bias["flip_out"], h - 1)
                    nc.tensor.matmul(bank[4 + h % 2][:, 0:SCOLS], mat("flip"), hankel[:, h, :], start=True, stop=True).then_inc(bias["flip_ps"], 1)
                pe.wait_ge(s["xcls"], 1)
                for k in range(KD):
                    ins = nc.tensor.transpose(bank[0][:, B * k:B * k + B], xcls[:, P * k:P * k + P], mat("ident", B)[:, 0:B])
                ins.then_inc(s["xct_ps"], 1)
                pe.wait_ge(s["xct"], 1)
                for k in range(KD):
                    ins = nc.tensor.matmul(bank[1][0:B, 0:E], x1ct[:, k, :], wg[:, k, :], start=(k == 0), stop=(k == KD - 1))
                ins.then_inc(s["lg_ps"], 1)
                pe.wait_ge(s["cls_m"], 1)
                ranks = bank[2][:, 0:NT * E]
                nc.tensor.matmul(ranks, mat("tri"), oh[:, 0:NT, :], start=True, stop=False)
                for t in range(NT - 1):
                    nc.tensor.matmul(bank[2][:, E * (t + 1):E * NT], ones, rep(oh[:, t, :], 1, NT - 1 - t), start=False, stop=False)
                nc.tensor.matmul(ranks, mat("ones", B), ohcm[:, :, :], start=False, stop=True).then_inc(s["rank_ps"], 1)
                nc.tensor.matmul(bank[3][0:B, 0:E], mat("tri8", B), oh[0:B, NT, :], start=True, stop=False)
                after = mat("after").rearrange("p (j b) -> p j b", b=B)
                for t in range(NT):
                    ins = nc.tensor.matmul(bank[3][0:B, 0:E], after[:, t // TPB, :], oh[:, t, :], start=False, stop=(t == NT - 1))
                ins.then_inc(s["rank_ps"], 1)
        scope.close()
        attn0.close()
        nc.clear_and_free_semaphores(early)
        nc.all_engine_barrier()
        scope = ExitStack()
        b1rows = sb("b1rows", [E * KF, P], scope=scope)
        b1t = sb("b1t", [P, E * KF], scope=scope)
        b2b = sb("b2b", [P, E, D], scope=scope)
        xe = [sb(f"xe_{i}", [MR, MT, D], scope=scope) for i in range(2)]
        xet = [sb(f"xet_{i}", [P, KD, MT * MR], scope=scope) for i in range(2)]
        ht = sb("ht", [P, KF, MT * MR], scope=scope)
        ys = [sb(f"ys_{i}", [MR, MT, D], scope=scope) for i in range(2)]
        names = "b_in b1_ps b1t xet_ps xet h_ps gelu y_ps y_ready f2_done".split()
        s = {n: sem("e_" + n) for n in names}
        xe_in = [sem(f"xe_in{i}") for i in range(2)]
        y_out = [sem(f"y_out{i}") for i in range(2)]
        last_rows = CAP - (MT - 1) * MR

        def per_expert(eng, body):
            body(0, 0, 1, True, False)
            with eng.Fori(0, E // 2 - 1) as pair:
                body(pair * 2 + 1, 1, pair + 1, False, False)
                body(pair * 2 + 2, 0, pair + 2, False, False)
            body(E - 1, (E - 1) % 2, E // 2, False, True)

        with nc.Block() as block:
            @block.sync
            def _(sp):
                def load_rows(e, slot):
                    sp.dma_start(xe[slot][:, :, :], buf[bass.ds(e * CAP, MT * MR), :].rearrange("(t p) d -> p t d", p=MR)).then_inc(xe_in[slot], 16)

                load_rows(0, 0)
                sp.dma_start(b1rows[:, :], dram["L0_ffn_b1"].rearrange("e (m p) -> (e m) p", p=P)).then_inc(s["b_in"], 16)
                sp.dma_start(b2b[:, :, :], dram["L0_ffn_b2"].partition_broadcast(P)).then_inc(s["b_in"], 16)

                def expert(e, slot, use, first, last):
                    if not last:
                        if not first:
                            sp.wait_ge(s["xet_ps"], e)
                        load_rows(e + 1, 1 - slot)
                        if not first:
                            sp.wait_ge(s["f2_done"], e)
                            w1_of, w2_of = (dram[n][bass.ds(e + 1, 1)].rearrange("o (k p) n -> p (o k) n", p=P) for n in ("L0_ffn_W1", "L0_ffn_W2"))
                            sp.dma_start(w1e[1 - slot][:, :, :], w1_of).then_inc(w1e_in[1 - slot], 16)
                            sp.dma_start(w2e[1 - slot][:, :, :], w2_of).then_inc(w2e_in[1 - slot], 16)
                    sp.wait_ge(s["y_ready"], 2 * e + 2)
                    whole = (MT - 1) * MR
                    sp.dma_start(ybuf[bass.ds(e * CAP, whole), :].rearrange("(t p) d -> p t d", p=MR), ys[slot][:, 0:MT - 1, :]).then_inc(y_out[slot], 16)
                    sp.dma_start(ybuf[bass.ds(e * CAP + whole, last_rows), :], ys[slot][0:last_rows, MT - 1, :]).then_inc(y_out[slot], 16)

                per_expert(sp, expert)
                for slot in range(2):
                    sp.wait_ge(y_out[slot], 32 * (E // 2 + 1))
                sp.dma_start(w1e[0][:, :, :], dram["L1_ffn_w1"].rearrange("(k p) f -> p k f", p=P)).then_inc(w1e_in[0], 16)
                sp.dma_start(w2e[0][:, :, :], dram["L1_ffn_w2"].rearrange("(k p) d -> p k d", p=P)).then_inc(w2e_in[0], 16)

            @block.vector
            def _(dve):
                for slot in range(2):
                    dve.sem_inc(y_out[slot], 32)
                dve.wait_ge(s["b1_ps"], 1)
                nc.vector.tensor_copy(b1t[:, :], bank[5][:, 0:E * KF]).then_inc(s["b1t"], 1)
                dve.wait_ge(s["b_in"], 32)

                def expert(e, slot, use, first, last):
                    dve.wait_ge(s["y_ps"], e + 1)
                    dve.wait_ge(y_out[slot], use * 32)
                    bias = b2b[0:MR, bass.ds(e, 1), :]
                    nc.vector.tensor_tensor(ys[slot][:, 0:2, :], bank[3][0:MR, :].rearrange("p (t d) -> p t d", t=2),
                                            rep(bias.rearrange("p o d -> p (o d)"), 1, 2), ALU.add).then_inc(s["y_ready"], 1)
                    nc.vector.tensor_tensor(ys[slot][:, 2, :], bank[4][0:MR, 0:D], bias.rearrange("p o d -> p (o d)"), ALU.add).then_inc(s["y_ready"], 1)

                per_expert(dve, expert)

            @block.scalar
            def _(act):
                def evac_rows(e, slot):
                    act.wait_ge(s["xet_ps"], e + 1)
                    for k in range(KD):
                        ins = nc.scalar.copy(xet[slot][:, k, :], bank[k][:, 0:MT * MR])
                    ins.then_inc(s["xet"], 1)

                evac_rows(0, 0)
                act.wait_ge(s["b1t"], 1)

                def expert(e, slot, use, first, last):
                    for m in range(KF):
                        act.wait_ge(s["h_ps"], e * KF + m + 1)
                        nc.scalar.activation(ht[:, m, :], kvbank[:, m % 2, 0:MT * MR], ACT.Gelu, bias=b1t[:, bass.ds(e * KF + m, 1)]).then_inc(s["gelu"], 1)
                    if not last:
                        evac_rows(e + 1, 1 - slot)

                per_expert(act, expert)

            @block.tensor
            def _(pe):
                def turn_rows(e, slot, use):
                    pe.wait_ge(xe_in[slot], use * 16)
                    for k in range(KD):
                        for t in range(MT):
                            ins = nc.tensor.transpose(bank[k][:, MR * t:MR * t + MR], xe[slot][:, t, P * k:P * k + P], mat("ident", MR)[:, 0:MR])
                    ins.then_inc(s["xet_ps"], 1)

                pe.wait_ge(s["b_in"], 32)
                nc.tensor.transpose(bank[5][:, 0:E * KF], b1rows[:, :], mat("ident", E * KF)[:, 0:E * KF]).then_inc(s["b1_ps"], 1)
                turn_rows(0, 0, 1)

                def expert(e, slot, use, first, last):
                    pe.wait_ge(w1e_in[slot], use * 16)
                    pe.wait_ge(s["xet"], e + 1)
                    for m in range(KF):
                        if not (first and m < 2):
                            pe.wait_ge(s["gelu"], e * KF + m - 1)
                        for k in range(KD):
                            ins = nc.tensor.matmul(kvbank[:, m % 2, 0:MT * MR], w1e[slot][:, k, P * m:P * m + P], xet[slot][:, k, :],
                                                   start=(k == 0), stop=(k == KD - 1))
                        ins.then_inc(s["h_ps"], 1)
                    if not last:
                        turn_rows(e + 1, 1 - slot, use + slot)
                    pe.wait_ge(w2e_in[slot], use * 16)
                    if not first:
                        pe.wait_ge(s["y_ready"], 2 * e)
                    for t in range(MT):
                        o = bank[3][0:MR, D * t:D * t + D] if t < 2 else bank[4][0:MR, 0:D]
                        for m in range(KF):
                            if t == 0:
                                pe.wait_ge(s["gelu"], e * KF + m + 1)
                            ins = nc.tensor.matmul(o, ht[:, m, MR * t:MR * t + MR], w2e[slot][:, m, :], start=(m == 0), stop=(m == KF - 1))
                    ins.then_inc(s["y_ps"], 1)
                    pe.sem_inc(s["f2_done"], 1)

                per_expert(pe, expert)
        scope.close()

        x2ct = sb("x2ct", [P, KD, B])
        gath = [sem(f"gathered{t}") for t in range(NTC)]
        scope = ExitStack()
        stat2 = sb("stat2", [P, NTC, 6], scope=scope)
        mv2 = sb("mv2", [P, NT, 2], scope=scope)
        var2 = sb("var2", [P, NT], scope=scope)
        rstd2 = sb("rstd2", [P, NT], scope=scope)
        nh2 = sb("nh2", [P, NT], scope=scope)
        mvc2 = sb("mvc2", [B, 2], scope=scope)
        varc2 = sb("varc2", [B, 1], scope=scope)
        rstdc2 = sb("rstdc2", [B, 1], scope=scope)
        xc2 = sb("xc2", [B, D], scope=scope)
        oc = sb("oc", [B, INNER], scope=scope)
        oct_ = sb("oct", [P, KI, B], scope=scope)
        hcb2 = sb("hcb2", [B, D], scope=scope)
        g = {n: sem("g_" + n) for n in "h2 h2c stat statc aggr aggrc var rstd nh xc xct_ps xct oc_ps oc oct_ps oct oo_ps hcb hcls".split()}
        xn2 = [sb(f"xn2_{i}", [P, TPB, D], scope=scope) for i in range(2)]
        x2t = [sb(f"x2t_{i}", [P, KD, POS], scope=scope) for i in range(2)]
        qk = [sb(f"qk_{i}", [P, 2 * KI, POS], scope=scope) for i in range(2)]
        vrow = [sb(f"vrow_{i}", [P, TPB, INNER], scope=scope) for i in range(2)]
        vcls = [sb(f"vcls_{i}", [P, INNER], scope=scope) for i in range(2)]
        sx = [sb(f"sx_{i}", [P, SCOLS], scope=scope) for i in range(2)]
        low = sb("low", [P, 2, TPB], scope=scope)
        prob = sb("prob", [P, H1, SCOLS], scope=scope)
        total = [sb(f"total_{i}", [P, TPB, H1], scope=scope) for i in range(2)]
        inv = sb("inv", [P, TPB, H1], scope=scope)
        pt = [sb(f"pt_{i}", [P, 3 * P], scope=scope) for i in range(2)]
        osb = sb("osb", [P, TPB, INNER], scope=scope)
        ot = sb("ot", [P, KI, ROWS], scope=scope)
        xcb = [sb(f"xcb_{i}", [P, KD, P], scope=scope) for i in range(2)]
        names = ("xn2 x2t_ps x2t x2c xcb qk_ps even_out odd_out vc_ps vc s_ps smax p_done pt_ps pt pv inv o_tmp o_add o_fin "
                 "ot_ps ot wo_ps hb h_done").split()
        s = {n: sem("b_" + n) for n in names}
        UNITS = 2 * KI + TPB
        HALF = UNITS // 2
        tile_at = (0, 1 + P)

        with nc.Block() as block:
            @block.gpsimd
            def _(pool):
                def fetch(t):
                    nc.gpsimd.indirect_dma_start(xrow[:, t, :], None, ybuf[:, :], bass.IndirectOffsetOnAxis(from_slot[:, t:t + 1], 0)).then_inc(gath[t], 16)

                nc.gpsimd.indirect_dma_start(xcls[:, :], None, ybuf[:, :], bass.IndirectOffsetOnAxis(from_slot[0:B, NT:NTC], 0)).then_inc(gath[NT], 16)
                for t in range(2 * TPB):
                    fetch(t)
                nc.gpsimd.memset(nh2[:, :], -0.5).then_inc(g["nh"], 1)
                pool.wait_ge(g["nh"], 1)
                pool.wait_ge(g["aggrc"], 1)
                nc.gpsimd.tensor_scalar(varc2[:, :], mvc2[:, 1:2], EPS, None, ALU.add).then_inc(g["var"], 1)
                pool.wait_ge(g["var"], 1)
                nc.gpsimd.tensor_tensor(rstdc2[:, :], varc2[:, :], nh2[0:B, 0:1], ALU.pow).then_inc(g["rstd"], 1)

                def deviations(n, t0, t1):
                    pool.wait_ge(g["aggr"], t1)
                    nc.gpsimd.tensor_scalar(var2[:, t0:t1], mv2[:, t0:t1, 1], EPS, None, ALU.add).then_inc(g["var"], 1)
                    pool.wait_ge(g["var"], n)
                    nc.gpsimd.tensor_tensor(rstd2[:, t0:t1], var2[:, t0:t1], nh2[:, t0:t1], ALU.pow).then_inc(g["rstd"], 1)

                deviations(2, 0, TPB)
                for t in range(2 * TPB, NT):
                    fetch(t)
                nc.gpsimd.tensor_tensor(hcb2[:, :], hcls[:, :], bo1[0:B, :], ALU.add).then_inc(g["hcb"], 1)
                deviations(3, TPB, NT)

                def cls_column(b, slot):
                    nc.gpsimd.tensor_copy(x2t[slot][:, :, 0:1], x2ct[:, :, bass.ds(b, 1)]).then_inc(s["x2c"], 1)
                    nc.gpsimd.tensor_copy(xcb[slot][:, :, :], x2ct[:, :, bass.ds(b, 1)].broadcast_to([P, KD, P])).then_inc(s["xcb"], 1)

                def image(b, slot, first, last):
                    if not last:
                        if not first:
                            pool.wait_ge(s["vc_ps"], b)
                        cls_column(b + 1, 1 - slot)
                    pool.wait_ge(s["xn2"], b + 1)
                    nc.gpsimd.tensor_tensor(hrow[:, tiles(b), :], hrow[:, tiles(b), :], rep(bo1[:, :], 1, TPB), ALU.add).then_inc(s["hb"], 1)
                    pool.wait_ge(s["p_done"], H1 * b + H1)
                    pool.wait_ge(s["vc"], b + 1)
                    if not first:
                        pool.wait_ge(s["ot_ps"], TPB * b)
                    for t in range(TPB):
                        nc.gpsimd.tensor_tensor(osb[:, t, :].rearrange("p (h d) -> p h d", h=H1), vcls[slot][:, :].rearrange("p (h d) -> p h d", h=H1),
                                                rep(prob[:, :, tile_at[t]], 2, HD1), ALU.mult).then_inc(s["o_tmp"], 1)
                    pool.wait_ge(s["inv"], b + 1)
                    for t in range(TPB):
                        pool.wait_ge(s["o_add"], TPB * b + t + 1)
                        o = osb[:, t, :].rearrange("p (h d) -> p h d", h=H1)
                        nc.gpsimd.tensor_tensor(o, o, rep(inv[:, t, :], 2, HD1), ALU.mult).then_inc(s["o_fin"], 1)

                per_image(pool, image)

            @block.vector
            def _(dve):
                def norm2(b, slot):
                    for t in range(TPB):
                        at = bass.ds(b * TPB + t, 1)
                        ins = nc.vector.tensor_scalar(xn2[slot][:, t, :], hrow[:, at, :].rearrange("p o d -> p (o d)"),
                                                      mv2[:, at, 0:1].rearrange("p o d -> p (o d)"), rstd2[:, at], ALU.subtract, ALU.mult)
                    ins.then_inc(s["xn2"], 1)

                def even_unit(b, slot, u):
                    dve.wait_ge(s["qk_ps"], UNITS * b + u + 1)
                    if u < 2 * KI:
                        nc.vector.tensor_copy(qk[slot][:, u, :], kvbank[:, 0, 0:POS]).then_inc(s["even_out"], 1)
                    else:
                        nc.vector.tensor_copy(vrow[slot][:, u - 2 * KI, :], kvbank[:, 0, :]).then_inc(s["even_out"], 1)

                def scores(b, h, first):
                    used = [] if first and h < 2 else [(s["p_done"], H1 * b + h - 1)]
                    waits_apart(dve, (s["s_ps"], H1 * b + h + 1), *used)
                    for t in range(TPB):
                        at, n = tile_at[t], 1 + P * (t + 1)
                        ins = nc.vector.tensor_tensor_reduce(sx[h % 2][:, at:at + n], bank[1 + h % 2][:, at:at + n], toeplitz[:, h, at:at + n],
                                                             -0.125, 3e38, ALU.add, ALU.min, low[:, h % 2, t:t + 1])
                    ins.then_inc(s["smax"], 1)

                def take(t):
                    dve.wait_ge(gath[t], 16)
                    nc.vector.scalar_tensor_tensor(hrow[:, t, :], xrow[:, t, :], weight[:, t:t + 1], hrow[:, t, :], ALU.mult, ALU.add).then_inc(g["h2"], 1)
                    dve.wait_ge(g["h2"], t + 1)
                    nc.vector.bn_stats(stat2[:, t, :], hrow[:, t, :]).then_inc(g["stat"], 1)
                    dve.wait_ge(g["stat"], t + 1)
                    nc.vector.bn_aggr(mv2[:, t, :], stat2[:, t, :]).then_inc(g["aggr"], 1)

                dve.wait_ge(gath[NT], 16)
                nc.vector.scalar_tensor_tensor(hcls[:, :], xcls[:, :], weight[0:B, NT:NTC], hcls[:, :], ALU.mult, ALU.add).then_inc(g["h2c"], 1)
                dve.wait_ge(g["h2c"], 1)
                nc.vector.bn_stats(stat2[0:B, NT, :], hcls[:, :]).then_inc(g["statc"], 1)
                dve.wait_ge(g["statc"], 1)
                nc.vector.bn_aggr(mvc2[:, :], stat2[0:B, NT, :]).then_inc(g["aggrc"], 1)
                for t in range(TPB):
                    take(t)
                dve.wait_ge(g["rstd"], 1)
                dve.wait_ge(g["aggrc"], 1)
                nc.vector.tensor_scalar(xc2[:, :], hcls[:, :], mvc2[:, 0:1], rstdc2[:, 0:1], ALU.subtract, ALU.mult).then_inc(g["xc"], 1)
                dve.wait_ge(g["rstd"], 2)
                dve.wait_ge(g["aggr"], TPB)
                norm2(0, 0)
                t = TPB
                for u in range(0, UNITS, 2):
                    for _ in range(3):
                        if t < NT:
                            take(t)
                            t += 1
                    even_unit(0, 0, u)
                dve.wait_ge(g["oo_ps"], 1)
                dve.wait_ge(g["hcb"], 1)
                dve.wait_ge(g["xc"], 1)
                nc.vector.tensor_tensor(hcls[:, :], bank[5][0:B, 0:D], hcb2[:, :], ALU.add).then_inc(g["hcls"], 1)
                dve.wait_ge(g["rstd"], 3)
                dve.wait_ge(g["aggr"], NT)

                def image(b, slot, first, last):
                    if not last:
                        if not first:
                            dve.wait_ge(s["x2t_ps"], b)
                        norm2(b + 1, 1 - slot)
                    scores(b, 0, first)
                    scores(b, 1, first)
                    for h in range(H1):
                        if h + 2 < H1:
                            scores(b, h + 2, first)
                        if h % 2 == 0 and not last:
                            even_unit(b + 1, 1 - slot, h)
                        dve.wait_ge(s["pt_ps"], H1 * b + h + 1)
                        if not (first and h < 2):
                            dve.wait_ge(s["pv"], H1 * b + h - 1)
                        nc.vector.tensor_copy(pt[h % 2][:, :], bank[3][:, 0:3 * P]).then_inc(s["pt"], 1)
                        if h == 3 and not first:
                            dve.wait_ge(s["wo_ps"], b)
                            dve.wait_ge(s["hb"], b)
                            nc.vector.tensor_tensor(hrow[:, tiles(b - 1), :], bank[0][:, :].rearrange("p (t d) -> p t d", t=TPB),
                                                    hrow[:, tiles(b - 1), :], ALU.add).then_inc(s["h_done"], 1)
                    if not last:
                        even_unit(b + 1, 1 - slot, H1)
                    dve.wait_ge(s["p_done"], H1 * b + H1)
                    if not first:
                        dve.wait_ge(s["o_fin"], TPB * b)
                    nc.vector.reciprocal(inv[:, :, :], total[slot][:, :, :]).then_inc(s["inv"], 1)
                    dve.wait_ge(s["pv"], H1 * b + H1)
                    for t in range(TPB):
                        dve.wait_ge(s["o_tmp"], TPB * b + t + 1)
                        nc.vector.tensor_tensor(osb[:, t, :], bank[4 + t][:, :], osb[:, t, :], ALU.add).then_inc(s["o_add"], 1)

                per_image(dve, image)
                dve.wait_ge(s["wo_ps"], B)
                dve.wait_ge(s["hb"], B)
                nc.vector.tensor_tensor(hrow[:, tiles(B - 1), :], bank[0][:, :].rearrange("p (t d) -> p t d", t=TPB),
                                        hrow[:, tiles(B - 1), :], ALU.add).then_inc(s["h_done"], 1)

            @block.scalar
            def _(act):
                def rows_t(b, slot, early):
                    act.wait_ge(s["x2t_ps"], b + 1)
                    if not early:
                        act.wait_ge(s["vc_ps"], b - 1)
                    nc.scalar.copy(x2t[slot][:, :, 1:POS], bank[0][:, :].rearrange("p (k n) -> p k n", k=KD)).then_inc(s["x2t"], 1)

                def odd_unit(b, slot, u):
                    act.wait_ge(s["qk_ps"], UNITS * b + u + 1)
                    if u < 2 * KI:
                        nc.scalar.copy(qk[slot][:, u, :], kvbank[:, 1, 0:POS]).then_inc(s["odd_out"], 1)
                    else:
                        nc.scalar.copy(vrow[slot][:, u - 2 * KI, :], kvbank[:, 1, :]).then_inc(s["odd_out"], 1)

                def cls_v(b, slot):
                    act.wait_ge(s["vc_ps"], b + 1)
                    nc.scalar.copy(vcls[slot][:, :], bank[0][:, :]).then_inc(s["vc"], 1)

                def out_t(b, t):
                    act.wait_ge(s["ot_ps"], TPB * b + t + 1)
                    nc.scalar.copy(ot[:, :, P * t:P * t + P], bank[0][:, :].rearrange("p (c n) -> p c n", c=KI)).then_inc(s["ot"], 1)

                act.wait_ge(g["xct_ps"], 1)
                nc.scalar.copy(x2ct[:, :, :], bank[1][:, 0:KD * B].rearrange("p (k b) -> p k b", k=KD)).then_inc(g["xct"], 1)
                first_cls = bank[1][:, 0:KD * B].rearrange("p (k b) -> p k b", k=KD)[:, :, 0:1]
                nc.scalar.copy(x2t[0][:, :, 0:1], first_cls).then_inc(s["x2c"], 1)
                nc.scalar.copy(xcb[0][:, :, :], first_cls.broadcast_to([P, KD, P])).then_inc(s["xcb"], 1)
                rows_t(0, 0, True)
                odd_unit(0, 0, 1)
                odd_unit(0, 0, 3)
                act.wait_ge(g["oc_ps"], 1)
                nc.scalar.copy(oc[:, :], bank[3][0:B, :]).then_inc(g["oc"], 1)
                odd_unit(0, 0, 5)
                act.wait_ge(g["oct_ps"], 1)
                nc.scalar.copy(oct_[:, :, :], bank[4][:, 0:KI * B].rearrange("p (k b) -> p k b", k=KI)).then_inc(g["oct"], 1)
                for u in range(7, UNITS, 2):
                    odd_unit(0, 0, u)
                cls_v(0, 0)

                def image(b, slot, first, last):
                    if not last:
                        rows_t(b + 1, 1 - slot, first)
                    for h in range(H1):
                        act.wait_ge(s["smax"], H1 * b + h + 1)
                        if h == 0 and not first:
                            act.wait_ge(s["pt_ps"], H1 * b)
                            act.wait_ge(s["o_tmp"], TPB * b)
                            act.wait_ge(s["inv"], b)
                        for t in range(TPB):
                            at, n = tile_at[t], 1 + P * (t + 1)
                            ins = nc.scalar.activation(prob[:, h, at:at + n], sx[h % 2][:, at:at + n], ACT.Exp, bias=low[:, h % 2, t:t + 1],
                                                       scale=-1.0, accum_out=total[slot][:, t, h:h + 1])
                        ins.then_inc(s["p_done"], 1)
                        if h < TPB and not first:
                            out_t(b - 1, h)
                        if h % 2 == 1 and not last:
                            odd_unit(b + 1, 1 - slot, h)
                    if not last:
                        odd_unit(b + 1, 1 - slot, H1 + 1)
                        cls_v(b + 1, 1 - slot)

                per_image(act, image)
                for t in range(TPB):
                    out_t(B - 1, t)

            @block.tensor
            def _(pe):
                def turn_rows(b, slot):
                    pe.wait_ge(s["xn2"], b + 1)
                    for k in range(KD):
                        for t in range(TPB):
                            ins = nc.tensor.transpose(bank[0][:, ROWS * k + P * t:ROWS * k + P * t + P], xn2[slot][:, t, P * k:P * k + P], ident)
                    ins.then_inc(s["x2t_ps"], 1)

                def unit(b, slot, u, early):
                    if not (early and u < 2):
                        pe.wait_ge(s["odd_out" if u % 2 else "even_out"], HALF * b + u // 2)
                    for k in range(KD):
                        if u < 2 * KI:
                            w = wq1[:, k, P * u:P * u + P] if u < KI else wkv1[:, k, P * (u - KI):P * (u - KI) + P]
                            ins = nc.tensor.matmul(kvbank[:, u % 2, 0:POS], w, x2t[slot][:, k, :], start=(k == 0), stop=(k == KD - 1))
                        else:
                            at = 1 + P * (u - 2 * KI)
                            ins = nc.tensor.matmul(kvbank[:, u % 2, :], x2t[slot][:, k, at:at + P], wkv1[:, k, INNER:2 * INNER], start=(k == 0), stop=(k == KD - 1))
                    ins.then_inc(s["qk_ps"], 1)

                def cls_v(b, slot):
                    for k in range(KD):
                        ins = nc.tensor.matmul(bank[0][:, :], xcb[slot][:, k, :], wkv1[:, k, INNER:2 * INNER], start=(k == 0), stop=(k == KD - 1))
                    ins.then_inc(s["vc_ps"], 1)

                def scores(b, slot, h, first):
                    if not (first and h < 2):
                        pe.wait_ge(s["smax"], H1 * b + h - 1)
                    rows = slice(HD1 * (h % 2), HD1 * (h % 2) + HD1)
                    for t in range(TPB):
                        at, n = tile_at[t], 1 + P * (t + 1)
                        ins = nc.tensor.matmul(bank[1 + h % 2][:, at:at + n], qk[slot][rows, h // 2, 1 + P * t:1 + P * t + P],
                                               qk[slot][rows, KI + h // 2, 0:n], start=True, stop=True)
                    ins.then_inc(s["s_ps"], 1)

                def turn_probs(b, h, first):
                    pe.wait_ge(s["p_done"], H1 * b + h + 1)
                    if not (first and h == 0):
                        pe.wait_ge(s["pt"], H1 * b + h)
                    for i, at in enumerate((1, 2 + P, 2 + 2 * P)):
                        ins = nc.tensor.transpose(bank[3][:, P * i:P * i + P], prob[:, h, at:at + P], ident)
                    ins.then_inc(s["pt_ps"], 1)

                def weighted(b, slot, h):
                    pe.wait_ge(s["pt"], H1 * b + h + 1)
                    cols = slice(HD1 * h, HD1 * h + HD1)
                    nc.tensor.matmul(bank[4][:, cols], pt[h % 2][:, 0:P], vrow[slot][:, 0, cols], start=True, stop=True)
                    nc.tensor.matmul(bank[5][:, cols], pt[h % 2][:, P:2 * P], vrow[slot][:, 0, cols], start=True, stop=False)
                    nc.tensor.matmul(bank[5][:, cols], pt[h % 2][:, 2 * P:3 * P], vrow[slot][:, 1, cols], start=False, stop=True).then_inc(s["pv"], 1)

                def turn_out(b, t):
                    pe.wait_ge(s["o_fin"], TPB * b + t + 1)
                    for c in range(KI):
                        ins = nc.tensor.transpose(bank[0][:, P * c:P * c + P], osb[:, t, P * c:P * c + P], ident)
                    ins.then_inc(s["ot_ps"], 1)

                def project(b):
                    pe.wait_ge(s["ot"], TPB * b + TPB)
                    for t in range(TPB):
                        for c in range(KI):
                            ins = nc.tensor.matmul(bank[0][:, D * t:D * t + D], ot[:, c, P * t:P * t + P], wo1[:, c, :], start=(c == 0), stop=(c == KI - 1))
                    ins.then_inc(s["wo_ps"], 1)

                pe.wait_ge(g["xc"], 1)
                for k in range(KD):
                    ins = nc.tensor.transpose(bank[1][:, B * k:B * k + B], xc2[:, P * k:P * k + P], mat("ident", B)[:, 0:B])
                ins.then_inc(g["xct_ps"], 1)
                turn_rows(0, 0)
                pe.wait_ge(l1_in, 16 * 4)
                pe.wait_ge(s["x2t"], 1)
                pe.wait_ge(s["x2c"], 1)
                pe.wait_ge(s["xcb"], 1)
                for u in range(UNITS):
                    unit(0, 0, u, True)
                    if u == 2:
                        pe.wait_ge(g["xct"], 1)
                        for k in range(KD):
                            ins = nc.tensor.matmul(bank[3][0:B, :], x2ct[:, k, :], wkv1[:, k, INNER:2 * INNER], start=(k == 0), stop=(k == KD - 1))
                        ins.then_inc(g["oc_ps"], 1)
                    if u == 5:
                        pe.wait_ge(g["oc"], 1)
                        for k in range(KI):
                            ins = nc.tensor.transpose(bank[4][:, B * k:B * k + B], oc[:, P * k:P * k + P], mat("ident", B)[:, 0:B])
                        ins.then_inc(g["oct_ps"], 1)
                    if u == 8:
                        pe.wait_ge(g["oct"], 1)
                        for k in range(KI):
                            ins = nc.tensor.matmul(bank[5][0:B, 0:D], oct_[:, k, :], wo1[:, k, :], start=(k == 0), stop=(k == KI - 1))
                        ins.then_inc(g["oo_ps"], 1)
                cls_v(0, 0)

                def image(b, slot, first, last):
                    pe.wait_ge(s["even_out"], HALF * b + KI)
                    pe.wait_ge(s["odd_out"], HALF * b + KI)
                    scores(b, slot, 0, first)
                    scores(b, slot, 1, first)
                    if not last:
                        pe.wait_ge(s["vc"], b + 1)
                        turn_rows(b + 1, 1 - slot)
                    for h in range(H1):
                        if h + 2 < H1:
                            scores(b, slot, h + 2, first)
                        if not last:
                            if h == 0:
                                pe.wait_ge(s["x2t"], b + 2)
                                pe.wait_ge(s["x2c"], b + 2)
                            unit(b + 1, 1 - slot, h, False)
                        if h < TPB and not first:
                            if h > 0 or last:
                                pe.wait_ge(s["ot" if h else "vc"], TPB * b - TPB + 1 if h else b + 1)
                            turn_out(b - 1, h)
                        turn_probs(b, h, first)
                        if h == 0:
                            pe.wait_ge(s["even_out"], HALF * b + HALF)
                            pe.wait_ge(s["odd_out"], HALF * b + HALF)
                            if not first:
                                pe.wait_ge(s["o_add"], TPB * b)
                        else:
                            weighted(b, slot, h - 1)
                        if h == 2 and not first:
                            project(b - 1)
                    if not last:
                        for u in range(H1, UNITS):
                            unit(b + 1, 1 - slot, u, False)
                        if not first:
                            pe.wait_ge(s["h_done"], b)
                        pe.wait_ge(s["xcb"], b + 2)
                        cls_v(b + 1, 1 - slot)
                    weighted(b, slot, H1 - 1)

                per_image(pe, image)
                pe.wait_ge(s["h_done"], B - 1)
                for t in range(TPB):
                    if t:
                        pe.wait_ge(s["ot"], TPB * B - 1)
                    turn_out(B - 1, t)
                project(B - 1)
        scope.close()

        scope = ExitStack()
        NP = B // 2
        TP = 2 * TPB
        w1, w2 = w1e[0], w2e[0]
        b1q = sb("b1q", [P, KF], scope=scope)
        b1r = sb("b1r", [KF, P], scope=scope)
        b2q = sb("b2q", [P, D], scope=scope)
        stat3 = sb("stat3", [P, TP, 6], scope=scope)
        mv3 = sb("mv3", [P, TP, 2], scope=scope)
        var3 = sb("var3", [P, TP], scope=scope)
        rstd3 = sb("rstd3", [P, TP], scope=scope)
        nh3 = sb("nh3", [P, TP], scope=scope)
        xn3 = sb("xn3", [P, TP, D], scope=scope)
        x3t = [sb(f"x3t_{i}", [P, KD, TP * P], scope=scope) for i in range(2)]
        x3ct = sb("x3ct", [P, KD, B], scope=scope)
        statc3 = sb("statc3", [B, 6], scope=scope)
        mvc3 = sb("mvc3", [B, 2], scope=scope)
        varc3 = sb("varc3", [B, 1], scope=scope)
        rstdc3 = sb("rstdc3", [B, 1], scope=scope)
        xc3 = sb("xc3", [B, D], scope=scope)
        W = TP * P
        hq = [sb(f"hq_{i}", [P, W], scope=scope) for i in range(2)]
        knot = [sb(f"knot_{i}", [P, W], scope=scope) for i in range(2)]
        gl = [sb(f"gl_{i}", [P, W], scope=scope) for i in range(2)]
        gr = [sb(f"gr_{i}", [P, W], scope=scope) for i in range(2)]
        frac = [sb(f"frac_{i}", [P, W], scope=scope) for i in range(2)]
        yt = [sb(f"yt_{i}", [P, KF, W], scope=scope) for i in range(2)]
        ytc = sb("ytc", [P, KF, B], scope=scope)
        z = [sb(f"z_{i}", [P, TPB, D], scope=scope) for i in range(2)]
        zc = sb("zc", [B, D], scope=scope)
        shift = sb("shift", [P, 2], scope=scope)
        names = ("w_in b1_ps b1 shift stat aggr var rstd xn x_ps xt h_ps hq knot gl frac rise y0 y1 y z_ps z zr h_out "
                 "statc aggrc varc rstdc xc xc_ps xct hc_ps zc_ps zc").split()
        s = {n: sem("f_" + n) for n in names}
        STEP = 0.25
        N_CHUNK = NP * KF + 1

        def chunk_cols(c):
            return slice(0, W) if c < NP * KF else slice(0, KF * B)

        with nc.Block() as block:
            @block.sync
            def _(sp):
                sp.dma_start(b1r[:, :], dram["L1_ffn_b1"].rearrange("(m p) -> m p", p=P)).then_inc(s["w_in"], 16)
                sp.dma_start(b2q[:, :], dram["L1_ffn_b2"].partition_broadcast(P)).then_inc(s["w_in"], 16)
                for p in range(NP):
                    for i in range(2):
                        sp.wait_ge(s["h_out"], 2 * p + i + 1)
                        b = 2 * p + i
                        sp.dma_start(out[b, 1:POS, :].rearrange("(t p) d -> p t d", p=P), hrow[:, TPB * b:TPB * b + TPB, :]).then_inc(out_stored, 16)
                sp.wait_ge(s["h_out"], B + 1)
                sp.dma_start(out[:, 0, :], hcls[:, :]).then_inc(out_stored, 16)
                sp.wait_ge(out_stored, 16 * (B + 1))

            @block.gpsimd
            def _(pool):
                nc.gpsimd.memset(nh3[:, :], -0.5).then_inc(s["shift"], 1)
                nc.gpsimd.memset(shift[:, 0:1], -ROUND).then_inc(s["shift"], 1)
                nc.gpsimd.memset(shift[:, 1:2], STEP - ROUND).then_inc(s["shift"], 1)
                pool.wait_ge(s["shift"], 3)

                def deviations(p):
                    pool.wait_ge(s["aggr"], TP * p + TP)
                    nc.gpsimd.tensor_scalar(var3[:, :], mv3[:, :, 1], EPS, None, ALU.add).then_inc(s["var"], 1)
                    pool.wait_ge(s["var"], p + 1)
                    nc.gpsimd.tensor_tensor(rstd3[:, :], var3[:, :], nh3[:, :], ALU.pow).then_inc(s["rstd"], 1)

                def chunk(c):
                    i, n = c % 2, chunk_cols(c)
                    pool.wait_ge(s["knot"], c + 1)
                    nc.gpsimd.tensor_tensor(frac[i][:, n], hq[i][:, n], knot[i][:, n], ALU.subtract).then_inc(s["frac"], 1)
                    pool.wait_ge(s["gl"], 2 * c + 2)
                    nc.gpsimd.tensor_tensor(gr[i][:, n], gr[i][:, n], gl[i][:, n], ALU.subtract).then_inc(s["rise"], 1)

                deviations(0)
                pool.wait_ge(s["aggrc"], 1)
                nc.gpsimd.tensor_scalar(varc3[:, :], mvc3[:, 1:2], EPS, None, ALU.add).then_inc(s["varc"], 1)
                pool.wait_ge(s["varc"], 1)
                nc.gpsimd.tensor_tensor(rstdc3[:, :], varc3[:, :], nh3[0:B, 0:1], ALU.pow).then_inc(s["rstdc"], 1)
                deviations(1)
                for p in range(NP):
                    for m in range(KF):
                        chunk(p * KF + m)
                        if m == 1 and p + 2 < NP:
                            deviations(p + 2)
                chunk(NP * KF)

            @block.vector
            def _(dve):
                def statistics(p):
                    for t in range(TP):
                        nc.vector.bn_stats(stat3[:, t, :], hrow[:, TP * p + t, :]).then_inc(s["stat"], 1)
                    for t in range(TP):
                        dve.wait_ge(s["stat"], TP * p + t + 1)
                        nc.vector.bn_aggr(mv3[:, t, :], stat3[:, t, :]).then_inc(s["aggr"], 1)

                def normalise(p):
                    dve.wait_ge(s["rstd"], p + 1)
                    dve.wait_ge(s["aggr"], TP * p + TP)
                    if p:
                        dve.wait_ge(s["x_ps"], p)
                    for t in range(TP):
                        ins = nc.vector.tensor_scalar(xn3[:, t, :], hrow[:, TP * p + t, :], mv3[:, t, 0:1], rstd3[:, t:t + 1], ALU.subtract, ALU.mult)
                    ins.then_inc(s["xn"], 1)

                def knots(c):
                    i, n = c % 2, chunk_cols(c)
                    dve.wait_ge(s["h_ps"], c + 1)
                    if c >= 2:
                        dve.wait_ge(s["frac"], c - 1)
                        dve.wait_ge(s["gl"], 2 * c - 2)
                    if c < NP * KF:
                        nc.vector.tensor_scalar(hq[i][:, n], kvbank[:, i, :], b1q[:, c % KF:c % KF + 1], ROUND, ALU.add, ALU.add).then_inc(s["hq"], 1)
                    else:
                        v = frac[i][:, n].rearrange("p (m b) -> p m b", b=B)
                        dve.wait_ge(s["y0"], c - 1)
                        nc.vector.tensor_tensor(v, bank[2][:, n].rearrange("p (m b) -> p m b", b=B), rep(b1q[:, :], 2, B), ALU.add).then_inc(s["zc"], 1)
                        dve.wait_ge(s["zc"], 1)
                        nc.vector.tensor_scalar(hq[i][:, n], frac[i][:, n], ROUND, None, ALU.add).then_inc(s["hq"], 1)
                    dve.wait_ge(s["hq"], c + 1)
                    nc.vector.tensor_scalar(knot[i][:, n].bitcast(I32), hq[i][:, n].bitcast(I32), -64, None, ALU.bitwise_and).then_inc(s["knot"], 1)

                def interpolate(c):
                    i, n = c % 2, chunk_cols(c)
                    dve.wait_ge(s["frac"], c + 1)
                    dve.wait_ge(s["rise"], c + 1)
                    nc.vector.tensor_tensor(frac[i][:, n], frac[i][:, n], gr[i][:, n], ALU.mult).then_inc(s["y0"], 1)
                    dve.wait_ge(s["y0"], c + 1)
                    nc.vector.scalar_tensor_tensor(gl[i][:, n], frac[i][:, n], 1.0 / STEP, gl[i][:, n], ALU.mult, ALU.add).then_inc(s["y1"], 1)
                    dve.wait_ge(s["y1"], c + 1)
                    if c < NP * KF:
                        p, m = divmod(c, KF)
                        if p >= 2 and m == 0:
                            dve.wait_ge(s["z_ps"], 2 * (p - 1))
                        dst = yt[p % 2][:, m, :]
                        nc.vector.tensor_scalar(dst, gl[i][:, n], ROUND, -ROUND, ALU.add, ALU.add).then_inc(s["y"], 1)
                    else:
                        nc.vector.tensor_scalar(ytc[:, :, :].rearrange("p m b -> p (m b)"), gl[i][:, n], ROUND, -ROUND, ALU.add, ALU.add).then_inc(s["y"], 1)

                def store(p, i):
                    at = TPB * (2 * p + i)
                    n = 2 * p + i
                    dve.wait_ge(s["z_ps"], n + 1)
                    if n >= 2:
                        dve.wait_ge(s["h_out"], n - 1)
                    nc.vector.tensor_tensor(z[i][:, :, :], bank[3 + i][:, :].rearrange("p (t d) -> p t d", t=TPB), rep(b2q[:, :], 1, TPB), ALU.add).then_inc(s["z"], 1)
                    dve.wait_ge(s["z"], n + 1)
                    nc.vector.tensor_scalar(z[i][:, :, :], z[i][:, :, :], ROUND, -ROUND, ALU.add, ALU.add).then_inc(s["zr"], 1)
                    dve.wait_ge(s["zr"], n + 1)
                    nc.vector.tensor_tensor(hrow[:, at:at + TPB, :], hrow[:, at:at + TPB, :], z[i][:, :, :], ALU.add).then_inc(s["h_out"], 1)

                dve.wait_ge(s["w_in"], 32)
                dve.wait_ge(s["b1_ps"], 1)
                nc.vector.tensor_copy(b1q[:, :], bank[5][:, 0:KF]).then_inc(s["b1"], 1)
                statistics(0)
                normalise(0)
                nc.vector.bn_stats(statc3[:, :], hcls[:, :]).then_inc(s["statc"], 1)
                dve.wait_ge(s["statc"], 1)
                nc.vector.bn_aggr(mvc3[:, :], statc3[:, :]).then_inc(s["aggrc"], 1)
                dve.wait_ge(s["rstdc"], 1)
                dve.wait_ge(s["aggrc"], 1)
                nc.vector.tensor_scalar(xc3[:, :], hcls[:, :], mvc3[:, 0:1], rstdc3[:, 0:1], ALU.subtract, ALU.mult).then_inc(s["xc"], 1)
                dve.wait_ge(s["b1"], 1)
                statistics(1)
                normalise(1)
                for c in range(N_CHUNK + 1):
                    if c < N_CHUNK:
                        knots(c)
                    if c:
                        interpolate(c - 1)
                    if c < NP * KF:
                        p, m = divmod(c, KF)
                        if p >= 1 and m == 5:
                            store(p - 1, 0)
                        if p >= 2 and m == 1:
                            store(p - 2, 1)
                        if m == 1 and p + 2 < NP:
                            statistics(p + 2)
                        if m == 4 and p + 2 < NP:
                            normalise(p + 2)
                store(NP - 2, 1)
                for i in range(2):
                    store(NP - 1, i)
                dve.wait_ge(s["zc_ps"], 1)
                nc.vector.tensor_tensor(zc[:, :], bank[5][0:B, 0:D], b2q[0:B, :], ALU.add).then_inc(s["zc"], 1)
                dve.wait_ge(s["zc"], 2)
                nc.vector.tensor_scalar(zc[:, :], zc[:, :], ROUND, -ROUND, ALU.add, ALU.add).then_inc(s["zc"], 1)
                dve.wait_ge(s["zc"], 3)
                nc.vector.tensor_tensor(hcls[:, :], hcls[:, :], zc[:, :], ALU.add).then_inc(s["h_out"], 1)

            @block.scalar
            def _(act):
                def rows_t(p):
                    act.wait_ge(s["x_ps"], p + 1)
                    for k in range(KD):
                        ins = nc.scalar.copy(x3t[p % 2][:, k, :], bank[k][:, :])
                    ins.then_inc(s["xt"], 1)

                rows_t(0)
                act.wait_ge(s["xc_ps"], 1)
                nc.scalar.copy(x3ct[:, :, :], bank[2][:, 0:KD * B].rearrange("p (k b) -> p k b", k=KD)).then_inc(s["xct"], 1)
                act.wait_ge(s["shift"], 3)
                for c in range(N_CHUNK):
                    i, n = c % 2, chunk_cols(c)
                    act.wait_ge(s["knot"], c + 1)
                    if c >= 2:
                        act.wait_ge(s["y"], c - 1)
                    nc.scalar.activation(gl[i][:, n], knot[i][:, n], ACT.Gelu, bias=shift[:, 0:1]).then_inc(s["gl"], 1)
                    nc.scalar.activation(gr[i][:, n], knot[i][:, n], ACT.Gelu, bias=shift[:, 1:2]).then_inc(s["gl"], 1)
                    if c % KF == 0 and c // KF + 1 < NP:
                        rows_t(c // KF + 1)

            @block.tensor
            def _(pe):
                def turn_rows(p):
                    pe.wait_ge(s["xn"], p + 1)
                    if p:
                        pe.wait_ge(s["xt"], p)
                    for k in range(KD):
                        for t in range(TP):
                            ins = nc.tensor.transpose(bank[k][:, P * t:P * t + P], xn3[:, t, P * k:P * k + P], ident)
                    ins.then_inc(s["x_ps"], 1)

                def up(c):
                    p, m = divmod(c, KF)
                    if m == 0:
                        pe.wait_ge(s["xt"], p + 1)
                    if c >= 2:
                        pe.wait_ge(s["hq"], c - 1)
                    for k in range(KD):
                        ins = nc.tensor.matmul(kvbank[:, c % 2, :], w1[:, k, P * m:P * m + P], x3t[p % 2][:, k, :], start=(k == 0), stop=(k == KD - 1))
                    ins.then_inc(s["h_ps"], 1)

                def down(p, t):
                    i = t // TPB
                    n = 2 * p + i
                    if t % TPB == 0 and n >= 2:
                        pe.wait_ge(s["z"], n - 1)
                    if t == 0:
                        pe.wait_ge(s["y"], p * KF + KF)
                    o = bank[3 + i][:, D * (t % TPB):D * (t % TPB) + D]
                    for m in range(KF):
                        ins = nc.tensor.matmul(o, yt[p % 2][:, m, P * t:P * t + P], w2[:, m, :], start=(m == 0), stop=(m == KF - 1))
                    if t % TPB == TPB - 1:
                        ins.then_inc(s["z_ps"], 1)

                pe.wait_ge(s["w_in"], 32)
                nc.tensor.transpose(bank[5][:, 0:KF], b1r[:, :], mat("ident", KF)[:, 0:KF]).then_inc(s["b1_ps"], 1)
                turn_rows(0)
                pe.wait_ge(s["xc"], 1)
                for k in range(KD):
                    ins = nc.tensor.transpose(bank[2][:, B * k:B * k + B], xc3[:, P * k:P * k + P], mat("ident", B)[:, 0:B])
                ins.then_inc(s["xc_ps"], 1)
                pe.wait_ge(w1e_in[0], 16 * 5)
                pe.wait_ge(w2e_in[0], 16 * 5)
                for m in range(KF):
                    up(m)
                    if m == 0:
                        turn_rows(1)
                for p in range(NP):
                    for j in range(KF):
                        if p + 1 < NP:
                            up(KF * (p + 1) + j)
                            if j == 0 and p + 2 < NP:
                                turn_rows(p + 2)
                        if j % 2 == 1:
                            down(p, j // 2)
                    if p == NP - 2:
                        pe.wait_ge(s["xct"], 1)
                        for m in range(KF):
                            for k in range(KD):
                                ins = nc.tensor.matmul(bank[2][:, B * m:B * m + B], w1[:, k, P * m:P * m + P], x3ct[:, k, :], start=(k == 0), stop=(k == KD - 1))
                        ins.then_inc(s["h_ps"], 1)
                pe.wait_ge(s["y"], N_CHUNK)
                for m in range(KF):
                    ins = nc.tensor.matmul(bank[5][0:B, 0:D], ytc[:, m, :], w2[:, m, :], start=(m == 0), stop=(m == KF - 1))
                ins.then_inc(s["zc_ps"], 1)
        scope.close()


_OUT = (B, POS, D)


def kernel(**inputs):
    import numpy as _np
    import concourse.bacc as _bacc
    from concourse import mybir as _mybir
    from concourse.bass_utils import run_bass_kernel_spmd as _run

    nc = _bacc.Bacc("TRN2", target_bir_lowering=False, num_devices=1)
    arrays, dram = {}, {}
    for name, a in [*inputs.items(), *_shape_constants().items()]:
        a = _np.ascontiguousarray(a)
        arrays[f"in_{name}"] = a
        dram[name] = nc.dram_tensor(f"in_{name}", a.shape, _mybir.dt.from_np(a.dtype), kind="ExternalInput").ap()
    out = nc.dram_tensor("out_0", _OUT, _mybir.dt.float32, kind="ExternalOutput").ap()
    vit_tower_kernel(nc, dram, out)
    r = _run(nc, [arrays], core_ids=[0])
    return r.results[0]["out_0"]
```

```python
from contextlib import ExitStack

import numpy as np

import concourse.bass as bass
from concourse import mybir

ALU = mybir.AluOpType
ACT = mybir.ActivationFunctionType
AX = mybir.AxisListType
F32 = mybir.dt.float32
F32R = mybir.dt.float32r
I32 = mybir.dt.int32
U32 = mybir.dt.uint32

P = 128
B = 8
ROWS = 256
D = 256
POS = ROWS + 1
KD = D // P
TPB = ROWS // P
NT = B * TPB
NTC = NT + 1
N_TOK = B * POS
EPS = 1e-5
HD0 = 16
E = 8
F = 1024
KF = F // P
CAP = int(N_TOK / E * 1.25) + 1
MT = 3
MR = -(-CAP // MT)
SLOTS = E * CAP
FAR = 1 << 20
H1 = 8
HD1 = 64
INNER = H1 * HD1
KI = INNER // P
BUCKETS = 32
SCOLS = (1 + P) + POS
MASKED = -1e30
ROUND = 49152.0

MATS = {}


def _columns(spec):
    at = 0
    for name, n in spec:
        MATS[name] = (at, n)
        at += n
    return at


N_MATS = _columns([("ident", P), ("flip", P), ("ones", P), ("tri", P), ("above", P), ("haar2", P), ("unhaar2", P), ("haar3", 64),
                   ("unhaar3", 64), ("blocks", KD * P), ("after", B * B), ("tri8", B), ("order", NTC * E),
                   ("first_slot", NTC * E), ("before", NT * E), ("is_cls", 1), ("neg_half", 2)])


def _shape_constants():
    f = np.float32
    m = np.zeros((P, N_MATS), f)

    def put(name, a):
        at, n = MATS[name]
        m[:a.shape[0], at:at + n] = a.reshape(a.shape[0], n)

    put("ident", np.eye(P))
    put("flip", np.eye(P)[::-1])
    put("ones", np.ones((P, P)))
    put("tri", np.triu(np.ones((P, P))))
    put("above", np.triu(np.ones((P, P)), 1))

    def haar(n):
        a = np.zeros((n, n))
        for i in range(n // 2):
            a[2 * i, i] = a[2 * i + 1, i] = a[2 * i, n // 2 + i] = 1
            a[2 * i + 1, n // 2 + i] = -1
        return a

    put("haar2", haar(P))
    put("unhaar2", 0.25 * haar(P).T)
    put("haar3", haar(64))
    put("unhaar3", 0.25 * haar(64).T)
    heads = np.arange(P) // HD0
    block = (heads[:, None] == heads[None, :]) / np.sqrt(HD0)
    put("blocks", np.concatenate([block] * KD, 1))
    after = np.zeros((P, B, B))
    for j in range(B):
        after[:, j, j + 1:] = 1
    put("after", after)
    put("tri8", np.triu(np.ones((B, B))))
    put("order", np.broadcast_to(np.arange(E, 0, -1), (P, NTC, E)))
    put("first_slot", np.broadcast_to(np.arange(E) * CAP - 1, (P, NTC, E)))
    before = np.zeros((B, NT, E))
    for b in range(B):
        before[b, b * TPB:] = 1
    put("before", before)
    put("is_cls", (np.arange(P) < B).astype(f)[:, None])
    put("neg_half", np.full((P, 2), -0.5))

    freqs = (f(1.0) / np.power(f(10000.0), np.arange(0, HD0, 2, dtype=f))).astype(f)
    angle = (np.arange(POS, dtype=f)[:, None] * freqs[None, :]).astype(f)[1:]
    cos = np.repeat(np.cos(angle), 2, axis=1).astype(f)
    sin = np.stack([-np.sin(angle), np.sin(angle)], -1).reshape(ROWS, HD0).astype(f)
    pairs = np.concatenate([np.arange(r, ROWS, 2) for r in range(2)])
    cos, sin = (np.tile(a[pairs], (1, D // HD0)) for a in (cos, sin))
    rope_t = np.stack([cos.T.reshape(KD, P, ROWS), sin.T.reshape(KD, P, ROWS)])
    rope_q = np.ascontiguousarray(rope_t.transpose(2, 0, 1, 3)).astype(f)
    rope_k = np.stack([cos.reshape(TPB, P, D), sin.reshape(TPB, P, D)])
    rope_k = np.ascontiguousarray(rope_k.transpose(2, 0, 1, 3)).astype(f)

    n = (ROWS - np.arange(2 * ROWS)).astype(np.int64)
    exact = BUCKETS // 2
    big = exact + (np.log(np.maximum(n, 1).astype(f) / exact) / np.log(128 / exact)
                   * (BUCKETS - exact)).astype(np.int32)
    bucket = np.where(n < exact, n, np.minimum(big, BUCKETS - 1))
    hot = np.zeros((BUCKETS + 1, 2 * ROWS), f)
    for v in range(2 * ROWS):
        hot[bucket[v] if n[v] >= 0 else BUCKETS, v] = 1
    far = np.full((1, H1), MASKED, f)
    return {"c_mats": m, "c_rope_q": rope_q, "c_rope_k": rope_k, "c_buckets": hot, "c_masked": far}


def rep(ap, axis, n):
    wide = ap.unsqueeze(axis)
    shape = list(wide.shape)
    shape[axis] = n
    return wide.broadcast_to(shape)


def vit_tower_kernel(nc, dram, out):
    ctx = ExitStack()
    with ctx:
        def sem(name):
            return ctx.enter_context(nc.semaphore(name))

        def sb(name, shape, dt=F32, scope=ctx):
            return scope.enter_context(nc.sbuf_tensor(name, shape, dt))

        early = []

        def early_sem(name):
            early.append(nc.alloc_semaphore(name=name))
            return early[-1]

        bank = [ctx.enter_context(nc.psum_tensor(f"bank{i}", [P, 512], F32)) for i in range(3)]
        kvbank = ctx.enter_context(nc.psum_tensor("kvbank", [P, 2, 512], F32))
        bank += [ctx.enter_context(nc.psum_tensor(f"bank{i}", [P, 512], F32)) for i in range(3, 6)]

        mats = sb("mats", [P, N_MATS])

        def mat(name, parts=P):
            at, n = MATS[name]
            return mats[0:parts, at:at + n]

        ident, ones = mat("ident"), mat("ones")

        hrow = sb("hrow", [P, NT, D])
        hcls = sb("hcls", [B, D])
        w1 = sb("w1", [P, KD, F])
        w2 = sb("w2", [P, KF, D])
        w1h, w1l, w2h, w2l = ([sb(n, [P, KD, F] if n < "w2" else [P, KF, D], F32R)] for n in ("w1h0", "w1l0", "w2h0", "w2l0"))
        wq1 = sb("wq1", [P, KD, INNER])
        wkv1 = sb("wkv1", [P, KD, 2 * INNER])
        wo1 = sb("wo1", [P, KI, D])
        bo1 = sb("bo1", [P, D])
        toeplitz = sb("toeplitz", [P, H1, SCOLS])
        xrow = sb("xrow", [P, NT, D])
        xcls = sb("xcls", [B, D])
        to_slot = sb("to_slot", [P, NTC], U32)
        back_pairs = sb("back_pairs", [P, TPB, 2, B])
        back = sb("back", [P, TPB, 2, B])
        back_cls = sb("back_cls", [B, 2])

        buf = nc.dram_tensor("expert_in", [SLOTS + MT * MR - CAP, D], F32, kind="Internal").ap()
        ybuf = nc.dram_tensor("expert_out", [SLOTS, D], F32, kind="Internal").ap()
        bias_rev = nc.dram_tensor("bias_rev", [H1, 2 * ROWS], F32, kind="Internal").ap()

        mats_in = sem("mats_in")
        w1_in, w2_in = sem("w1_in"), sem("w2_in")
        w1_high, w2_high, w1_low, w2_low = (sem(n) for n in ("w1_high", "w2_high", "w1_low", "w2_low"))
        buf_zeroed = sem("buf_zeroed")
        l0_in = sem("l0_in")
        l1_in = sem("l1_in")
        out_stored = sem("out_stored")
        stored = 0

        def apart(eng):
            eng.wait_ge(mats_in, 16)

        def waits_apart(eng, *waits):
            waits = [(which, value if isinstance(value, int) else eng.to_reg(value)) for which, value in waits]
            if not all(isinstance(value, int) for _, value in waits):
                apart(eng)
            for which, value in waits:
                eng.wait_ge(which, value)

        def high(engine, x, to):
            return (engine.copy if engine is nc.scalar else engine.tensor_copy)(to, x)

        def low_part(engine, x, of, to):
            return engine.tensor_tensor(to, x, of.bitcast(F32), ALU.subtract)

        def product(to, ws, xs, start, stop):
            (wh, wl), (xh, xl) = ws, xs
            nc.tensor.matmul(to, wl, xh, start=start, stop=False)
            nc.tensor.matmul(to, wh, xl, start=False, stop=False)
            return nc.tensor.matmul(to, wh, xh, start=False, stop=stop)

        attn0 = ExitStack()
        wq0 = sb("wq0", [P, KD, D], scope=attn0)
        wqs0 = sb("wqs0", [P, KD, D], scope=attn0)
        wkv0 = sb("wkv0", [P, KD, 2 * D], scope=attn0)
        wo0 = sb("wo0", [P, KD, D], scope=attn0)
        wg = sb("wg", [P, KD, E], scope=attn0)
        ropeq = sb("ropeq", [P, 2, KD, ROWS], scope=attn0)
        ropek = sb("ropek", [P, 2, TPB, D], scope=attn0)
        bqm = sb("bqm", [P, KD], scope=attn0)
        bqs = sb("bqs", [P, KD], scope=attn0)
        bkv = sb("bkv", [P, 2 * D], scope=attn0)
        bo0 = sb("bo0", [P, D], scope=attn0)
        clsb = sb("clsb", [B, D], scope=attn0)
        emb = sb("emb", [BUCKETS + 1, H1], scope=attn0)
        hot = sb("hot", [BUCKETS + 1, 2 * ROWS], scope=attn0)
        bias = {n: early_sem("bias_" + n) for n in "emb_in emb brev_ps brev brev_out rev_in flip_ps flip_out".split()}

        nh16 = sb("nh16", [P, NT], scope=attn0)
        statc = sb("statc", [B, 6], scope=attn0)
        mvc = sb("mvc", [B, 2], scope=attn0)
        varc = sb("varc", [B, 1], scope=attn0)
        rstdc = sb("rstdc", [B, 1], scope=attn0)
        xc0 = sb("xc0", [B, D], scope=attn0)
        xct0 = sb("xct0", [P, KD, B], scope=attn0)
        qc0 = sb("qc0", [P, KD, B], scope=attn0)
        kvc = sb("kvc", [1, 2 * D], scope=attn0)
        c = {n: early_sem("c_" + n) for n in "nh swapped stat aggr var rstd xc0 xct_ps xct qc_ps qc kvc_ps kvc".split()}
        l0_all = 16 * 14

        tok = ExitStack()
        img = xrow[:, :, :].rearrange("p (b r) w -> p b r w", r=2)
        lohi = sb("lohi", [P, B, 2, 2, P], scope=tok)
        a1 = sb("a1", [P, B, P], scope=tok)
        d1 = sb("d1", [P, B, 3, P], scope=tok)
        wd3 = sb("wd3", [P, 3, 3 * P], scope=tok)
        wd2 = sb("wd2", [P, 2, 64 * 3], scope=tok)
        wd1 = sb("wd1", [64, 2, 32 * 3], scope=tok)
        wa = sb("wa", [32, 32], scope=tok)
        tokb = sb("tokb", [P, 10], scope=tok)
        lh2 = sb("lh2", [P, 2, B, 64], scope=tok)
        c2 = sb("c2", [P, 2, B, 64], scope=tok)
        lh3 = sb("lh3", [64, 2, B, 32], scope=tok)
        c3 = sb("c3", [64, 2, B, 32], scope=tok)
        junk = sb("junk", [P, 2, 3, P], scope=tok)
        dots = sb("dots", [P, 80], scope=tok)
        lev = sb("lev", [P, 4, 3 * B * 3], scope=tok)
        red = sb("red", [P, 3, 3 * B], scope=tok)
        asig = sb("asig", [P, 3, B], scope=tok)
        f1 = sb("f1", [P, 2, B, 3], scope=tok)
        f2 = sb("f2", [P, 2, B], scope=tok)
        f3 = sb("f3", [64, 2, B], scope=tok)

        names = ("tok_w_in tok_zero lo_done a1_done d1_done lh2_done c2_ps c2_done lh3_done c3_ps c3_done dots_done "
                 "dots_ps logit_done exp_done w_step w_done scaled c3_scaled c2_scaled un3_ps un3_done a2_done un2_ps un2_done a1_new "
                 "merged").split()
        s = {n: early_sem("t_" + n) for n in names}
        img_in = [early_sem(f"img_in{half}") for half in range(2)]

        def split(engine, half, hi):
            q = slice(B // 2 * half, B // 2 * half + B // 2)
            engine.tensor_tensor(lohi[:, q, hi, :, :], img[:, q, :, 0::2], img[:, q, :, 1::2], ALU.subtract if hi else ALU.add).then_inc(s["lo_done"], 1)

        def merge(engine, half, odd):
            q = slice(B // 2 * half, B // 2 * half + B // 2)
            to = hrow[:, :, :].rearrange("p (b r) d -> p b r d", r=2)[:, q, :, odd::2]
            engine.tensor_tensor(to, lohi[:, q, 0, :, :], lohi[:, q, 1, :, :], ALU.subtract if odd else ALU.add).then_inc(s["merged"], 1)
        with nc.Block() as block:
            @block.sync
            def _(sp):
                for half in range(2):
                    b0, b1 = B // 2 * half, B // 2 * half + B // 2
                    sp.dma_start(img[:, b0:b1, :, :], dram["x"][b0:b1].rearrange("b (p r) w o -> p b r (w o)", r=2)).then_inc(img_in[half], 16)
                    if half == 0:
                        sp.dma_start(mats[:, :], dram["c_mats"]).then_inc(mats_in, 16)
                sp.dma_start(wd3[:, :, :], dram["L0_tok_Wd3"].rearrange("(c i j) k -> i c (j k)", c=3, i=P)).then_inc(s["tok_w_in"], 16)
                v2 = dram["L0_tok_Wd2"].rearrange("(c i j) k -> c i (j k)", c=3, i=64)
                v1 = dram["L0_tok_Wd1"].rearrange("(c i j) k -> c i (j k)", c=3, i=32)
                for w, v, n in ((wd2, v2, 64), (wd1, v1, 32)):
                    sp.dma_start(w[n:2 * n, 0, :], v[0]).then_inc(s["tok_w_in"], 16)
                    sp.dma_start(w[0:n, 1, :], v[1]).then_inc(s["tok_w_in"], 16)
                    sp.dma_start(w[n:2 * n, 1, :], v[2]).then_inc(s["tok_w_in"], 16)
                sp.dma_start(wa[:, :], dram["L0_tok_Wa"].rearrange("(i j) o -> i (j o)", i=32)).then_inc(s["tok_w_in"], 16)
                for i, n in enumerate(("L0_tok_bd3", "L0_tok_bd2", "L0_tok_bd1")):
                    sp.dma_start(tokb[:, 3 * i:3 * i + 3], dram[n].partition_broadcast(P)).then_inc(s["tok_w_in"], 16)
                sp.dma_start(tokb[:, 9:10], dram["L0_tok_ba"].partition_broadcast(P)).then_inc(s["tok_w_in"], 16)
                sp.dma_start(wq0[:, :, :], dram["L0_attn_Wq"].rearrange("(k p) n -> p k n", p=P)).then_inc(l0_in, 16)
                sp.dma_start(wkv0[:, :, 0:D], dram["L0_attn_Wk"].rearrange("(k p) n -> p k n", p=P)).then_inc(l0_in, 16)
                sp.dma_start(wkv0[:, :, D:2 * D], dram["L0_attn_Wv"].rearrange("(k p) n -> p k n", p=P)).then_inc(l0_in, 16)
                sp.dma_start(wo0[:, :, :], dram["L0_attn_Wo"].rearrange("(k p) n -> p k n", p=P)).then_inc(l0_in, 16)
                sp.dma_start(wg[:, :, :], dram["L0_ffn_wg"].rearrange("(k p) n -> p k n", p=P)).then_inc(l0_in, 16)
                sp.dma_start(ropeq[:, :, :, :], dram["c_rope_q"]).then_inc(l0_in, 16)
                sp.dma_start(ropek[:, :, :, :], dram["c_rope_k"]).then_inc(l0_in, 16)
                with nc.allow_non_contiguous_dma(reason="one bias per partition"):
                    sp.dma_start(bqm[:, :], dram["L0_attn_bq"].rearrange("(m p) -> p m", p=P)).then_inc(l0_in, 16)
                    for r in range(2):
                        sp.dma_start(bqs[r:P:2, :], dram["L0_attn_bq"].rearrange("(m q r) -> r q m", m=KD, r=2)[1 - r]).then_inc(l0_in, 16)
                sp.dma_start(bkv[:, 0:D], dram["L0_attn_bk"].partition_broadcast(P)).then_inc(l0_in, 16)
                sp.dma_start(bkv[:, D:2 * D], dram["L0_attn_bv"].partition_broadcast(P)).then_inc(l0_in, 16)
                sp.dma_start(bo0[:, :], dram["L0_attn_bo"].partition_broadcast(P)).then_inc(l0_in, 16)
                sp.dma_start(clsb[:, :], dram["cls_tok"].rearrange("a b d -> (a b d)").partition_broadcast(B)).then_inc(l0_in, 16)
                sp.dma_start(emb[0:BUCKETS, :], dram["L1_attn_rel_emb"]).then_inc(bias["emb_in"], 16)
                sp.dma_start(emb[BUCKETS:BUCKETS + 1, :], dram["c_masked"]).then_inc(bias["emb_in"], 16)
                sp.dma_start(hot[:, :], dram["c_buckets"]).then_inc(bias["emb_in"], 16)

            @block.gpsimd
            def _(pool):
                pool.wait_ge(img_in[1], 16)
                split(nc.gpsimd, 1, 1)
                nc.gpsimd.memset(nh16[:, :], -0.5).then_inc(c["nh"], 1)
                pool.wait_ge(l0_in, l0_all)
                nc.gpsimd.tensor_copy(wqs0[:, :, 0::2], wq0[:, :, 1::2]).then_inc(c["swapped"], 1)
                nc.gpsimd.tensor_copy(wqs0[:, :, 1::2], wq0[:, :, 0::2]).then_inc(c["swapped"], 1)
                pool.wait_ge(c["aggr"], 1)
                pool.wait_ge(c["nh"], 1)
                nc.gpsimd.tensor_scalar(varc[:, :], mvc[:, 1:2], EPS, None, ALU.add).then_inc(c["var"], 1)
                pool.wait_ge(c["var"], 1)
                nc.gpsimd.tensor_tensor(rstdc[:, :], varc[:, :], nh16[0:B, 0:1], ALU.pow).then_inc(c["rstd"], 1)
                pool.wait_ge(s["w_done"], 7)
                nc.gpsimd.tensor_tensor(d1[:, :, 0, :], d1[:, :, 0, :], rep(f1[:, 0, :, 0], 2, P), ALU.mult).then_inc(s["scaled"], 1)
                pool.wait_ge(s["a1_new"], 6)
                merge(nc.gpsimd, 1, 1)

            @block.vector
            def _(dve):
                nc.vector.memset(dots[:, :], 0.0).then_inc(s["tok_zero"], 1)
                nc.vector.memset(wd2[0:64, 0, :], 0.0).then_inc(s["tok_zero"], 1)
                nc.vector.memset(wd1[0:32, 0, :], 0.0).then_inc(s["tok_zero"], 1)
                for half, hi in ((0, 0), (0, 1), (1, 0)):
                    dve.wait_ge(img_in[half], 16)
                    split(nc.vector, half, hi)
                dve.wait_ge(s["lo_done"], 4)
                nc.vector.tensor_tensor(a1[:, :, :], lohi[:, :, 0, 0, :], lohi[:, :, 0, 1, :], ALU.add).then_inc(s["a1_done"], 1)
                nc.vector.tensor_tensor(d1[:, :, 0, :], lohi[:, :, 0, 0, :], lohi[:, :, 0, 1, :], ALU.subtract).then_inc(s["d1_done"], 1)
                nc.vector.tensor_tensor(d1[:, :, 1, :], lohi[:, :, 1, 0, :], lohi[:, :, 1, 1, :], ALU.add).then_inc(s["d1_done"], 1)
                nc.vector.tensor_tensor(d1[:, :, 2, :], lohi[:, :, 1, 0, :], lohi[:, :, 1, 1, :], ALU.subtract).then_inc(s["d1_done"], 1)
                dve.wait_ge(s["a1_done"], 1)
                nc.vector.tensor_tensor(lh2[:, 0, :, :], a1[:, :, 0::2], a1[:, :, 1::2], ALU.add).then_inc(s["lh2_done"], 1)
                nc.vector.tensor_tensor(lh2[:, 1, :, :], a1[:, :, 0::2], a1[:, :, 1::2], ALU.subtract).then_inc(s["lh2_done"], 1)
                dve.wait_ge(s["tok_w_in"], 16 * 12)
                dve.wait_ge(s["tok_zero"], 3)
                dve.wait_ge(s["d1_done"], 3)
                n_dots = 0

                def products():
                    nonlocal n_dots
                    n_dots += 1
                    if n_dots > 2:
                        dve.wait_ge(s["dots_done"], n_dots - 2)
                    return junk[:, n_dots % 2, :, :]

                w3v = wd3[:, :, :].rearrange("p c (j k) -> p c j k", k=3)
                for b in range(B):
                    for k in range(3):
                        nc.vector.tensor_tensor_reduce(products(), d1[:, b, :, :], w3v[:, :, :, k], 1.0, 0.0, ALU.mult,
                                                       ALU.add, dots[:, 3 * b + k:3 * b + k + 1]).then_inc(s["dots_done"], 1)
                dve.wait_ge(s["c2_done"], 2)
                nc.vector.tensor_tensor(lh3[:, 0, :, :], c2[0:64, 0, :, 0::2], c2[0:64, 0, :, 1::2], ALU.add).then_inc(s["lh3_done"], 1)
                nc.vector.tensor_tensor(lh3[:, 1, :, :], c2[0:64, 0, :, 0::2], c2[0:64, 0, :, 1::2], ALU.subtract).then_inc(s["lh3_done"], 1)
                w2v = wd2[:, :, :].rearrange("p c (j k) -> p c j k", k=3)
                for b in range(B):
                    for k in range(3):
                        nc.vector.tensor_tensor_reduce(products()[:, 0:2, 0:64], c2[:, :, b, :], w2v[:, :, :, k], 1.0, 0.0, ALU.mult,
                                                       ALU.add, dots[:, 24 + 3 * b + k:24 + 3 * b + k + 1]).then_inc(s["dots_done"], 1)
                dve.wait_ge(l0_in, l0_all)
                nc.vector.bn_stats(statc[:, :], clsb[:, :]).then_inc(c["stat"], 1)
                dve.wait_ge(c["stat"], 1)
                nc.vector.bn_aggr(mvc[:, :], statc[:, :]).then_inc(c["aggr"], 1)
                dve.wait_ge(s["c3_done"], 1)
                w1v = wd1[:, :, :].rearrange("p c (j k) -> p c j k", k=3)
                for b in range(B):
                    for k in range(3):
                        nc.vector.tensor_tensor_reduce(products()[0:64, 0:2, 0:32], c3[:, :, b, :], w1v[:, :, :, k], 1.0, 0.0, ALU.mult,
                                                       ALU.add, dots[0:64, 48 + 3 * b + k:48 + 3 * b + k + 1]).then_inc(s["dots_done"], 1)
                    nc.vector.tensor_tensor_reduce(products()[0:32, 0, 0:32], c3[0:32, 0, b, :], wa[:, :], 1.0, 0.0, ALU.mult,
                                                   ALU.add, dots[0:32, 72 + b:73 + b]).then_inc(s["dots_done"], 1)
                dve.wait_ge(c["rstd"], 1)
                dve.wait_ge(c["aggr"], 1)
                nc.vector.tensor_scalar(xc0[:, :], clsb[:, :], mvc[:, 0:1], rstdc[:, 0:1], ALU.subtract, ALU.mult).then_inc(c["xc0"], 1)
                dve.wait_ge(s["dots_ps"], 1)
                for i in range(3):
                    nc.vector.scalar_tensor_tensor(lev[:, 0, 24 * i:24 * i + 24].rearrange("p (b k) -> p b k", k=3),
                                                   bank[1][:, 24 * i:24 * i + 24].rearrange("p (b k) -> p b k", k=3),
                                                   0.5 ** (i + 1), rep(tokb[:, 3 * i:3 * i + 3], 1, B), ALU.mult,
                                                   ALU.add).then_inc(s["w_step"], 1)
                nc.vector.tensor_scalar(asig[:, 0, :], bank[1][:, 72:80], 0.125, tokb[:, 9:10], ALU.mult, ALU.add).then_inc(s["w_step"], 1)
                dve.wait_ge(s["w_step"], 4)
                z = lev[:, 0, :].rearrange("p (n k) -> p n k", k=3)
                nc.vector.tensor_reduce(red[:, 0, :], z, AX.X, ALU.max).then_inc(s["w_step"], 1)
                dve.wait_ge(s["w_step"], 5)
                nc.vector.tensor_tensor(lev[:, 1, :].rearrange("p (n k) -> p n k", k=3), z, rep(red[:, 0, :], 2, 3), ALU.subtract).then_inc(s["logit_done"], 1)
                dve.wait_ge(s["exp_done"], 2)
                ez = lev[:, 2, :].rearrange("p (n k) -> p n k", k=3)
                nc.vector.tensor_reduce(red[:, 1, :], ez, AX.X, ALU.add).then_inc(s["w_step"], 1)
                nc.vector.tensor_scalar(asig[:, 2, :], asig[:, 1, :], 1.0, None, ALU.add).then_inc(s["w_step"], 1)
                dve.wait_ge(s["w_step"], 7)
                nc.vector.reciprocal(red[:, 2, :], red[:, 1, :]).then_inc(s["w_step"], 1)
                nc.vector.reciprocal(asig[:, 0, :], asig[:, 2, :]).then_inc(s["w_step"], 1)
                dve.wait_ge(s["w_step"], 9)
                nc.vector.tensor_tensor(lev[:, 3, :].rearrange("p (n k) -> p n k", k=3), ez, rep(red[:, 2, :], 2, 3), ALU.mult).then_inc(s["w_step"], 1)
                dve.wait_ge(s["w_step"], 10)
                wv = lev[:, 3, :].rearrange("p (l b k) -> p l k b", l=3, k=3)
                nc.vector.tensor_copy(f3[0:32, 0, :], asig[0:32, 0, :]).then_inc(s["w_done"], 1)
                nc.vector.tensor_copy(f3[0:32, 1, :], wv[0:32, 2, 1, :]).then_inc(s["w_done"], 1)
                nc.vector.tensor_copy(f3[32:64, :, :], wv[32:64, 2, 0::2, :]).then_inc(s["w_done"], 1)
                nc.vector.memset(f2[0:64, 0, :], 1.0).then_inc(s["w_done"], 1)
                nc.vector.tensor_copy(f2[0:64, 1, :], wv[0:64, 1, 1, :]).then_inc(s["w_done"], 1)
                nc.vector.tensor_copy(f2[64:P, :, :], wv[64:P, 1, 0::2, :]).then_inc(s["w_done"], 1)
                nc.vector.tensor_scalar(f1[:, 0, :, :], lev[:, 3, 0:24].rearrange("p (b k) -> p b k", k=3), 0.25, None, ALU.mult).then_inc(s["w_done"], 1)
                dve.wait_ge(s["w_done"], 7)
                nc.vector.tensor_tensor(c3[:, :, :, :], c3[:, :, :, :], rep(f3[:, :, :], 3, 32), ALU.mult).then_inc(s["c3_scaled"], 1)
                for k in range(1, 3):
                    nc.vector.tensor_tensor(d1[:, :, k, :], d1[:, :, k, :], rep(f1[:, 0, :, k], 2, P), ALU.mult).then_inc(s["scaled"], 1)
                dve.wait_ge(s["un3_done"], 1)
                u3 = lh3
                nc.vector.tensor_tensor(c2[0:64, 0, :, 0::2], u3[:, 0, :, :], u3[:, 1, :, :], ALU.add).then_inc(s["a2_done"], 1)
                nc.vector.tensor_tensor(c2[0:64, 0, :, 1::2], u3[:, 0, :, :], u3[:, 1, :, :], ALU.subtract).then_inc(s["a2_done"], 1)
                dve.wait_ge(s["a2_done"], 2)
                nc.vector.tensor_tensor(c2[:, :, :, :], c2[:, :, :, :], rep(f2[:, :, :], 3, 64), ALU.mult).then_inc(s["c2_scaled"], 1)
                dve.wait_ge(s["scaled"], 3)
                dve.wait_ge(c["qc_ps"], 1)
                for m in range(KD):
                    nc.vector.tensor_scalar(qc0[:, m, :], bank[4][:, B * m:B * m + B], bqm[:, m:m + 1], None, ALU.add).then_inc(c["qc"], 1)
                dve.wait_ge(c["kvc_ps"], 1)
                nc.vector.tensor_tensor(kvc[:, :], bank[5][0:1, :], bkv[0:1, :], ALU.add).then_inc(c["kvc"], 1)
                nc.vector.tensor_tensor(lohi[:, :, 1, 0, :], d1[:, :, 1, :], d1[:, :, 2, :], ALU.add).then_inc(s["a1_new"], 1)
                nc.vector.tensor_tensor(lohi[:, :, 1, 1, :], d1[:, :, 1, :], d1[:, :, 2, :], ALU.subtract).then_inc(s["a1_new"], 1)
                dve.wait_ge(s["un2_done"], 2)
                nc.vector.tensor_tensor(a1[:, :, 0::2], lh2[:, 0, :, :], lh2[:, 1, :, :], ALU.add).then_inc(s["a1_new"], 1)
                nc.vector.tensor_tensor(a1[:, :, 1::2], lh2[:, 0, :, :], lh2[:, 1, :, :], ALU.subtract).then_inc(s["a1_new"], 1)
                dve.wait_ge(s["a1_new"], 4)
                nc.vector.tensor_tensor(lohi[:, :, 0, 0, :], a1[:, :, :], d1[:, :, 0, :], ALU.add).then_inc(s["a1_new"], 1)
                nc.vector.tensor_tensor(lohi[:, :, 0, 1, :], a1[:, :, :], d1[:, :, 0, :], ALU.subtract).then_inc(s["a1_new"], 1)
                dve.wait_ge(s["a1_new"], 6)
                for half, hi in ((0, 0), (0, 1), (1, 0)):
                    merge(nc.vector, half, hi)

            @block.tensor
            def _(pe):
                pe.wait_ge(mats_in, 16)
                for g in range(2):
                    pe.wait_ge(s["lh2_done"], g + 1)
                    nc.tensor.matmul(kvbank[:, g, :], mat("haar2"), lh2[:, g, :, :], start=True, stop=True).then_inc(s["c2_ps"], 1)
                pe.wait_ge(s["lh3_done"], 2)
                nc.tensor.matmul(bank[0][0:64, :], mat("haar3", 64), lh3[:, :, :, :], start=True, stop=True).then_inc(s["c3_ps"], 1)
                pe.wait_ge(s["dots_done"], 24 + 24 + 32)
                nc.tensor.matmul(bank[1][:, 0:80], ones, dots[:, :], start=True, stop=True).then_inc(s["dots_ps"], 1)
                pe.wait_ge(l0_in, l0_all)
                pe.wait_ge(c["xc0"], 1)
                for k in range(KD):
                    ins = nc.tensor.transpose(bank[3][:, B * k:B * k + B], xc0[:, P * k:P * k + P], mat("ident", B)[:, 0:B])
                ins.then_inc(c["xct_ps"], 1)
                pe.wait_ge(c["xct"], 1)
                for m in range(KD):
                    for k in range(KD):
                        ins = nc.tensor.matmul(bank[4][:, B * m:B * m + B], wq0[:, k, P * m:P * m + P], xct0[:, k, :], start=(k == 0), stop=(k == KD - 1))
                ins.then_inc(c["qc_ps"], 1)
                for k in range(KD):
                    ins = nc.tensor.matmul(bank[5][0:1, :], xct0[:, k, 0:1], wkv0[:, k, :], start=(k == 0), stop=(k == KD - 1))
                ins.then_inc(c["kvc_ps"], 1)
                pe.wait_ge(s["c3_scaled"], 1)
                nc.tensor.matmul(bank[0][0:64, :], mat("unhaar3", 64), c3[:, :, :, :], start=True, stop=True).then_inc(s["un3_ps"], 1)
                pe.wait_ge(s["c2_scaled"], 1)
                for g in range(2):
                    nc.tensor.matmul(kvbank[:, g, :], mat("unhaar2"), c2[:, g, :, :], start=True, stop=True).then_inc(s["un2_ps"], 1)

            @block.scalar
            def _(act):
                for g in range(2):
                    act.wait_ge(s["c2_ps"], g + 1)
                    nc.scalar.copy(c2[:, g, :, :], kvbank[:, g, :].rearrange("p (b j) -> p b j", b=B)).then_inc(s["c2_done"], 1)
                act.wait_ge(s["c3_ps"], 1)
                nc.scalar.copy(c3[:, :, :, :].rearrange("p c b j -> p (c b j)"), bank[0][0:64, :]).then_inc(s["c3_done"], 1)
                act.wait_ge(s["logit_done"], 1)
                nc.scalar.activation(lev[:, 2, :], lev[:, 1, :], ACT.Exp).then_inc(s["exp_done"], 1)
                nc.scalar.activation(asig[:, 1, :], asig[:, 0, :], ACT.Exp, scale=-1.0).then_inc(s["exp_done"], 1)
                act.wait_ge(c["xct_ps"], 1)
                nc.scalar.copy(xct0[:, :, :], bank[3][:, 0:KD * B].rearrange("p (k b) -> p k b", k=KD)).then_inc(c["xct"], 1)
                act.wait_ge(s["un3_ps"], 1)
                nc.scalar.copy(lh3[:, :, :, :].rearrange("p c b j -> p (c b j)"), bank[0][0:64, :]).then_inc(s["un3_done"], 1)
                for g in range(2):
                    act.wait_ge(s["un2_ps"], g + 1)
                    nc.scalar.mul(lh2[:, g, :, :].rearrange("p b j -> p (b j)"), kvbank[:, g, :], 0.25).then_inc(s["un2_done"], 1)
        tok.close()
        brev = sb("brev", [H1, 2 * ROWS], scope=attn0)
        scope = ExitStack()
        stat0 = sb("stat0", [P, NT, 6], scope=scope)
        mv0 = sb("mv0", [P, NT, 2], scope=scope)
        var0 = sb("var0", [P, NT], scope=scope)
        rstd0 = sb("rstd0", [P, NT], scope=scope)
        xn0 = [sb(f"xn0_{i}", [P, TPB, D], scope=scope) for i in range(2)]
        xt0 = [sb(f"xt0_{i}", [P, KD, ROWS], scope=scope) for i in range(2)]
        t1 = sb("t1", [P, KD, ROWS], scope=scope)
        t2 = sb("t2", [P, KD, ROWS], scope=scope)
        qt0 = [sb(f"qt0_{i}", [P, KD, ROWS], scope=scope) for i in range(2)]
        kvb = [sb(f"kvb_{i}", [P, TPB, 2 * D], scope=scope) for i in range(2)]
        kt1 = sb("kt1", [P, TPB, D], scope=scope)
        kt2 = sb("kt2", [P, TPB, D], scope=scope)
        kr = sb("kr", [P, TPB, D], scope=scope)
        vtkm = sb("vtkm", [P, KD, P], scope=scope)
        gs = sb("gs", [P, KD, D], scope=scope)
        xn1 = [sb(f"xn1_{i}", [P, TPB, D], scope=scope) for i in range(2)]
        zrow = sb("zrow", [P, 2, D], scope=scope)
        x1t = sb("x1t", [P, KD, ROWS], scope=scope)
        stat1 = sb("stat1", [P, TPB, 6], scope=scope)
        mv1 = sb("mv1", [P, TPB, 2], scope=scope)
        var1 = sb("var1", [P, TPB], scope=scope)
        rstd1 = sb("rstd1", [P, TPB], scope=scope)
        clsrow = sb("clsrow", [1, B, D], scope=scope)
        clsatt = sb("clsatt", [B, D], scope=scope)
        logits = sb("logits", [P, NTC, E], scope=scope)

        names = ("stat0 aggr0 var0 rstd0 swapped xc0 xct_ps xct qc_ps qc kvc_ps kvc xn_ready xt_ps xt_ready q_ps q_used "
                 "kv_ps kvb_ready kt1 kt2 qr_ready kr_ready vtk_ps vtk_ready g_ps g_ready out_ps hb_done h_done cls_copied "
                 "stat1 aggr1 var1 rstd1 xn1_ready x1t_ps x1t_ready lg_ps lg_done nh xrow_done cls_ps").split()
        s = {n: early_sem("a_" + n) for n in names}

        def per_image(eng, body):
            body(0, 0, True, False)
            with eng.Fori(0, B // 2 - 1) as pair:
                body(pair * 2 + 1, 1, False, False)
                body(pair * 2 + 2, 0, False, False)
            body(B - 1, (B - 1) % 2, False, True)

        def tiles(b):
            return bass.ds(b * TPB, TPB)

        with nc.Block() as block:
            @block.sync
            def _(sp):
                sp.dma_start(w1[:, :, :], dram["L0_ffn_W1"][0].rearrange("(k p) f -> p k f", p=P)).then_inc(w1_in, 16)
                sp.dma_start(w2[:, :, :], dram["L0_ffn_W2"][0].rearrange("(k p) d -> p k d", p=P)).then_inc(w2_in, 16)
                for src, dst in (("L1_attn_Wq", wq1), ("L1_attn_Wkv", wkv1), ("L1_attn_Wo", wo1)):
                    sp.dma_start(dst[:, :, :], dram[src].rearrange("(k p) n -> p k n", p=P)).then_inc(l1_in, 16)
                sp.dma_start(bo1[:, :], dram["L1_attn_bo"].partition_broadcast(P)).then_inc(l1_in, 16)
                sp.wait_ge(bias["brev"], 1)
                sp.dma_start(bias_rev, brev[:, :]).then_inc(bias["brev_out"], 16)
                sp.wait_ge(bias["brev_out"], 16)
                for t in range(TPB):
                    n, at = 1 + P * (t + 1), (1 + P) * t
                    rows = bass.AP(tensor=bias_rev.tensor, offset=ROWS - P * t - P, ap=[[1, P], [2 * ROWS, H1], [1, n]])
                    sp.dma_start(toeplitz[:, :, at:at + n], rows).then_inc(bias["rev_in"], 16)
                sp.wait_ge(s["nh"], 1)
                for c in range(0, buf.shape[0], 256):
                    n = min(256, buf.shape[0] - c)
                    sp.dma_start(buf[c:c + n, :], zrow[0:n // 2, :, :]).then_inc(buf_zeroed, 16)
                sp.wait_ge(buf_zeroed, 16 * -(-buf.shape[0] // 256))

            @block.gpsimd
            def _(pool):
                nc.gpsimd.memset(zrow[:, :, :], 0.0).then_inc(s["nh"], 1)
                nc.gpsimd.memset(logits[:, :, :], 0.0).then_inc(s["nh"], 1)

                def deviations0(n, t0, t1):
                    pool.wait_ge(s["aggr0"], t1)
                    nc.gpsimd.tensor_scalar(var0[:, t0:t1], mv0[:, t0:t1, 1], EPS, None, ALU.add).then_inc(s["var0"], 1)
                    pool.wait_ge(s["var0"], n)
                    nc.gpsimd.tensor_tensor(rstd0[:, t0:t1], var0[:, t0:t1], nh16[:, t0:t1], ALU.pow).then_inc(s["rstd0"], 1)

                deviations0(1, 0, TPB)
                deviations0(2, TPB, NT // 2)

                def turn_qk(b, slot, first):
                    pool.wait_ge(s["q_used"], b + 1)
                    if not first:
                        pool.wait_ge(s["out_ps"], b)
                    nc.gpsimd.tensor_tensor(qt0[slot][:, :, :], t1[:, :, :], t2[:, :, :], ALU.add).then_inc(s["qr_ready"], 1)
                    pool.wait_ge(s["kvb_ready"], b + 1)
                    if not first:
                        pool.wait_ge(s["kr_ready"], b)
                    nc.gpsimd.tensor_tensor(kt1[:, :, :], kvb[slot][:, :, 0:D], ropek[:, 0, :, :], ALU.mult).then_inc(s["kt1"], 1)
                    pool.wait_ge(s["kt1"], b + 1)
                    pool.wait_ge(s["kt2"], 2 * b + 2)
                    if not first:
                        pool.wait_ge(s["vtk_ps"], b + 1)
                    nc.gpsimd.tensor_tensor(kr[:, :, :], kt1[:, :, :], kt2[:, :, :], ALU.add).then_inc(s["kr_ready"], 1)

                def deviations(b):
                    waits_apart(pool, (s["aggr1"], 2 * b + 2))
                    nc.gpsimd.tensor_scalar(var1[:, :], mv1[:, :, 1], EPS, None, ALU.add).then_inc(s["var1"], 1)
                    pool.wait_ge(s["var1"], b + 1)
                    nc.gpsimd.tensor_tensor(rstd1[:, :], var1[:, :], nh16[:, 0:TPB], ALU.pow).then_inc(s["rstd1"], 1)

                def keep_rows(b, slot):
                    pool.wait_ge(s["xn1_ready"], b + 1)
                    nc.gpsimd.tensor_copy(xrow[:, tiles(b), :], xn1[slot][:, :, :]).then_inc(s["xrow_done"], 1)

                turn_qk(0, 0, True)
                deviations0(3, NT // 2, NT)

                def image(b, slot, first, last):
                    if not first:
                        deviations(b - 1)
                    pool.wait_ge(s["xn_ready"], b + 1)
                    nc.gpsimd.tensor_tensor(hrow[:, tiles(b), :], hrow[:, tiles(b), :], rep(bo0[:, :], 1, TPB), ALU.add).then_inc(s["hb_done"], 1)
                    if not last:
                        turn_qk(b + 1, 1 - slot, False)
                    if not first:
                        keep_rows(b - 1, 1 - slot)

                pool.sem_inc(s["xrow_done"], 1)
                per_image(pool, image)
                deviations(B - 1)
                keep_rows(B - 1, (B - 1) % 2)

            @block.vector
            def _(dve):
                dve.wait_ge(bias["emb_in"], 16 * 3)
                nc.vector.tensor_scalar(emb[0:BUCKETS, :], emb[0:BUCKETS, :], 64.0, None, ALU.mult).then_inc(bias["emb"], 1)

                def statistics(t0, t1):
                    for t in range(t0, t1):
                        nc.vector.bn_stats(stat0[:, t, :], hrow[:, t, :]).then_inc(s["stat0"], 1)
                    for t in range(t0, t1):
                        dve.wait_ge(s["stat0"], t + 1)
                        nc.vector.bn_aggr(mv0[:, t, :], stat0[:, t, :]).then_inc(s["aggr0"], 1)

                statistics(0, TPB)
                dve.wait_ge(bias["brev_ps"], 1)
                nc.vector.tensor_copy(brev[:, :], bank[1][0:H1, :]).then_inc(bias["brev"], 1)

                def norm0(b, slot):
                    for t in range(TPB):
                        at = bass.ds(b * TPB + t, 1)
                        ins = nc.vector.tensor_scalar(xn0[slot][:, t, :], hrow[:, at, :].rearrange("p o d -> p (o d)"),
                                                      mv0[:, at, 0:1].rearrange("p o d -> p (o d)"), rstd0[:, at], ALU.subtract, ALU.mult)
                    ins.then_inc(s["xn_ready"], 1)

                dve.wait_ge(s["rstd0"], 1)
                dve.wait_ge(s["aggr0"], TPB)
                norm0(0, 0)
                statistics(TPB, NT // 2)

                def rotate(b, slot, first):
                    dve.wait_ge(s["q_ps"], b + 1)
                    if not first:
                        dve.wait_ge(s["qr_ready"], b)
                    for m in range(KD):
                        cols = slice(ROWS * m, ROWS * m + ROWS)
                        nc.vector.scalar_tensor_tensor(t1[:, m, :], bank[1][:, cols], bqm[:, m:m + 1], ropeq[:, 0, m, :], ALU.add, ALU.mult)
                        ins = nc.vector.scalar_tensor_tensor(t2[:, m, :], bank[2][:, cols], bqs[:, m:m + 1], ropeq[:, 1, m, :], ALU.add, ALU.mult)
                    ins.then_inc(s["q_used"], 1)
                    dve.wait_ge(s["kv_ps"], b + 1)
                    if not first:
                        dve.wait_ge(s["vtk_ps"], b)
                        dve.wait_ge(s["kr_ready"], b)
                    nc.vector.tensor_tensor(kvb[slot][:, :, :], kvbank[:, :, :], rep(bkv[:, :], 1, TPB), ALU.add).then_inc(s["kvb_ready"], 1)
                    dve.wait_ge(s["kvb_ready"], b + 1)
                    nc.vector.tensor_tensor(kt2[:, :, 0::2], kvb[slot][:, :, 1:D:2], ropek[:, 1, :, 0::2], ALU.mult).then_inc(s["kt2"], 1)
                    nc.vector.tensor_tensor(kt2[:, :, 1::2], kvb[slot][:, :, 0:D:2], ropek[:, 1, :, 1::2], ALU.mult).then_inc(s["kt2"], 1)

                def residual(b, slot):
                    dve.wait_ge(s["out_ps"], b + 2)
                    dve.wait_ge(s["hb_done"], b + 1)
                    nc.vector.tensor_tensor(hrow[:, tiles(b), :], bank[5][:, :].rearrange("p (t d) -> p t d", t=TPB),
                                            hrow[:, tiles(b), :], ALU.add).then_inc(s["h_done"], 1)
                    waits_apart(dve, (s["h_done"], b + 1))
                    for t in range(TPB):
                        ins = nc.vector.bn_stats(stat1[:, t, :], hrow[:, bass.ds(b * TPB + t, 1), :].rearrange("p o d -> p (o d)"))
                    ins.then_inc(s["stat1"], 1)
                    waits_apart(dve, (s["stat1"], b + 1))
                    for t in range(TPB):
                        nc.vector.bn_aggr(mv1[:, t, :], stat1[:, t, :]).then_inc(s["aggr1"], 1)
                    dve.wait_ge(s["rstd1"], b + 1)
                    dve.wait_ge(s["x1t_ps"], b + 1)
                    dve.wait_ge(s["xrow_done"], b + 1)
                    dve.wait_ge(s["aggr1"], 2 * b + 2)
                    for t in range(TPB):
                        at = bass.ds(b * TPB + t, 1)
                        ins = nc.vector.tensor_scalar(xn1[slot][:, t, :], hrow[:, at, :].rearrange("p o d -> p (o d)"),
                                                      mv1[:, t, 0:1], rstd1[:, t:t + 1], ALU.subtract, ALU.mult)
                    ins.then_inc(s["xn1_ready"], 1)

                rotate(0, 0, True)
                statistics(NT // 2, NT)
                dve.wait_ge(s["rstd0"], 3)
                dve.wait_ge(s["aggr0"], NT)

                def image(b, slot, first, last):
                    if not last:
                        if not first:
                            dve.wait_ge(s["xt_ps"], b)
                        norm0(b + 1, 1 - slot)
                    dve.wait_ge(s["vtk_ps"], b + 2)
                    if not first:
                        dve.wait_ge(s["g_ps"], b)
                    nc.vector.tensor_tensor(vtkm[:, :, :], bank[3][:, 0:D].rearrange("p (g n) -> p g n", g=KD),
                                            mat("blocks").rearrange("p (g n) -> p g n", g=KD), ALU.mult).then_inc(s["vtk_ready"], 1)
                    if not first:
                        residual(b - 1, 1 - slot)
                    if not last:
                        rotate(b + 1, 1 - slot, False)

                per_image(dve, image)
                residual(B - 1, (B - 1) % 2)

            @block.scalar
            def _(act):
                def evac_xt(b, slot, early):
                    act.wait_ge(s["xt_ps"], b + 1)
                    if not early:
                        act.wait_ge(s["kv_ps"], b - 1)
                    nc.scalar.copy(xt0[slot][:, :, :], bank[0][:, :].rearrange("p (k n) -> p k n", k=KD)).then_inc(s["xt_ready"], 1)

                def evac_expert_rows(b):
                    act.wait_ge(s["x1t_ps"], b + 2)
                    nc.scalar.copy(x1t[:, :, :], bank[0][:, :].rearrange("p (k n) -> p k n", k=KD)).then_inc(s["x1t_ready"], 1)
                    act.wait_ge(s["lg_ps"], b + 1)
                    nc.scalar.copy(logits[:, tiles(b), :], bank[0][:, 0:TPB * E].rearrange("p (t e) -> p t e", t=TPB)).then_inc(s["lg_done"], 1)

                evac_xt(0, 0, True)
                act.wait_ge(s["nh"], 2)

                def image(b, slot, first, last):
                    if not last:
                        evac_xt(b + 1, 1 - slot, first)
                    act.wait_ge(s["g_ps"], b + 1)
                    if not first:
                        act.wait_ge(s["out_ps"], b + 1)
                    nc.scalar.copy(gs[:, :, :], bank[4][:, :].rearrange("p (g n) -> p g n", g=KD)).then_inc(s["g_ready"], 1)
                    if not first:
                        evac_expert_rows(b - 1)
                    act.wait_ge(s["cls_ps"], b + 1)
                    nc.scalar.copy(clsrow[0:1, bass.ds(b, 1), :].rearrange("p o d -> p (o d)"), bank[3][0:1, D:2 * D]).then_inc(s["cls_copied"], 1)

                per_image(act, image)
                evac_expert_rows(B - 1)

            @block.tensor
            def _(pe):
                pe.sem_inc(s["out_ps"], 1)
                pe.sem_inc(s["vtk_ps"], 1)
                pe.sem_inc(s["x1t_ps"], 1)
                pe.sem_inc(s["lg_done"], 1)
                pe.wait_ge(mats_in, 16)
                pe.wait_ge(l0_in, l0_all)
                pe.wait_ge(bias["emb"], 1)
                nc.tensor.matmul(bank[1][0:H1, :], emb[:, :], hot[:, :], start=True, stop=True).then_inc(bias["brev_ps"], 1)

                def turn(src, done):
                    for k in range(KD):
                        for t in range(TPB):
                            ins = nc.tensor.transpose(bank[0][:, ROWS * k + P * t:ROWS * k + P * t + P], src(t)[:, P * k:P * k + P], ident)
                    ins.then_inc(done, 1)

                def expert_rows_t(b, slot):
                    pe.wait_ge(s["xn1_ready"], b + 1)
                    for k in range(KD):
                        for t in range(TPB):
                            ins = nc.tensor.transpose(bank[0][:, ROWS * k + P * t:ROWS * k + P * t + P], xn1[slot][:, t, P * k:P * k + P], ident)
                    ins.then_inc(s["x1t_ps"], 1)

                def logits_of(b):
                    pe.wait_ge(s["x1t_ready"], b + 1)
                    for t in range(TPB):
                        for k in range(KD):
                            ins = nc.tensor.matmul(bank[0][:, E * t:E * t + E], x1t[:, k, P * t:P * t + P], wg[:, k, :], start=(k == 0), stop=(k == KD - 1))
                    ins.then_inc(s["lg_ps"], 1)

                pe.wait_ge(s["xn_ready"], 1)
                turn(lambda t: xn0[0][:, t, :], s["xt_ps"])
                pe.wait_ge(bias["brev"], 1)

                def project_q(b, slot):
                    pe.wait_ge(s["xt_ready"], b + 1)
                    for w, o in ((wq0, bank[1]), (wqs0, bank[2])):
                        for m in range(KD):
                            for k in range(KD):
                                ins = nc.tensor.matmul(o[:, ROWS * m:ROWS * m + ROWS], w[:, k, P * m:P * m + P], xt0[slot][:, k, :],
                                                       start=(k == 0), stop=(k == KD - 1))
                    ins.then_inc(s["q_ps"], 1)

                def project_kv(b, slot):
                    for t in range(TPB):
                        for k in range(KD):
                            ins = nc.tensor.matmul(kvbank[:, t, :], xt0[slot][:, k, P * t:P * t + P], wkv0[:, k, :], start=(k == 0), stop=(k == KD - 1))
                    ins.then_inc(s["kv_ps"], 1)

                project_q(0, 0)
                project_kv(0, 0)

                def image(b, slot, first, last):
                    pe.wait_ge(s["kr_ready"], b + 1)
                    if not first:
                        pe.wait_ge(s["vtk_ready"], b)
                        pe.wait_ge(s["cls_copied"], b)
                    for g in range(KD):
                        for t in range(TPB):
                            nc.tensor.matmul(bank[3][:, P * g:P * g + P], kvb[slot][:, t, D + P * g:D + P * g + P], kr[:, t, P * g:P * g + P],
                                             start=(t == 0), stop=False)
                        ins = nc.tensor.matmul(bank[3][:, P * g:P * g + P], kvc[0:1, D + P * g:D + P * g + P], kvc[0:1, P * g:P * g + P],
                                               start=False, stop=True)
                    ins.then_inc(s["vtk_ps"], 1)
                    if not first:
                        pe.wait_ge(s["lg_done"], b)
                    if not last:
                        pe.wait_ge(s["xn_ready"], b + 2)
                        turn(lambda t: xn0[1 - slot][:, t, :], s["xt_ps"])
                    pe.wait_ge(s["vtk_ready"], b + 1)
                    if not first:
                        pe.wait_ge(s["g_ready"], b)
                    for g in range(KD):
                        ins = nc.tensor.matmul(bank[4][:, D * g:D * g + D], vtkm[:, g, :], wo0[:, g, :], start=True, stop=True)
                    ins.then_inc(s["g_ps"], 1)
                    if not last:
                        pe.wait_ge(s["q_used"], b + 1)
                        project_q(b + 1, 1 - slot)
                    if not first:
                        expert_rows_t(b - 1, 1 - slot)
                    if not last:
                        pe.wait_ge(s["kvb_ready"], b + 1)
                        project_kv(b + 1, 1 - slot)
                    if not first:
                        logits_of(b - 1)
                    pe.wait_ge(s["g_ready"], b + 1)
                    pe.wait_ge(s["qr_ready"], b + 1)
                    if not first:
                        pe.wait_ge(s["h_done"], b)
                    for g in range(KD):
                        ins = nc.tensor.matmul(bank[3][0:1, D:2 * D], qc0[:, g, 0:1], gs[:, g, :], start=(g == 0), stop=(g == KD - 1))
                    ins.then_inc(s["cls_ps"], 1)
                    for t in range(TPB):
                        for g in range(KD):
                            ins = nc.tensor.matmul(bank[5][:, D * t:D * t + D], qt0[slot][:, g, P * t:P * t + P], gs[:, g, :],
                                                   start=(g == 0), stop=(g == KD - 1))
                    ins.then_inc(s["out_ps"], 1)

                per_image(pe, image)
                pe.wait_ge(s["lg_done"], B)
                expert_rows_t(B - 1, (B - 1) % 2)
                logits_of(B - 1)

        names = ("cls_in hcb hcls stat aggr var rstd xcls xct_ps xct lg_ps lg mx cw_d cw_e best_d oh_w best oh cls_m rank_ps "
                 "rk_zero rk step idx scattered").split()
        s = {n: early_sem("r_" + n) for n in names}
        hcb = sb("hcb", [B, D], scope=scope)
        x1ct = sb("x1ct", [P, KD, B], scope=scope)
        route = sb("route", [P, 6, NTC], scope=scope)
        oh = sb("oh", [P, NTC, E], scope=scope)
        wt = sb("wt", [P, NTC, E], scope=scope)
        wt2 = sb("wt2", [P, NTC, E], scope=scope)
        rk = sb("rk", [P, NTC, E], scope=scope)
        ohcm = sb("ohcm", [B, NT, E], scope=scope)
        with nc.Block() as block:
            @block.sync
            def _(sp):
                for b in range(B):
                    sp.dma_start(clsatt[b:b + 1, :], clsrow[0:1, b, :]).then_inc(s["cls_in"], 16)
                sp.wait_ge(s["cls_in"], 16 * B)

            @block.gpsimd
            def _(pool):
                nc.gpsimd.tensor_tensor(hcb[:, :], clsb[:, :], bo0[0:B, :], ALU.add).then_inc(s["hcb"], 1)
                pool.wait_ge(s["aggr"], 1)
                nc.gpsimd.tensor_scalar(varc[:, :], mvc[:, 1:2], EPS, None, ALU.add).then_inc(s["var"], 1)
                pool.wait_ge(s["var"], 1)
                nc.gpsimd.tensor_tensor(rstdc[:, :], varc[:, :], nh16[0:B, 0:1], ALU.pow).then_inc(s["rstd"], 1)
                pool.wait_ge(s["idx"], 1)
                for t in range(NT):
                    nc.gpsimd.indirect_dma_start(buf[0:SLOTS, :], bass.IndirectOffsetOnAxis(to_slot[:, t:t + 1], 0), xrow[:, t, :], None,
                                                 bounds_check=SLOTS - 1, oob_is_err=False).then_inc(s["scattered"], 16)
                nc.gpsimd.indirect_dma_start(buf[0:SLOTS, :], bass.IndirectOffsetOnAxis(to_slot[0:B, NT:NTC], 0), xcls[:, :], None,
                                             bounds_check=SLOTS - 1, oob_is_err=False).then_inc(s["scattered"], 16)
                pool.wait_ge(s["scattered"], 16 * NTC)

            @block.vector
            def _(dve):
                dve.wait_ge(s["cls_in"], 16 * B)
                dve.wait_ge(s["hcb"], 1)
                nc.vector.tensor_tensor(hcls[:, :], clsatt[:, :], hcb[:, :], ALU.add).then_inc(s["hcls"], 1)
                dve.wait_ge(s["hcls"], 1)
                nc.vector.bn_stats(statc[:, :], hcls[:, :]).then_inc(s["stat"], 1)
                dve.wait_ge(s["stat"], 1)
                nc.vector.bn_aggr(mvc[:, :], statc[:, :]).then_inc(s["aggr"], 1)
                nc.vector.memset(rk[:, :, :], 0.0).then_inc(s["rk_zero"], 1)
                dve.wait_ge(s["rstd"], 1)
                dve.wait_ge(s["aggr"], 1)
                nc.vector.tensor_scalar(xcls[:, :], hcls[:, :], mvc[:, 0:1], rstdc[:, 0:1], ALU.subtract, ALU.mult).then_inc(s["xcls"], 1)
                dve.wait_ge(s["lg"], 1)
                lg = logits[:, :, :]
                mx, total, prob, rank, slot, valid = (route[:, i, :] for i in range(6))
                nc.vector.tensor_reduce(mx, lg, AX.X, ALU.max).then_inc(s["mx"], 1)
                dve.wait_ge(s["mx"], 1)
                nc.vector.tensor_tensor(wt[:, :, :], lg, rep(mx, 2, E), ALU.subtract).then_inc(s["cw_d"], 1)
                nc.vector.tensor_tensor(oh[:, :, :], lg, rep(mx, 2, E), ALU.is_equal).then_inc(s["best_d"], 1)
                dve.wait_ge(s["best_d"], 1)
                nc.vector.tensor_tensor(wt2[:, :, :], oh[:, :, :], mat("order").rearrange("p (t e) -> p t e", e=E), ALU.mult).then_inc(s["oh_w"], 1)
                dve.wait_ge(s["oh_w"], 1)
                nc.vector.tensor_reduce(rank, wt2[:, :, :], AX.X, ALU.max).then_inc(s["best"], 1)
                dve.wait_ge(s["best"], 1)
                nc.vector.tensor_tensor(oh[:, :, :], wt2[:, :, :], rep(rank, 2, E), ALU.is_equal).then_inc(s["oh"], 1)
                dve.wait_ge(s["oh"], 1)
                nc.vector.tensor_tensor(ohcm[:, :, :], rep(oh[0:B, NT, :], 1, NT), mat("before", B).rearrange("p (t e) -> p t e", e=E), ALU.mult).then_inc(s["cls_m"], 1)
                dve.wait_ge(s["cw_e"], 1)
                nc.vector.tensor_reduce(total, wt[:, :, :], AX.X, ALU.add).then_inc(s["step"], 1)
                dve.wait_ge(s["step"], 1)
                nc.vector.reciprocal(prob, total).then_inc(s["step"], 1)
                dve.wait_ge(s["rank_ps"], 2)
                dve.wait_ge(s["rk_zero"], 1)
                nc.vector.tensor_copy(rk[:, 0:NT, :], bank[2][:, 0:NT * E].rearrange("p (t e) -> p t e", e=E)).then_inc(s["rk"], 1)
                nc.vector.tensor_copy(rk[0:B, NT, :], bank[3][0:B, 0:E]).then_inc(s["rk"], 1)
                dve.wait_ge(s["rk"], 2)
                nc.vector.tensor_tensor(wt2[:, :, :], rk[:, :, :], oh[:, :, :], ALU.mult).then_inc(s["step"], 1)
                nc.vector.tensor_tensor(rk[:, :, :], rk[:, :, :], mat("first_slot").rearrange("p (t e) -> p t e", e=E), ALU.add).then_inc(s["step"], 1)
                dve.wait_ge(s["step"], 4)
                nc.vector.tensor_reduce(rank, wt2[:, :, :], AX.X, ALU.add).then_inc(s["step"], 1)
                nc.vector.tensor_tensor(rk[:, :, :], rk[:, :, :], oh[:, :, :], ALU.mult).then_inc(s["step"], 1)
                dve.wait_ge(s["step"], 6)
                nc.vector.tensor_reduce(slot, rk[:, :, :], AX.X, ALU.add).then_inc(s["step"], 1)
                nc.vector.tensor_scalar(valid, rank, float(CAP), None, ALU.is_le).then_inc(s["step"], 1)
                dve.wait_ge(s["step"], 8)
                nc.vector.tensor_scalar(mx, valid, -float(FAR), float(FAR), ALU.mult, ALU.add).then_inc(s["step"], 1)
                dve.wait_ge(s["step"], 9)
                nc.vector.tensor_tensor(total, mx, slot, ALU.add).then_inc(s["step"], 1)
                dve.wait_ge(s["step"], 10)
                nc.vector.tensor_scalar(to_slot[:, :], total, 0.0, None, ALU.max).then_inc(s["idx"], 1)
                by_tile = lambda a: a[:, 0:NT].rearrange("p (b r) -> p r b", r=TPB)
                nc.vector.tensor_scalar(back_pairs[:, :, 0, :].bitcast(U32), by_tile(slot), float(SLOTS - 1), 0.0, ALU.min, ALU.max).then_inc(s["idx"], 1)
                nc.vector.tensor_tensor(back_pairs[:, :, 1, :], by_tile(prob), by_tile(valid), ALU.mult).then_inc(s["idx"], 1)
                nc.vector.tensor_scalar(back_cls[:, 0:1].bitcast(U32), slot[0:B, NT:NTC], float(SLOTS - 1), 0.0, ALU.min, ALU.max).then_inc(s["idx"], 1)
                nc.vector.tensor_tensor(back_cls[:, 1:2], prob[0:B, NT:NTC], valid[0:B, NT:NTC], ALU.mult).then_inc(s["idx"], 1)
                dve.wait_ge(w1_high, 1)
                low_part(nc.vector, w1[:, :, :], w1h[0][:, :, :], w1l[0][:, :, :]).then_inc(w1_low, 1)
                dve.wait_ge(w2_high, 1)
                low_part(nc.vector, w2[:, :, :], w2h[0][:, :, :], w2l[0][:, :, :]).then_inc(w2_low, 1)

            @block.scalar
            def _(act):
                for h in range(H1):
                    act.wait_ge(bias["flip_ps"], h + 1)
                    nc.scalar.copy(toeplitz[:, h, :], bank[4 + h % 2][:, 0:SCOLS]).then_inc(bias["flip_out"], 1)
                act.wait_ge(s["xct_ps"], 1)
                nc.scalar.copy(x1ct[:, :, :], bank[0][:, 0:KD * B].rearrange("p (k b) -> p k b", k=KD)).then_inc(s["xct"], 1)
                act.wait_ge(s["lg_ps"], 1)
                nc.scalar.copy(logits[0:B, NT, :], bank[1][0:B, 0:E]).then_inc(s["lg"], 1)
                act.wait_ge(s["cw_d"], 1)
                nc.scalar.activation(wt[:, :, :], wt[:, :, :], ACT.Exp).then_inc(s["cw_e"], 1)
                act.wait_ge(w1_in, 16)
                high(nc.scalar, w1[:, :, :], w1h[0][:, :, :]).then_inc(w1_high, 1)
                act.wait_ge(w2_in, 16)
                high(nc.scalar, w2[:, :, :], w2h[0][:, :, :]).then_inc(w2_high, 1)

            @block.tensor
            def _(pe):
                pe.wait_ge(bias["rev_in"], 16 * TPB)
                for h in range(H1):
                    if h >= 2:
                        pe.wait_ge(bias["flip_out"], h - 1)
                    nc.tensor.matmul(bank[4 + h % 2][:, 0:SCOLS], mat("flip"), toeplitz[:, h, :], start=True, stop=True).then_inc(bias["flip_ps"], 1)
                pe.wait_ge(s["xcls"], 1)
                for k in range(KD):
                    ins = nc.tensor.transpose(bank[0][:, B * k:B * k + B], xcls[:, P * k:P * k + P], mat("ident", B)[:, 0:B])
                ins.then_inc(s["xct_ps"], 1)
                pe.wait_ge(s["xct"], 1)
                for k in range(KD):
                    ins = nc.tensor.matmul(bank[1][0:B, 0:E], x1ct[:, k, :], wg[:, k, :], start=(k == 0), stop=(k == KD - 1))
                ins.then_inc(s["lg_ps"], 1)
                pe.wait_ge(s["cls_m"], 1)
                ranks = bank[2][:, 0:NT * E]
                nc.tensor.matmul(ranks, mat("tri"), oh[:, 0:NT, :], start=True, stop=False)
                of_pair = ranks.rearrange("p (b r e) -> p b r e", r=2, e=E)
                nc.tensor.matmul(of_pair[:, :, 1, :], mat("tri"), oh[:, 0:NT:2, :], start=False, stop=False)
                nc.tensor.matmul(of_pair[:, :, 0, :], mat("above"), oh[:, 1:NT:2, :], start=False, stop=False)
                for t in range(NT - TPB):
                    done = t // TPB * TPB + TPB
                    nc.tensor.matmul(bank[2][:, E * done:E * NT], ones, rep(oh[:, t, :], 1, NT - done), start=False, stop=False)
                nc.tensor.matmul(ranks, mat("ones", B), ohcm[:, :, :], start=False, stop=True).then_inc(s["rank_ps"], 1)
                nc.tensor.matmul(bank[3][0:B, 0:E], mat("tri8", B), oh[0:B, NT, :], start=True, stop=False)
                after = mat("after").rearrange("p (j b) -> p j b", b=B)
                for t in range(NT):
                    ins = nc.tensor.matmul(bank[3][0:B, 0:E], after[:, t // TPB, :], oh[:, t, :], start=False, stop=(t == NT - 1))
                ins.then_inc(s["rank_ps"], 1)
        scope.close()
        attn0.close()
        nc.clear_and_free_semaphores(early)
        nc.all_engine_barrier()
        hpairs, hrow = hrow, xrow
        yrow = hpairs
        in_order = sem("in_order")
        scope = ExitStack()
        b1rows = sb("b1rows", [E * KF, P], scope=scope)
        b1t = sb("b1t", [P, E * KF], scope=scope)
        b2b = sb("b2b", [P, E, D], scope=scope)
        xe = [sb(f"xe_{i}", [MR, MT, D], scope=scope) for i in range(2)]
        w1h.append(sb("w1h1", [P, KD, F], F32R, scope=scope))
        w1l.append(sb("w1l1", [P, KD, F], F32R, scope=scope))
        w2h.append(sb("w2h1", [P, KF, D], F32R, scope=scope))
        w2l.append(sb("w2l1", [P, KF, D], F32R, scope=scope))
        xeh = sb("xeh", [P, KD, MT * MR], F32R, scope=scope)
        xel = sb("xel", [P, KD, MT * MR], F32R, scope=scope)
        RING = 4
        hraw = sb("hraw", [P, RING, MT * MR], scope=scope)
        hth = sb("hth", [P, KF, MT * MR], F32R, scope=scope)
        htl = sb("htl", [P, KF, MT * MR], F32R, scope=scope)
        ys = [sb(f"ys_{i}", [MR, MT, D], scope=scope) for i in range(2)]
        names = "b_in b1_ps b1t xet_ps xeh xel h_ps gelu hth htl y_ps y_ready".split()
        s = {n: sem("e_" + n) for n in names}
        xe_in = [sem(f"xe_in{i}") for i in range(2)]
        y_out = [sem(f"y_out{i}") for i in range(2)]
        last_rows = CAP - (MT - 1) * MR

        def per_expert(eng, body):
            body(0, 0, 1, True, False)
            with eng.Fori(0, E // 2 - 1) as pair:
                body(pair * 2 + 1, 1, pair + 1, False, False)
                body(pair * 2 + 2, 0, pair + 2, False, False)
            body(E - 1, (E - 1) % 2, E // 2, False, True)

        with nc.Block() as block:
            @block.sync
            def _(sp):
                def load_rows(e, slot):
                    sp.dma_start(xe[slot][:, :, :], buf[bass.ds(e * CAP, MT * MR), :].rearrange("(t p) d -> p t d", p=MR)).then_inc(xe_in[slot], 16)

                load_rows(0, 0)
                sp.dma_start(b1rows[:, :], dram["L0_ffn_b1"].rearrange("e (m p) -> (e m) p", p=P)).then_inc(s["b_in"], 16)
                sp.dma_start(b2b[:, :, :], dram["L0_ffn_b2"].partition_broadcast(P)).then_inc(s["b_in"], 16)

                def rows_in_order():
                    with nc.allow_non_contiguous_dma(reason="a row is a kilobyte"):
                        for t in range(TPB):
                            for r in range(2):
                                some = slice(P // 2 * t, P // 2 * t + P // 2)
                                sp.dma_start(hrow[r:P:2, t:NT:TPB, :], hpairs[some, r:NT:TPB, :]).then_inc(in_order, 16)
                                sp.dma_start(back[r:P:2, t, :, :], back_pairs[some, r, :, :]).then_inc(in_order, 16)

                def expert(e, slot, use, first, last):
                    if not last:
                        if not first:
                            sp.wait_ge(s["xet_ps"], e)
                        load_rows(e + 1, 1 - slot)
                        for n, w, w_in, w_low in (("L0_ffn_W1", w1, w1_in, w1_low), ("L0_ffn_W2", w2, w2_in, w2_low)):
                            sp.wait_ge(w_low, e + 1)
                            row = dram[n][bass.ds(e + 1, 1)].rearrange("o (k p) n -> p (o k) n", p=P)
                            sp.dma_start(w[:, :, :], row).then_inc(w_in, 16)
                    if first:
                        rows_in_order()
                    if last:
                        sp.wait_ge(w1_low, E)
                        sp.dma_start(w1[:, :, :], dram["L1_ffn_w1"].rearrange("(k p) f -> p k f", p=P)).then_inc(w1_in, 16)
                        sp.wait_ge(w2_low, E)
                        sp.dma_start(w2[:, :, :], dram["L1_ffn_w2"].rearrange("(k p) d -> p k d", p=P)).then_inc(w2_in, 16)
                    sp.wait_ge(s["y_ready"], 2 * e + 2)
                    whole = (MT - 1) * MR
                    sp.dma_start(ybuf[bass.ds(e * CAP, whole), :].rearrange("(t p) d -> p t d", p=MR), ys[slot][:, 0:MT - 1, :]).then_inc(y_out[slot], 16)
                    sp.dma_start(ybuf[bass.ds(e * CAP + whole, last_rows), :], ys[slot][0:last_rows, MT - 1, :]).then_inc(y_out[slot], 16)

                per_expert(sp, expert)
                for slot in range(2):
                    sp.wait_ge(y_out[slot], 32 * (E // 2 + 1))
                sp.wait_ge(in_order, 16 * 4 * TPB)

            @block.gpsimd
            def _(pool):
                def expert(e, slot, use, first, last):
                    if not last:
                        for w, wh, wl, w_high, w_low in ((w1, w1h, w1l, w1_high, w1_low), (w2, w2h, w2l, w2_high, w2_low)):
                            pool.wait_ge(w_high, e + 2)
                            low_part(nc.gpsimd, w[:, :, :], wh[1 - slot][:, :, :], wl[1 - slot][:, :, :]).then_inc(w_low, 1)

                per_expert(pool, expert)

            @block.vector
            def _(dve):
                for slot in range(2):
                    dve.sem_inc(y_out[slot], 32)
                dve.wait_ge(s["b1_ps"], 1)
                nc.vector.tensor_copy(b1t[:, :], bank[5][:, 0:E * KF]).then_inc(s["b1t"], 1)
                dve.wait_ge(s["b_in"], 32)

                def rows_low(e):
                    dve.wait_ge(s["xeh"], e + 1)
                    for k in range(KD):
                        ins = low_part(nc.vector, bank[k][:, 0:MT * MR], xeh[:, k, :], xel[:, k, :])
                    ins.then_inc(s["xel"], 1)

                rows_low(0)

                def expert(e, slot, use, first, last):
                    for m in range(KF + 1):
                        if m < KF:
                            dve.wait_ge(s["gelu"], e * KF + m + 1)
                            high(nc.vector, hraw[:, m % RING, :], hth[:, m, :]).then_inc(s["hth"], 1)
                        if m:
                            dve.wait_ge(s["hth"], e * KF + m)
                            low_part(nc.vector, hraw[:, (m - 1) % RING, :], hth[:, m - 1, :], htl[:, m - 1, :]).then_inc(s["htl"], 1)
                    if not last:
                        rows_low(e + 1)
                    dve.wait_ge(s["y_ps"], e + 1)
                    dve.wait_ge(y_out[slot], use * 32)
                    bias = b2b[0:MR, bass.ds(e, 1), :]
                    nc.vector.tensor_tensor(ys[slot][:, 0:2, :], bank[3][0:MR, :].rearrange("p (t d) -> p t d", t=2),
                                            rep(bias.rearrange("p o d -> p (o d)"), 1, 2), ALU.add).then_inc(s["y_ready"], 1)
                    nc.vector.tensor_tensor(ys[slot][:, 2, :], bank[4][0:MR, 0:D], bias.rearrange("p o d -> p (o d)"), ALU.add).then_inc(s["y_ready"], 1)

                per_expert(dve, expert)

            @block.scalar
            def _(act):
                def rows_high(e):
                    act.wait_ge(s["xet_ps"], e + 1)
                    for k in range(KD):
                        ins = high(nc.scalar, bank[k][:, 0:MT * MR], xeh[:, k, :])
                    ins.then_inc(s["xeh"], 1)

                rows_high(0)
                act.wait_ge(s["b1t"], 1)

                def expert(e, slot, use, first, last):
                    for m in range(KF):
                        act.wait_ge(s["h_ps"], e * KF + m + 1)
                        if not (first and m < RING):
                            act.wait_ge(s["htl"], e * KF + m + 1 - RING)
                        nc.scalar.activation(hraw[:, m % RING, :], kvbank[:, m % 2, 0:MT * MR], ACT.Gelu, bias=b1t[:, bass.ds(e * KF + m, 1)]).then_inc(s["gelu"], 1)
                    if not last:
                        rows_high(e + 1)
                        for w, wh, w_in, w_high in ((w1, w1h, w1_in, w1_high), (w2, w2h, w2_in, w2_high)):
                            act.wait_ge(w_in, 16 * e + 32)
                            high(nc.scalar, w[:, :, :], wh[1 - slot][:, :, :]).then_inc(w_high, 1)

                per_expert(act, expert)

            @block.tensor
            def _(pe):
                def turn_rows(e, slot, use):
                    pe.wait_ge(xe_in[slot], use * 16)
                    for k in range(KD):
                        for t in range(MT):
                            ins = nc.tensor.transpose(bank[k][:, MR * t:MR * t + MR], xe[slot][:, t, P * k:P * k + P], mat("ident", MR)[:, 0:MR])
                    ins.then_inc(s["xet_ps"], 1)

                pe.wait_ge(s["b_in"], 32)
                nc.tensor.transpose(bank[5][:, 0:E * KF], b1rows[:, :], mat("ident", E * KF)[:, 0:E * KF]).then_inc(s["b1_ps"], 1)
                turn_rows(0, 0, 1)

                def expert(e, slot, use, first, last):
                    pe.wait_ge(w1_low, e + 1)
                    pe.wait_ge(s["xel"], e + 1)
                    for m in range(KF):
                        if not (first and m < 2):
                            pe.wait_ge(s["gelu"], e * KF + m - 1)
                        for k in range(KD):
                            cols = slice(P * m, P * m + P)
                            ins = product(kvbank[:, m % 2, 0:MT * MR], (w1h[slot][:, k, cols], w1l[slot][:, k, cols]), (xeh[:, k, :], xel[:, k, :]),
                                          k == 0, k == KD - 1)
                        ins.then_inc(s["h_ps"], 1)
                    if not last:
                        turn_rows(e + 1, 1 - slot, use + slot)
                    pe.wait_ge(w2_low, e + 1)
                    if not first:
                        pe.wait_ge(s["y_ready"], 2 * e)
                    for t in range(MT):
                        o = bank[3][0:MR, D * t:D * t + D] if t < 2 else bank[4][0:MR, 0:D]
                        rows = slice(MR * t, MR * t + MR)
                        for m in range(KF):
                            if t == 0:
                                pe.wait_ge(s["htl"], e * KF + m + 1)
                            ins = product(o, (hth[:, m, rows], htl[:, m, rows]), (w2h[slot][:, m, :], w2l[slot][:, m, :]), m == 0, m == KF - 1)
                    ins.then_inc(s["y_ps"], 1)

                per_expert(pe, expert)
        scope.close()

        x2ct = sb("x2ct", [P, KD, B])
        gath = [sem(f"gathered{t}") for t in range(NTC)]
        scope = ExitStack()
        stat2 = sb("stat2", [P, NTC, 6], scope=scope)
        mv2 = sb("mv2", [P, NT, 2], scope=scope)
        var2 = sb("var2", [P, NT], scope=scope)
        rstd2 = sb("rstd2", [P, NT], scope=scope)
        nh2 = sb("nh2", [P, NT], scope=scope)
        mvc2 = sb("mvc2", [B, 2], scope=scope)
        varc2 = sb("varc2", [B, 1], scope=scope)
        rstdc2 = sb("rstdc2", [B, 1], scope=scope)
        xc2 = sb("xc2", [B, D], scope=scope)
        oc = sb("oc", [B, INNER], scope=scope)
        oct_ = sb("oct", [P, KI, B], scope=scope)
        hcb2 = sb("hcb2", [B, D], scope=scope)
        g = {n: sem("g_" + n) for n in "h2 h2c stat statc aggr aggrc var rstd nh xc xct_ps xct oc_ps oc oct_ps oct oo_ps hcb hcls".split()}
        xn2 = [sb(f"xn2_{i}", [P, TPB, D], scope=scope) for i in range(2)]
        x2t = [sb(f"x2t_{i}", [P, KD, POS], scope=scope) for i in range(2)]
        qk = [sb(f"qk_{i}", [P, 2 * KI, POS], scope=scope) for i in range(2)]
        vrow = [sb(f"vrow_{i}", [P, TPB, INNER], scope=scope) for i in range(2)]
        vcls = [sb(f"vcls_{i}", [P, INNER], scope=scope) for i in range(2)]
        sx = [sb(f"sx_{i}", [P, SCOLS], scope=scope) for i in range(2)]
        low = sb("low", [P, 2, TPB], scope=scope)
        prob = sb("prob", [P, H1, SCOLS], scope=scope)
        total = [sb(f"total_{i}", [P, TPB, H1], scope=scope) for i in range(2)]
        inv = sb("inv", [P, TPB, H1], scope=scope)
        pt = [sb(f"pt_{i}", [P, 3 * P], scope=scope) for i in range(2)]
        osb = sb("osb", [P, TPB, INNER], scope=scope)
        ot = sb("ot", [P, KI, ROWS], scope=scope)
        xcb = [sb(f"xcb_{i}", [P, KD, P], scope=scope) for i in range(2)]
        names = ("xn2 x2t_ps x2t x2c xcb qk_ps even_out odd_out vc_ps vc s_ps smax p_done pt_ps pt pv inv o_tmp o_add o_fin "
                 "ot_ps ot wo_ps hb h_done").split()
        s = {n: sem("b_" + n) for n in names}
        UNITS = 2 * KI + TPB
        HALF = UNITS // 2
        tile_at = (0, 1 + P)

        with nc.Block() as block:
            @block.gpsimd
            def _(pool):
                def fetch(t):
                    b, half = divmod(t, TPB)
                    at = back[:, half, 0, b:b + 1].bitcast(U32)
                    nc.gpsimd.indirect_dma_start(yrow[:, t, :], None, ybuf[:, :], bass.IndirectOffsetOnAxis(at, 0)).then_inc(gath[t], 16)

                nc.gpsimd.indirect_dma_start(xcls[:, :], None, ybuf[:, :], bass.IndirectOffsetOnAxis(back_cls[:, 0:1].bitcast(U32), 0)).then_inc(gath[NT], 16)
                for t in range(2 * TPB):
                    fetch(t)
                nc.gpsimd.memset(nh2[:, :], -0.5).then_inc(g["nh"], 1)
                pool.wait_ge(g["nh"], 1)
                pool.wait_ge(g["aggrc"], 1)
                nc.gpsimd.tensor_scalar(varc2[:, :], mvc2[:, 1:2], EPS, None, ALU.add).then_inc(g["var"], 1)
                pool.wait_ge(g["var"], 1)
                nc.gpsimd.tensor_tensor(rstdc2[:, :], varc2[:, :], nh2[0:B, 0:1], ALU.pow).then_inc(g["rstd"], 1)

                def deviations(n, t0, t1):
                    pool.wait_ge(g["aggr"], t1)
                    nc.gpsimd.tensor_scalar(var2[:, t0:t1], mv2[:, t0:t1, 1], EPS, None, ALU.add).then_inc(g["var"], 1)
                    pool.wait_ge(g["var"], n)
                    nc.gpsimd.tensor_tensor(rstd2[:, t0:t1], var2[:, t0:t1], nh2[:, t0:t1], ALU.pow).then_inc(g["rstd"], 1)

                deviations(2, 0, TPB)
                for t in range(2 * TPB, NT):
                    fetch(t)
                nc.gpsimd.tensor_tensor(hcb2[:, :], hcls[:, :], bo1[0:B, :], ALU.add).then_inc(g["hcb"], 1)
                deviations(3, TPB, NT)

                def cls_column(b, slot):
                    nc.gpsimd.tensor_copy(x2t[slot][:, :, 0:1], x2ct[:, :, bass.ds(b, 1)]).then_inc(s["x2c"], 1)
                    nc.gpsimd.tensor_copy(xcb[slot][:, :, :], x2ct[:, :, bass.ds(b, 1)].broadcast_to([P, KD, P])).then_inc(s["xcb"], 1)

                def image(b, slot, first, last):
                    if not last:
                        if not first:
                            pool.wait_ge(s["vc_ps"], b)
                        cls_column(b + 1, 1 - slot)
                    pool.wait_ge(s["xn2"], b + 1)
                    nc.gpsimd.tensor_tensor(hrow[:, tiles(b), :], hrow[:, tiles(b), :], rep(bo1[:, :], 1, TPB), ALU.add).then_inc(s["hb"], 1)
                    pool.wait_ge(s["p_done"], H1 * b + H1)
                    pool.wait_ge(s["vc"], b + 1)
                    if not first:
                        pool.wait_ge(s["ot_ps"], TPB * b)
                    for t in range(TPB):
                        nc.gpsimd.tensor_tensor(osb[:, t, :].rearrange("p (h d) -> p h d", h=H1), vcls[slot][:, :].rearrange("p (h d) -> p h d", h=H1),
                                                rep(prob[:, :, tile_at[t]], 2, HD1), ALU.mult).then_inc(s["o_tmp"], 1)
                    pool.wait_ge(s["inv"], b + 1)
                    for t in range(TPB):
                        pool.wait_ge(s["o_add"], TPB * b + t + 1)
                        o = osb[:, t, :].rearrange("p (h d) -> p h d", h=H1)
                        nc.gpsimd.tensor_tensor(o, o, rep(inv[:, t, :], 2, HD1), ALU.mult).then_inc(s["o_fin"], 1)

                per_image(pool, image)

            @block.vector
            def _(dve):
                def norm2(b, slot):
                    for t in range(TPB):
                        at = bass.ds(b * TPB + t, 1)
                        ins = nc.vector.tensor_scalar(xn2[slot][:, t, :], hrow[:, at, :].rearrange("p o d -> p (o d)"),
                                                      mv2[:, at, 0:1].rearrange("p o d -> p (o d)"), rstd2[:, at], ALU.subtract, ALU.mult)
                    ins.then_inc(s["xn2"], 1)

                def even_unit(b, slot, u):
                    dve.wait_ge(s["qk_ps"], UNITS * b + u + 1)
                    if u < 2 * KI:
                        nc.vector.tensor_copy(qk[slot][:, u, :], kvbank[:, 0, 0:POS]).then_inc(s["even_out"], 1)
                    else:
                        nc.vector.tensor_copy(vrow[slot][:, u - 2 * KI, :], kvbank[:, 0, :]).then_inc(s["even_out"], 1)

                def scores(b, h, first):
                    used = [] if first and h < 2 else [(s["p_done"], H1 * b + h - 1)]
                    waits_apart(dve, (s["s_ps"], H1 * b + h + 1), *used)
                    for t in range(TPB):
                        at, n = tile_at[t], 1 + P * (t + 1)
                        ins = nc.vector.tensor_tensor_reduce(sx[h % 2][:, at:at + n], bank[1 + h % 2][:, at:at + n], toeplitz[:, h, at:at + n],
                                                             -0.125, 3e38, ALU.add, ALU.min, low[:, h % 2, t:t + 1])
                    ins.then_inc(s["smax"], 1)

                def take(t):
                    dve.wait_ge(gath[t], 16)
                    nc.vector.scalar_tensor_tensor(hrow[:, t, :], yrow[:, t, :], back[:, t % TPB, 1, t // TPB:t // TPB + 1], hrow[:, t, :], ALU.mult, ALU.add).then_inc(g["h2"], 1)
                    dve.wait_ge(g["h2"], t + 1)
                    nc.vector.bn_stats(stat2[:, t, :], hrow[:, t, :]).then_inc(g["stat"], 1)
                    dve.wait_ge(g["stat"], t + 1)
                    nc.vector.bn_aggr(mv2[:, t, :], stat2[:, t, :]).then_inc(g["aggr"], 1)

                dve.wait_ge(gath[NT], 16)
                nc.vector.scalar_tensor_tensor(hcls[:, :], xcls[:, :], back_cls[:, 1:2], hcls[:, :], ALU.mult, ALU.add).then_inc(g["h2c"], 1)
                dve.wait_ge(g["h2c"], 1)
                nc.vector.bn_stats(stat2[0:B, NT, :], hcls[:, :]).then_inc(g["statc"], 1)
                dve.wait_ge(g["statc"], 1)
                nc.vector.bn_aggr(mvc2[:, :], stat2[0:B, NT, :]).then_inc(g["aggrc"], 1)
                for t in range(TPB):
                    take(t)
                dve.wait_ge(g["rstd"], 1)
                dve.wait_ge(g["aggrc"], 1)
                nc.vector.tensor_scalar(xc2[:, :], hcls[:, :], mvc2[:, 0:1], rstdc2[:, 0:1], ALU.subtract, ALU.mult).then_inc(g["xc"], 1)
                dve.wait_ge(g["rstd"], 2)
                dve.wait_ge(g["aggr"], TPB)
                norm2(0, 0)
                t = TPB
                for u in range(0, UNITS, 2):
                    for _ in range(3):
                        if t < NT:
                            take(t)
                            t += 1
                    even_unit(0, 0, u)
                dve.wait_ge(g["oo_ps"], 1)
                dve.wait_ge(g["hcb"], 1)
                dve.wait_ge(g["xc"], 1)
                nc.vector.tensor_tensor(hcls[:, :], bank[5][0:B, 0:D], hcb2[:, :], ALU.add).then_inc(g["hcls"], 1)
                dve.wait_ge(g["rstd"], 3)
                dve.wait_ge(g["aggr"], NT)

                def image(b, slot, first, last):
                    if not last:
                        if not first:
                            dve.wait_ge(s["x2t_ps"], b)
                        norm2(b + 1, 1 - slot)
                    scores(b, 0, first)
                    scores(b, 1, first)
                    for h in range(H1):
                        if h + 2 < H1:
                            scores(b, h + 2, first)
                        if h % 2 == 0 and not last:
                            even_unit(b + 1, 1 - slot, h)
                        dve.wait_ge(s["pt_ps"], H1 * b + h + 1)
                        if not (first and h < 2):
                            dve.wait_ge(s["pv"], H1 * b + h - 1)
                        nc.vector.tensor_copy(pt[h % 2][:, :], bank[3][:, 0:3 * P]).then_inc(s["pt"], 1)
                        if h == 3 and not first:
                            dve.wait_ge(s["wo_ps"], b)
                            dve.wait_ge(s["hb"], b)
                            nc.vector.tensor_tensor(hrow[:, tiles(b - 1), :], bank[0][:, :].rearrange("p (t d) -> p t d", t=TPB),
                                                    hrow[:, tiles(b - 1), :], ALU.add).then_inc(s["h_done"], 1)
                    if not last:
                        even_unit(b + 1, 1 - slot, H1)
                    dve.wait_ge(s["p_done"], H1 * b + H1)
                    if not first:
                        dve.wait_ge(s["o_fin"], TPB * b)
                    nc.vector.reciprocal(inv[:, :, :], total[slot][:, :, :]).then_inc(s["inv"], 1)
                    dve.wait_ge(s["pv"], H1 * b + H1)
                    for t in range(TPB):
                        dve.wait_ge(s["o_tmp"], TPB * b + t + 1)
                        nc.vector.tensor_tensor(osb[:, t, :], bank[4 + t][:, :], osb[:, t, :], ALU.add).then_inc(s["o_add"], 1)

                per_image(dve, image)
                dve.wait_ge(s["wo_ps"], B)
                dve.wait_ge(s["hb"], B)
                nc.vector.tensor_tensor(hrow[:, tiles(B - 1), :], bank[0][:, :].rearrange("p (t d) -> p t d", t=TPB),
                                        hrow[:, tiles(B - 1), :], ALU.add).then_inc(s["h_done"], 1)

            @block.scalar
            def _(act):
                def rows_t(b, slot, early):
                    act.wait_ge(s["x2t_ps"], b + 1)
                    if not early:
                        act.wait_ge(s["vc_ps"], b - 1)
                    nc.scalar.copy(x2t[slot][:, :, 1:POS], bank[0][:, :].rearrange("p (k n) -> p k n", k=KD)).then_inc(s["x2t"], 1)

                def odd_unit(b, slot, u):
                    act.wait_ge(s["qk_ps"], UNITS * b + u + 1)
                    if u < 2 * KI:
                        nc.scalar.copy(qk[slot][:, u, :], kvbank[:, 1, 0:POS]).then_inc(s["odd_out"], 1)
                    else:
                        nc.scalar.copy(vrow[slot][:, u - 2 * KI, :], kvbank[:, 1, :]).then_inc(s["odd_out"], 1)

                def cls_v(b, slot):
                    act.wait_ge(s["vc_ps"], b + 1)
                    nc.scalar.copy(vcls[slot][:, :], bank[0][:, :]).then_inc(s["vc"], 1)

                def out_t(b, t):
                    act.wait_ge(s["ot_ps"], TPB * b + t + 1)
                    nc.scalar.copy(ot[:, :, P * t:P * t + P], bank[0][:, :].rearrange("p (c n) -> p c n", c=KI)).then_inc(s["ot"], 1)

                act.wait_ge(g["xct_ps"], 1)
                nc.scalar.copy(x2ct[:, :, :], bank[1][:, 0:KD * B].rearrange("p (k b) -> p k b", k=KD)).then_inc(g["xct"], 1)
                first_cls = bank[1][:, 0:KD * B].rearrange("p (k b) -> p k b", k=KD)[:, :, 0:1]
                nc.scalar.copy(x2t[0][:, :, 0:1], first_cls).then_inc(s["x2c"], 1)
                nc.scalar.copy(xcb[0][:, :, :], first_cls.broadcast_to([P, KD, P])).then_inc(s["xcb"], 1)
                rows_t(0, 0, True)
                odd_unit(0, 0, 1)
                odd_unit(0, 0, 3)
                act.wait_ge(g["oc_ps"], 1)
                nc.scalar.copy(oc[:, :], bank[3][0:B, :]).then_inc(g["oc"], 1)
                odd_unit(0, 0, 5)
                act.wait_ge(g["oct_ps"], 1)
                nc.scalar.copy(oct_[:, :, :], bank[4][:, 0:KI * B].rearrange("p (k b) -> p k b", k=KI)).then_inc(g["oct"], 1)
                for u in range(7, UNITS, 2):
                    odd_unit(0, 0, u)
                cls_v(0, 0)

                def image(b, slot, first, last):
                    if not last:
                        rows_t(b + 1, 1 - slot, first)
                    for h in range(H1):
                        act.wait_ge(s["smax"], H1 * b + h + 1)
                        if h == 0 and not first:
                            act.wait_ge(s["pt_ps"], H1 * b)
                            act.wait_ge(s["o_tmp"], TPB * b)
                            act.wait_ge(s["inv"], b)
                        for t in range(TPB):
                            at, n = tile_at[t], 1 + P * (t + 1)
                            ins = nc.scalar.activation(prob[:, h, at:at + n], sx[h % 2][:, at:at + n], ACT.Exp, bias=low[:, h % 2, t:t + 1],
                                                       scale=-1.0, accum_out=total[slot][:, t, h:h + 1])
                        ins.then_inc(s["p_done"], 1)
                        if h < TPB and not first:
                            out_t(b - 1, h)
                        if h % 2 == 1 and not last:
                            odd_unit(b + 1, 1 - slot, h)
                    if not last:
                        odd_unit(b + 1, 1 - slot, H1 + 1)
                        cls_v(b + 1, 1 - slot)

                per_image(act, image)
                for t in range(TPB):
                    out_t(B - 1, t)

            @block.tensor
            def _(pe):
                def turn_rows(b, slot):
                    pe.wait_ge(s["xn2"], b + 1)
                    for k in range(KD):
                        for t in range(TPB):
                            ins = nc.tensor.transpose(bank[0][:, ROWS * k + P * t:ROWS * k + P * t + P], xn2[slot][:, t, P * k:P * k + P], ident)
                    ins.then_inc(s["x2t_ps"], 1)

                def unit(b, slot, u, early):
                    if not (early and u < 2):
                        pe.wait_ge(s["odd_out" if u % 2 else "even_out"], HALF * b + u // 2)
                    for k in range(KD):
                        if u < 2 * KI:
                            w = wq1[:, k, P * u:P * u + P] if u < KI else wkv1[:, k, P * (u - KI):P * (u - KI) + P]
                            ins = nc.tensor.matmul(kvbank[:, u % 2, 0:POS], w, x2t[slot][:, k, :], start=(k == 0), stop=(k == KD - 1))
                        else:
                            at = 1 + P * (u - 2 * KI)
                            ins = nc.tensor.matmul(kvbank[:, u % 2, :], x2t[slot][:, k, at:at + P], wkv1[:, k, INNER:2 * INNER], start=(k == 0), stop=(k == KD - 1))
                    ins.then_inc(s["qk_ps"], 1)

                def cls_v(b, slot):
                    for k in range(KD):
                        ins = nc.tensor.matmul(bank[0][:, :], xcb[slot][:, k, :], wkv1[:, k, INNER:2 * INNER], start=(k == 0), stop=(k == KD - 1))
                    ins.then_inc(s["vc_ps"], 1)

                def scores(b, slot, h, first):
                    if not (first and h < 2):
                        pe.wait_ge(s["smax"], H1 * b + h - 1)
                    rows = slice(HD1 * (h % 2), HD1 * (h % 2) + HD1)
                    for t in range(TPB):
                        at, n = tile_at[t], 1 + P * (t + 1)
                        ins = nc.tensor.matmul(bank[1 + h % 2][:, at:at + n], qk[slot][rows, h // 2, 1 + P * t:1 + P * t + P],
                                               qk[slot][rows, KI + h // 2, 0:n], start=True, stop=True)
                    ins.then_inc(s["s_ps"], 1)

                def turn_probs(b, h, first):
                    pe.wait_ge(s["p_done"], H1 * b + h + 1)
                    if not (first and h == 0):
                        pe.wait_ge(s["pt"], H1 * b + h)
                    for i, at in enumerate((1, 2 + P, 2 + 2 * P)):
                        ins = nc.tensor.transpose(bank[3][:, P * i:P * i + P], prob[:, h, at:at + P], ident)
                    ins.then_inc(s["pt_ps"], 1)

                def weighted(b, slot, h):
                    pe.wait_ge(s["pt"], H1 * b + h + 1)
                    cols = slice(HD1 * h, HD1 * h + HD1)
                    nc.tensor.matmul(bank[4][:, cols], pt[h % 2][:, 0:P], vrow[slot][:, 0, cols], start=True, stop=True)
                    nc.tensor.matmul(bank[5][:, cols], pt[h % 2][:, P:2 * P], vrow[slot][:, 0, cols], start=True, stop=False)
                    nc.tensor.matmul(bank[5][:, cols], pt[h % 2][:, 2 * P:3 * P], vrow[slot][:, 1, cols], start=False, stop=True).then_inc(s["pv"], 1)

                def turn_out(b, t):
                    pe.wait_ge(s["o_fin"], TPB * b + t + 1)
                    for c in range(KI):
                        ins = nc.tensor.transpose(bank[0][:, P * c:P * c + P], osb[:, t, P * c:P * c + P], ident)
                    ins.then_inc(s["ot_ps"], 1)

                def project(b):
                    pe.wait_ge(s["ot"], TPB * b + TPB)
                    for t in range(TPB):
                        for c in range(KI):
                            ins = nc.tensor.matmul(bank[0][:, D * t:D * t + D], ot[:, c, P * t:P * t + P], wo1[:, c, :], start=(c == 0), stop=(c == KI - 1))
                    ins.then_inc(s["wo_ps"], 1)

                pe.wait_ge(g["xc"], 1)
                for k in range(KD):
                    ins = nc.tensor.transpose(bank[1][:, B * k:B * k + B], xc2[:, P * k:P * k + P], mat("ident", B)[:, 0:B])
                ins.then_inc(g["xct_ps"], 1)
                turn_rows(0, 0)
                pe.wait_ge(l1_in, 16 * 4)
                pe.wait_ge(s["x2t"], 1)
                pe.wait_ge(s["x2c"], 1)
                pe.wait_ge(s["xcb"], 1)
                for u in range(UNITS):
                    unit(0, 0, u, True)
                    if u == 2:
                        pe.wait_ge(g["xct"], 1)
                        for k in range(KD):
                            ins = nc.tensor.matmul(bank[3][0:B, :], x2ct[:, k, :], wkv1[:, k, INNER:2 * INNER], start=(k == 0), stop=(k == KD - 1))
                        ins.then_inc(g["oc_ps"], 1)
                    if u == 5:
                        pe.wait_ge(g["oc"], 1)
                        for k in range(KI):
                            ins = nc.tensor.transpose(bank[4][:, B * k:B * k + B], oc[:, P * k:P * k + P], mat("ident", B)[:, 0:B])
                        ins.then_inc(g["oct_ps"], 1)
                    if u == 8:
                        pe.wait_ge(g["oct"], 1)
                        for k in range(KI):
                            ins = nc.tensor.matmul(bank[5][0:B, 0:D], oct_[:, k, :], wo1[:, k, :], start=(k == 0), stop=(k == KI - 1))
                        ins.then_inc(g["oo_ps"], 1)
                cls_v(0, 0)

                def image(b, slot, first, last):
                    pe.wait_ge(s["even_out"], HALF * b + KI)
                    pe.wait_ge(s["odd_out"], HALF * b + KI)
                    scores(b, slot, 0, first)
                    scores(b, slot, 1, first)
                    if not last:
                        pe.wait_ge(s["vc"], b + 1)
                        turn_rows(b + 1, 1 - slot)
                    for h in range(H1):
                        if h + 2 < H1:
                            scores(b, slot, h + 2, first)
                        if not last:
                            if h == 0:
                                pe.wait_ge(s["x2t"], b + 2)
                                pe.wait_ge(s["x2c"], b + 2)
                            unit(b + 1, 1 - slot, h, False)
                        if h < TPB and not first:
                            if h > 0 or last:
                                pe.wait_ge(s["ot" if h else "vc"], TPB * b - TPB + 1 if h else b + 1)
                            turn_out(b - 1, h)
                        turn_probs(b, h, first)
                        if h == 0:
                            pe.wait_ge(s["even_out"], HALF * b + HALF)
                            pe.wait_ge(s["odd_out"], HALF * b + HALF)
                            if not first:
                                pe.wait_ge(s["o_add"], TPB * b)
                        else:
                            weighted(b, slot, h - 1)
                        if h == 2 and not first:
                            project(b - 1)
                    if not last:
                        for u in range(H1, UNITS):
                            unit(b + 1, 1 - slot, u, False)
                        if not first:
                            pe.wait_ge(s["h_done"], b)
                        pe.wait_ge(s["xcb"], b + 2)
                        cls_v(b + 1, 1 - slot)
                    weighted(b, slot, H1 - 1)

                per_image(pe, image)
                pe.wait_ge(s["h_done"], B - 1)
                for t in range(TPB):
                    if t:
                        pe.wait_ge(s["ot"], TPB * B - 1)
                    turn_out(B - 1, t)
                project(B - 1)
        scope.close()

        scope = ExitStack()
        NP = B // 2
        TP = 2 * TPB
        b1q = sb("b1q", [P, KF], scope=scope)
        b1r = sb("b1r", [KF, P], scope=scope)
        b2q = sb("b2q", [P, D], scope=scope)
        stat3 = sb("stat3", [P, TP, 6], scope=scope)
        mv3 = sb("mv3", [P, TP, 2], scope=scope)
        var3 = sb("var3", [P, TP], scope=scope)
        rstd3 = sb("rstd3", [P, TP], scope=scope)
        nh3 = sb("nh3", [P, TP], scope=scope)
        xn3 = sb("xn3", [P, TP, D], scope=scope)
        x3t = [sb(f"x3t_{i}", [P, KD, TP * P], scope=scope) for i in range(2)]
        x3ct = sb("x3ct", [P, KD, B], scope=scope)
        statc3 = sb("statc3", [B, 6], scope=scope)
        mvc3 = sb("mvc3", [B, 2], scope=scope)
        varc3 = sb("varc3", [B, 1], scope=scope)
        rstdc3 = sb("rstdc3", [B, 1], scope=scope)
        xc3 = sb("xc3", [B, D], scope=scope)
        W = TP * P
        hq = [sb(f"hq_{i}", [P, W], scope=scope) for i in range(2)]
        knot = [sb(f"knot_{i}", [P, W], scope=scope) for i in range(2)]
        gl = [sb(f"gl_{i}", [P, W], scope=scope) for i in range(2)]
        gr = [sb(f"gr_{i}", [P, W], scope=scope) for i in range(2)]
        frac = [sb(f"frac_{i}", [P, W], scope=scope) for i in range(2)]
        yt = [sb(f"yt_{i}", [P, KF, W], scope=scope) for i in range(2)]
        ytc = sb("ytc", [P, KF, B], scope=scope)
        z = [sb(f"z_{i}", [P, TPB, D], scope=scope) for i in range(2)]
        zc = sb("zc", [B, D], scope=scope)
        shift = sb("shift", [P, 2], scope=scope)
        names = ("w_in b1_ps b1 shift stat aggr var rstd xn x_ps xt h_ps hq knot gl frac rise y0 y1 y z_ps z zr h_out "
                 "statc aggrc varc rstdc xc xc_ps xct hc_ps zc_ps zc").split()
        s = {n: sem("f_" + n) for n in names}
        STEP = 0.25
        N_CHUNK = NP * KF + 1

        def chunk_cols(c):
            return slice(0, W) if c < NP * KF else slice(0, KF * B)

        with nc.Block() as block:
            @block.sync
            def _(sp):
                sp.dma_start(b1r[:, :], dram["L1_ffn_b1"].rearrange("(m p) -> m p", p=P)).then_inc(s["w_in"], 16)
                sp.dma_start(b2q[:, :], dram["L1_ffn_b2"].partition_broadcast(P)).then_inc(s["w_in"], 16)
                for p in range(NP):
                    for i in range(2):
                        sp.wait_ge(s["h_out"], 2 * p + i + 1)
                        b = 2 * p + i
                        sp.dma_start(out[b, 1:POS, :].rearrange("(t p) d -> p t d", p=P), hrow[:, TPB * b:TPB * b + TPB, :]).then_inc(out_stored, 16)
                sp.wait_ge(s["h_out"], B + 1)
                sp.dma_start(out[:, 0, :], hcls[:, :]).then_inc(out_stored, 16)
                sp.wait_ge(out_stored, 16 * (B + 1))

            @block.gpsimd
            def _(pool):
                nc.gpsimd.memset(nh3[:, :], -0.5).then_inc(s["shift"], 1)
                nc.gpsimd.memset(shift[:, 0:1], -ROUND).then_inc(s["shift"], 1)
                nc.gpsimd.memset(shift[:, 1:2], STEP - ROUND).then_inc(s["shift"], 1)
                pool.wait_ge(s["shift"], 3)

                def deviations(p):
                    pool.wait_ge(s["aggr"], TP * p + TP)
                    nc.gpsimd.tensor_scalar(var3[:, :], mv3[:, :, 1], EPS, None, ALU.add).then_inc(s["var"], 1)
                    pool.wait_ge(s["var"], p + 1)
                    nc.gpsimd.tensor_tensor(rstd3[:, :], var3[:, :], nh3[:, :], ALU.pow).then_inc(s["rstd"], 1)

                def chunk(c):
                    i, n = c % 2, chunk_cols(c)
                    pool.wait_ge(s["knot"], c + 1)
                    nc.gpsimd.tensor_tensor(frac[i][:, n], hq[i][:, n], knot[i][:, n], ALU.subtract).then_inc(s["frac"], 1)
                    pool.wait_ge(s["gl"], 2 * c + 2)
                    nc.gpsimd.tensor_tensor(gr[i][:, n], gr[i][:, n], gl[i][:, n], ALU.subtract).then_inc(s["rise"], 1)

                deviations(0)
                pool.wait_ge(s["aggrc"], 1)
                nc.gpsimd.tensor_scalar(varc3[:, :], mvc3[:, 1:2], EPS, None, ALU.add).then_inc(s["varc"], 1)
                pool.wait_ge(s["varc"], 1)
                nc.gpsimd.tensor_tensor(rstdc3[:, :], varc3[:, :], nh3[0:B, 0:1], ALU.pow).then_inc(s["rstdc"], 1)
                deviations(1)
                for p in range(NP):
                    for m in range(KF):
                        chunk(p * KF + m)
                        if m == 1 and p + 2 < NP:
                            deviations(p + 2)
                chunk(NP * KF)

            @block.vector
            def _(dve):
                def statistics(p):
                    for t in range(TP):
                        nc.vector.bn_stats(stat3[:, t, :], hrow[:, TP * p + t, :]).then_inc(s["stat"], 1)
                    for t in range(TP):
                        dve.wait_ge(s["stat"], TP * p + t + 1)
                        nc.vector.bn_aggr(mv3[:, t, :], stat3[:, t, :]).then_inc(s["aggr"], 1)

                def normalise(p):
                    dve.wait_ge(s["rstd"], p + 1)
                    dve.wait_ge(s["aggr"], TP * p + TP)
                    if p:
                        dve.wait_ge(s["x_ps"], p)
                    for t in range(TP):
                        ins = nc.vector.tensor_scalar(xn3[:, t, :], hrow[:, TP * p + t, :], mv3[:, t, 0:1], rstd3[:, t:t + 1], ALU.subtract, ALU.mult)
                    ins.then_inc(s["xn"], 1)

                def knots(c):
                    i, n = c % 2, chunk_cols(c)
                    dve.wait_ge(s["h_ps"], c + 1)
                    if c >= 2:
                        dve.wait_ge(s["frac"], c - 1)
                        dve.wait_ge(s["gl"], 2 * c - 2)
                    if c < NP * KF:
                        nc.vector.tensor_scalar(hq[i][:, n], kvbank[:, i, :], b1q[:, c % KF:c % KF + 1], ROUND, ALU.add, ALU.add).then_inc(s["hq"], 1)
                    else:
                        v = frac[i][:, n].rearrange("p (m b) -> p m b", b=B)
                        dve.wait_ge(s["y0"], c - 1)
                        nc.vector.tensor_tensor(v, bank[2][:, n].rearrange("p (m b) -> p m b", b=B), rep(b1q[:, :], 2, B), ALU.add).then_inc(s["zc"], 1)
                        dve.wait_ge(s["zc"], 1)
                        nc.vector.tensor_scalar(hq[i][:, n], frac[i][:, n], ROUND, None, ALU.add).then_inc(s["hq"], 1)
                    dve.wait_ge(s["hq"], c + 1)
                    nc.vector.tensor_scalar(knot[i][:, n].bitcast(I32), hq[i][:, n].bitcast(I32), -64, None, ALU.bitwise_and).then_inc(s["knot"], 1)

                def interpolate(c):
                    i, n = c % 2, chunk_cols(c)
                    dve.wait_ge(s["frac"], c + 1)
                    dve.wait_ge(s["rise"], c + 1)
                    nc.vector.tensor_tensor(frac[i][:, n], frac[i][:, n], gr[i][:, n], ALU.mult).then_inc(s["y0"], 1)
                    dve.wait_ge(s["y0"], c + 1)
                    nc.vector.scalar_tensor_tensor(gl[i][:, n], frac[i][:, n], 1.0 / STEP, gl[i][:, n], ALU.mult, ALU.add).then_inc(s["y1"], 1)
                    dve.wait_ge(s["y1"], c + 1)
                    if c < NP * KF:
                        p, m = divmod(c, KF)
                        if p >= 2 and m == 0:
                            dve.wait_ge(s["z_ps"], 2 * (p - 1))
                        dst = yt[p % 2][:, m, :]
                        nc.vector.tensor_scalar(dst, gl[i][:, n], ROUND, -ROUND, ALU.add, ALU.add).then_inc(s["y"], 1)
                    else:
                        nc.vector.tensor_scalar(ytc[:, :, :].rearrange("p m b -> p (m b)"), gl[i][:, n], ROUND, -ROUND, ALU.add, ALU.add).then_inc(s["y"], 1)

                def store(p, i):
                    at = TPB * (2 * p + i)
                    n = 2 * p + i
                    dve.wait_ge(s["z_ps"], n + 1)
                    if n >= 2:
                        dve.wait_ge(s["h_out"], n - 1)
                    nc.vector.tensor_tensor(z[i][:, :, :], bank[3 + i][:, :].rearrange("p (t d) -> p t d", t=TPB), rep(b2q[:, :], 1, TPB), ALU.add).then_inc(s["z"], 1)
                    dve.wait_ge(s["z"], n + 1)
                    nc.vector.tensor_scalar(z[i][:, :, :], z[i][:, :, :], ROUND, -ROUND, ALU.add, ALU.add).then_inc(s["zr"], 1)
                    dve.wait_ge(s["zr"], n + 1)
                    nc.vector.tensor_tensor(hrow[:, at:at + TPB, :], hrow[:, at:at + TPB, :], z[i][:, :, :], ALU.add).then_inc(s["h_out"], 1)

                dve.wait_ge(s["w_in"], 32)
                dve.wait_ge(s["b1_ps"], 1)
                nc.vector.tensor_copy(b1q[:, :], bank[5][:, 0:KF]).then_inc(s["b1"], 1)
                statistics(0)
                normalise(0)
                nc.vector.bn_stats(statc3[:, :], hcls[:, :]).then_inc(s["statc"], 1)
                dve.wait_ge(s["statc"], 1)
                nc.vector.bn_aggr(mvc3[:, :], statc3[:, :]).then_inc(s["aggrc"], 1)
                dve.wait_ge(s["rstdc"], 1)
                dve.wait_ge(s["aggrc"], 1)
                nc.vector.tensor_scalar(xc3[:, :], hcls[:, :], mvc3[:, 0:1], rstdc3[:, 0:1], ALU.subtract, ALU.mult).then_inc(s["xc"], 1)
                dve.wait_ge(s["b1"], 1)
                statistics(1)
                normalise(1)
                for c in range(N_CHUNK + 1):
                    if c < N_CHUNK:
                        knots(c)
                    if c:
                        interpolate(c - 1)
                    if c < NP * KF:
                        p, m = divmod(c, KF)
                        if p >= 1 and m == 5:
                            store(p - 1, 0)
                        if p >= 2 and m == 1:
                            store(p - 2, 1)
                        if m == 1 and p + 2 < NP:
                            statistics(p + 2)
                        if m == 4 and p + 2 < NP:
                            normalise(p + 2)
                store(NP - 2, 1)
                for i in range(2):
                    store(NP - 1, i)
                dve.wait_ge(s["zc_ps"], 1)
                nc.vector.tensor_tensor(zc[:, :], bank[5][0:B, 0:D], b2q[0:B, :], ALU.add).then_inc(s["zc"], 1)
                dve.wait_ge(s["zc"], 2)
                nc.vector.tensor_scalar(zc[:, :], zc[:, :], ROUND, -ROUND, ALU.add, ALU.add).then_inc(s["zc"], 1)
                dve.wait_ge(s["zc"], 3)
                nc.vector.tensor_tensor(hcls[:, :], hcls[:, :], zc[:, :], ALU.add).then_inc(s["h_out"], 1)

            @block.scalar
            def _(act):
                def rows_t(p):
                    act.wait_ge(s["x_ps"], p + 1)
                    for k in range(KD):
                        ins = nc.scalar.copy(x3t[p % 2][:, k, :], bank[k][:, :])
                    ins.then_inc(s["xt"], 1)

                rows_t(0)
                act.wait_ge(s["xc_ps"], 1)
                nc.scalar.copy(x3ct[:, :, :], bank[2][:, 0:KD * B].rearrange("p (k b) -> p k b", k=KD)).then_inc(s["xct"], 1)
                act.wait_ge(s["shift"], 3)
                for c in range(N_CHUNK):
                    i, n = c % 2, chunk_cols(c)
                    act.wait_ge(s["knot"], c + 1)
                    if c >= 2:
                        act.wait_ge(s["y"], c - 1)
                    nc.scalar.activation(gl[i][:, n], knot[i][:, n], ACT.Gelu, bias=shift[:, 0:1]).then_inc(s["gl"], 1)
                    nc.scalar.activation(gr[i][:, n], knot[i][:, n], ACT.Gelu, bias=shift[:, 1:2]).then_inc(s["gl"], 1)
                    if c % KF == 0 and c // KF + 1 < NP:
                        rows_t(c // KF + 1)

            @block.tensor
            def _(pe):
                def turn_rows(p):
                    pe.wait_ge(s["xn"], p + 1)
                    if p:
                        pe.wait_ge(s["xt"], p)
                    for k in range(KD):
                        for t in range(TP):
                            ins = nc.tensor.transpose(bank[k][:, P * t:P * t + P], xn3[:, t, P * k:P * k + P], ident)
                    ins.then_inc(s["x_ps"], 1)

                def up(c):
                    p, m = divmod(c, KF)
                    if m == 0:
                        pe.wait_ge(s["xt"], p + 1)
                    if c >= 2:
                        pe.wait_ge(s["hq"], c - 1)
                    for k in range(KD):
                        ins = nc.tensor.matmul(kvbank[:, c % 2, :], w1[:, k, P * m:P * m + P], x3t[p % 2][:, k, :], start=(k == 0), stop=(k == KD - 1))
                    ins.then_inc(s["h_ps"], 1)

                def down(p, t):
                    i = t // TPB
                    n = 2 * p + i
                    if t % TPB == 0 and n >= 2:
                        pe.wait_ge(s["z"], n - 1)
                    if t == 0:
                        pe.wait_ge(s["y"], p * KF + KF)
                    o = bank[3 + i][:, D * (t % TPB):D * (t % TPB) + D]
                    for m in range(KF):
                        ins = nc.tensor.matmul(o, yt[p % 2][:, m, P * t:P * t + P], w2[:, m, :], start=(m == 0), stop=(m == KF - 1))
                    if t % TPB == TPB - 1:
                        ins.then_inc(s["z_ps"], 1)

                pe.wait_ge(s["w_in"], 32)
                nc.tensor.transpose(bank[5][:, 0:KF], b1r[:, :], mat("ident", KF)[:, 0:KF]).then_inc(s["b1_ps"], 1)
                turn_rows(0)
                pe.wait_ge(s["xc"], 1)
                for k in range(KD):
                    ins = nc.tensor.transpose(bank[2][:, B * k:B * k + B], xc3[:, P * k:P * k + P], mat("ident", B)[:, 0:B])
                ins.then_inc(s["xc_ps"], 1)
                pe.wait_ge(w1_in, 16 * (E + 1))
                pe.wait_ge(w2_in, 16 * (E + 1))
                for m in range(KF):
                    up(m)
                    if m == 0:
                        turn_rows(1)
                for p in range(NP):
                    for j in range(KF):
                        if p + 1 < NP:
                            up(KF * (p + 1) + j)
                            if j == 0 and p + 2 < NP:
                                turn_rows(p + 2)
                        if j % 2 == 1:
                            down(p, j // 2)
                    if p == NP - 2:
                        pe.wait_ge(s["xct"], 1)
                        for m in range(KF):
                            for k in range(KD):
                                ins = nc.tensor.matmul(bank[2][:, B * m:B * m + B], w1[:, k, P * m:P * m + P], x3ct[:, k, :], start=(k == 0), stop=(k == KD - 1))
                        ins.then_inc(s["h_ps"], 1)
                pe.wait_ge(s["y"], N_CHUNK)
                for m in range(KF):
                    ins = nc.tensor.matmul(bank[5][0:B, 0:D], ytc[:, m, :], w2[:, m, :], start=(m == 0), stop=(m == KF - 1))
                ins.then_inc(s["zc_ps"], 1)
        scope.close()


_OUT = (B, POS, D)


def kernel(**inputs):
    import numpy as _np
    import concourse.bacc as _bacc
    from concourse import mybir as _mybir
    from concourse.bass_utils import run_bass_kernel_spmd as _run

    nc = _bacc.Bacc("TRN2", target_bir_lowering=False, num_devices=1)
    arrays, dram = {}, {}
    for name, a in [*inputs.items(), *_shape_constants().items()]:
        a = _np.ascontiguousarray(a)
        arrays[f"in_{name}"] = a
        dram[name] = nc.dram_tensor(f"in_{name}", a.shape, _mybir.dt.from_np(a.dtype), kind="ExternalInput").ap()
    out = nc.dram_tensor("out_0", _OUT, _mybir.dt.float32, kind="ExternalOutput").ap()
    vit_tower_kernel(nc, dram, out)
    r = _run(nc, [arrays], core_ids=[0])
    return r.results[0]["out_0"]
```

```python
from contextlib import ExitStack

import numpy as np

import concourse.bass as bass
from concourse import mybir

ALU = mybir.AluOpType
ACT = mybir.ActivationFunctionType
AX = mybir.AxisListType
F32 = mybir.dt.float32
F32R = mybir.dt.float32r
I32 = mybir.dt.int32
U32 = mybir.dt.uint32

P = 128
B = 8
ROWS = 256
D = 256
POS = ROWS + 1
EVEN = POS + POS % 2
KD = D // P
TPB = ROWS // P
NT = B * TPB
NTC = NT + 1
N_TOK = B * POS
EPS = 1e-5
HD0 = 16
E = 8
F = 1024
KF = F // P
CAP = int(N_TOK / E * 1.25) + 1
MT = 3
MR = -(-CAP // MT)
SLOTS = E * CAP
FAR = 1 << 20
H1 = 8
HD1 = 64
INNER = H1 * HD1
KI = INNER // P
BUCKETS = 32
SCOLS = (1 + P) + POS
MASKED = -1e30
ROUND = 49152.0

MATS = {}


def _columns(spec):
    at = 0
    for name, n in spec:
        MATS[name] = (at, n)
        at += n
    return at


N_MATS = _columns([("ident", P), ("flip", P), ("ones", P), ("tri", P), ("above", P), ("haar2", P), ("unhaar2", P), ("haar3", 64),
                   ("unhaar3", 64), ("blocks", KD * P), ("after", B * B), ("tri8", B), ("order", NTC * E),
                   ("first_slot", NTC * E), ("before", NT * E), ("is_cls", 1), ("neg_half", 2)])


def _shape_constants():
    f = np.float32
    m = np.zeros((P, N_MATS), f)

    def put(name, a):
        at, n = MATS[name]
        m[:a.shape[0], at:at + n] = a.reshape(a.shape[0], n)

    put("ident", np.eye(P))
    put("flip", np.eye(P)[::-1])
    put("ones", np.ones((P, P)))
    put("tri", np.triu(np.ones((P, P))))
    put("above", np.triu(np.ones((P, P)), 1))

    def haar(n):
        a = np.zeros((n, n))
        for i in range(n // 2):
            a[2 * i, i] = a[2 * i + 1, i] = a[2 * i, n // 2 + i] = 1
            a[2 * i + 1, n // 2 + i] = -1
        return a

    put("haar2", haar(P))
    put("unhaar2", 0.25 * haar(P).T)
    put("haar3", haar(64))
    put("unhaar3", 0.25 * haar(64).T)
    heads = np.arange(P) // HD0
    block = (heads[:, None] == heads[None, :]) / np.sqrt(HD0)
    put("blocks", np.concatenate([block] * KD, 1))
    after = np.zeros((P, B, B))
    for j in range(B):
        after[:, j, j + 1:] = 1
    put("after", after)
    put("tri8", np.triu(np.ones((B, B))))
    put("order", np.broadcast_to(np.arange(E, 0, -1), (P, NTC, E)))
    put("first_slot", np.broadcast_to(np.arange(E) * CAP - 1, (P, NTC, E)))
    before = np.zeros((B, NT, E))
    for b in range(B):
        before[b, b * TPB:] = 1
    put("before", before)
    put("is_cls", (np.arange(P) < B).astype(f)[:, None])
    put("neg_half", np.full((P, 2), -0.5))

    freqs = (f(1.0) / np.power(f(10000.0), np.arange(0, HD0, 2, dtype=f))).astype(f)
    angle = (np.arange(POS, dtype=f)[:, None] * freqs[None, :]).astype(f)[1:]
    cos = np.repeat(np.cos(angle), 2, axis=1).astype(f)
    sin = np.stack([-np.sin(angle), np.sin(angle)], -1).reshape(ROWS, HD0).astype(f)
    pairs = np.concatenate([np.arange(r, ROWS, 2) for r in range(2)])
    cos, sin = (np.tile(a[pairs], (1, D // HD0)) for a in (cos, sin))
    rope_t = np.stack([cos.T.reshape(KD, P, ROWS), sin.T.reshape(KD, P, ROWS)])
    rope_q = np.ascontiguousarray(rope_t.transpose(2, 0, 1, 3)).astype(f)
    rope_k = np.stack([cos.reshape(TPB, P, D), sin.reshape(TPB, P, D)])
    rope_k = np.ascontiguousarray(rope_k.transpose(2, 0, 1, 3)).astype(f)

    n = (ROWS - np.arange(2 * ROWS)).astype(np.int64)
    exact = BUCKETS // 2
    big = exact + (np.log(np.maximum(n, 1).astype(f) / exact) / np.log(128 / exact)
                   * (BUCKETS - exact)).astype(np.int32)
    bucket = np.where(n < exact, n, np.minimum(big, BUCKETS - 1))
    hot = np.zeros((BUCKETS + 1, 2 * ROWS), f)
    for v in range(2 * ROWS):
        hot[bucket[v] if n[v] >= 0 else BUCKETS, v] = 1
    far = np.full((1, H1), MASKED, f)
    return {"c_mats": m, "c_rope_q": rope_q, "c_rope_k": rope_k, "c_buckets": hot, "c_masked": far}


def rep(ap, axis, n):
    wide = ap.unsqueeze(axis)
    shape = list(wide.shape)
    shape[axis] = n
    return wide.broadcast_to(shape)


def vit_tower_kernel(nc, dram, out):
    ctx = ExitStack()
    with ctx:
        def sem(name):
            return ctx.enter_context(nc.semaphore(name))

        def sb(name, shape, dt=F32, scope=ctx):
            return scope.enter_context(nc.sbuf_tensor(name, shape, dt))

        early = []

        def early_sem(name):
            early.append(nc.alloc_semaphore(name=name))
            return early[-1]

        bank = [ctx.enter_context(nc.psum_tensor(f"bank{i}", [P, 512], F32)) for i in range(3)]
        kvbank = ctx.enter_context(nc.psum_tensor("kvbank", [P, 2, 512], F32))
        bank += [ctx.enter_context(nc.psum_tensor(f"bank{i}", [P, 512], F32)) for i in range(3, 6)]

        mats = sb("mats", [P, N_MATS])

        def mat(name, parts=P):
            at, n = MATS[name]
            return mats[0:parts, at:at + n]

        ident, ones = mat("ident"), mat("ones")

        hrow = sb("hrow", [P, NT, D])
        hcls = sb("hcls", [B, D])
        w1 = sb("w1", [P, KD, F])
        w2 = sb("w2", [P, KF, D])
        w1h, w1l, w2h, w2l = ([sb(n, [P, KD, F] if n < "w2" else [P, KF, D], F32R)] for n in ("w1h0", "w1l0", "w2h0", "w2l0"))
        wq1 = sb("wq1", [P, KD, INNER])
        wkv1 = sb("wkv1", [P, KD, 2 * INNER])
        wo1 = sb("wo1", [P, KI, D])
        bo1 = sb("bo1", [P, D])
        toeplitz = sb("toeplitz", [P, H1, SCOLS])
        xrow = sb("xrow", [P, NT, D])
        xcls = sb("xcls", [B, D])
        to_slot = sb("to_slot", [P, NTC], U32)
        back_pairs = sb("back_pairs", [P, TPB, 2, B])
        back = sb("back", [P, TPB, 2, B])
        back_cls = sb("back_cls", [B, 2])

        buf = nc.dram_tensor("expert_in", [SLOTS + MT * MR - CAP, D], F32, kind="Internal").ap()
        ybuf = nc.dram_tensor("expert_out", [SLOTS, D], F32, kind="Internal").ap()
        bias_rev = nc.dram_tensor("bias_rev", [H1, 2 * ROWS], F32, kind="Internal").ap()

        mats_in = sem("mats_in")
        w1_in, w2_in = sem("w1_in"), sem("w2_in")
        w1_high, w2_high, w1_low, w2_low = (sem(n) for n in ("w1_high", "w2_high", "w1_low", "w2_low"))
        buf_zeroed = sem("buf_zeroed")
        l0_in = sem("l0_in")
        l1_in = sem("l1_in")
        out_stored = sem("out_stored")
        stored = 0

        def apart(eng):
            eng.wait_ge(mats_in, 16)

        def waits_apart(eng, *waits):
            waits = [(which, value if isinstance(value, int) else eng.to_reg(value)) for which, value in waits]
            if not all(isinstance(value, int) for _, value in waits):
                apart(eng)
            for which, value in waits:
                eng.wait_ge(which, value)

        def high(engine, x, to):
            return (engine.copy if engine is nc.scalar else engine.tensor_copy)(to, x)

        def low_part(engine, x, of, to):
            return engine.tensor_tensor(to, x, of.bitcast(F32), ALU.subtract)

        def product(to, ws, xs, start, stop):
            (wh, wl), (xh, xl) = ws, xs
            nc.tensor.matmul(to, wl, xh, start=start, stop=False)
            nc.tensor.matmul(to, wh, xl, start=False, stop=False)
            return nc.tensor.matmul(to, wh, xh, start=False, stop=stop)

        attn0 = ExitStack()
        wq0 = sb("wq0", [P, KD, D], scope=attn0)
        wqs0 = sb("wqs0", [P, KD, D], scope=attn0)
        wkv0 = sb("wkv0", [P, KD, 2 * D], scope=attn0)
        wo0 = sb("wo0", [P, KD, D], scope=attn0)
        wg = sb("wg", [P, KD, E], scope=attn0)
        ropeq = sb("ropeq", [P, 2, KD, ROWS], scope=attn0)
        ropek = sb("ropek", [P, 2, TPB, D], scope=attn0)
        bqm = sb("bqm", [P, KD], scope=attn0)
        bqs = sb("bqs", [P, KD], scope=attn0)
        bkv = sb("bkv", [P, 2 * D], scope=attn0)
        bo0 = sb("bo0", [P, D], scope=attn0)
        clsb = sb("clsb", [B, D], scope=attn0)
        emb = sb("emb", [BUCKETS + 1, H1], scope=attn0)
        hot = sb("hot", [BUCKETS + 1, 2 * ROWS], scope=attn0)
        bias = {n: early_sem("bias_" + n) for n in "emb_in emb brev_ps brev brev_out rev_in flip_ps flip_out".split()}

        nh16 = sb("nh16", [P, NT], scope=attn0)
        statc = sb("statc", [B, 6], scope=attn0)
        mvc = sb("mvc", [B, 2], scope=attn0)
        varc = sb("varc", [B, 1], scope=attn0)
        rstdc = sb("rstdc", [B, 1], scope=attn0)
        xc0 = sb("xc0", [B, D], scope=attn0)
        xct0 = sb("xct0", [P, KD, B], scope=attn0)
        qc0 = sb("qc0", [P, KD, B], scope=attn0)
        kvc = sb("kvc", [1, 2 * D], scope=attn0)
        c = {n: early_sem("c_" + n) for n in "nh swapped stat aggr var rstd xc0 xct_ps xct qc_ps qc kvc_ps kvc".split()}
        l0_all = 16 * 14

        tok = ExitStack()
        img = xrow[:, :, :].rearrange("p (b r) w -> p b r w", r=2)
        lohi = sb("lohi", [P, B, 2, 2, P], scope=tok)
        a1 = sb("a1", [P, B, P], scope=tok)
        d1 = sb("d1", [P, B, 3, P], scope=tok)
        wd3 = sb("wd3", [P, 3, 3 * P], scope=tok)
        wd2 = sb("wd2", [P, 2, 64 * 3], scope=tok)
        wd1 = sb("wd1", [64, 2, 32 * 3], scope=tok)
        wa = sb("wa", [32, 32], scope=tok)
        tokb = sb("tokb", [P, 10], scope=tok)
        lh2 = sb("lh2", [P, 2, B, 64], scope=tok)
        c2 = sb("c2", [P, 2, B, 64], scope=tok)
        lh3 = sb("lh3", [64, 2, B, 32], scope=tok)
        c3 = sb("c3", [64, 2, B, 32], scope=tok)
        junk = sb("junk", [P, 2, 3, P], scope=tok)
        dots = sb("dots", [P, 80], scope=tok)
        lev = sb("lev", [P, 4, 3 * B * 3], scope=tok)
        red = sb("red", [P, 3, 3 * B], scope=tok)
        asig = sb("asig", [P, 3, B], scope=tok)
        f1 = sb("f1", [P, 2, B, 3], scope=tok)
        f2 = sb("f2", [P, 2, B], scope=tok)
        f3 = sb("f3", [64, 2, B], scope=tok)

        names = ("tok_w_in tok_zero lo_done a1_done d1_done lh2_done c2_ps c2_done lh3_done c3_ps c3_done dots_done "
                 "dots_ps logit_done exp_done w_step w_done scaled c3_scaled c2_scaled un3_ps un3_done a2_done un2_ps un2_done a1_new "
                 "merged").split()
        s = {n: early_sem("t_" + n) for n in names}
        img_in = [early_sem(f"img_in{half}") for half in range(2)]

        def split(engine, half, hi):
            q = slice(B // 2 * half, B // 2 * half + B // 2)
            engine.tensor_tensor(lohi[:, q, hi, :, :], img[:, q, :, 0::2], img[:, q, :, 1::2], ALU.subtract if hi else ALU.add).then_inc(s["lo_done"], 1)

        def merge(engine, half, odd):
            q = slice(B // 2 * half, B // 2 * half + B // 2)
            to = hrow[:, :, :].rearrange("p (b r) d -> p b r d", r=2)[:, q, :, odd::2]
            engine.tensor_tensor(to, lohi[:, q, 0, :, :], lohi[:, q, 1, :, :], ALU.subtract if odd else ALU.add).then_inc(s["merged"], 1)
        with nc.Block() as block:
            @block.sync
            def _(sp):
                for half in range(2):
                    b0, b1 = B // 2 * half, B // 2 * half + B // 2
                    sp.dma_start(img[:, b0:b1, :, :], dram["x"][b0:b1].rearrange("b (p r) w o -> p b r (w o)", r=2)).then_inc(img_in[half], 16)
                    if half == 0:
                        sp.dma_start(mats[:, :], dram["c_mats"]).then_inc(mats_in, 16)
                sp.dma_start(wd3[:, :, :], dram["L0_tok_Wd3"].rearrange("(c i j) k -> i c (j k)", c=3, i=P)).then_inc(s["tok_w_in"], 16)
                v2 = dram["L0_tok_Wd2"].rearrange("(c i j) k -> c i (j k)", c=3, i=64)
                v1 = dram["L0_tok_Wd1"].rearrange("(c i j) k -> c i (j k)", c=3, i=32)
                for w, v, n in ((wd2, v2, 64), (wd1, v1, 32)):
                    sp.dma_start(w[n:2 * n, 0, :], v[0]).then_inc(s["tok_w_in"], 16)
                    sp.dma_start(w[0:n, 1, :], v[1]).then_inc(s["tok_w_in"], 16)
                    sp.dma_start(w[n:2 * n, 1, :], v[2]).then_inc(s["tok_w_in"], 16)
                sp.dma_start(wa[:, :], dram["L0_tok_Wa"].rearrange("(i j) o -> i (j o)", i=32)).then_inc(s["tok_w_in"], 16)
                for i, n in enumerate(("L0_tok_bd3", "L0_tok_bd2", "L0_tok_bd1")):
                    sp.dma_start(tokb[:, 3 * i:3 * i + 3], dram[n].partition_broadcast(P)).then_inc(s["tok_w_in"], 16)
                sp.dma_start(tokb[:, 9:10], dram["L0_tok_ba"].partition_broadcast(P)).then_inc(s["tok_w_in"], 16)
                sp.dma_start(wq0[:, :, :], dram["L0_attn_Wq"].rearrange("(k p) n -> p k n", p=P)).then_inc(l0_in, 16)
                sp.dma_start(wkv0[:, :, 0:D], dram["L0_attn_Wk"].rearrange("(k p) n -> p k n", p=P)).then_inc(l0_in, 16)
                sp.dma_start(wkv0[:, :, D:2 * D], dram["L0_attn_Wv"].rearrange("(k p) n -> p k n", p=P)).then_inc(l0_in, 16)
                sp.dma_start(wo0[:, :, :], dram["L0_attn_Wo"].rearrange("(k p) n -> p k n", p=P)).then_inc(l0_in, 16)
                sp.dma_start(wg[:, :, :], dram["L0_ffn_wg"].rearrange("(k p) n -> p k n", p=P)).then_inc(l0_in, 16)
                sp.dma_start(ropeq[:, :, :, :], dram["c_rope_q"]).then_inc(l0_in, 16)
                sp.dma_start(ropek[:, :, :, :], dram["c_rope_k"]).then_inc(l0_in, 16)
                with nc.allow_non_contiguous_dma(reason="one bias per partition"):
                    sp.dma_start(bqm[:, :], dram["L0_attn_bq"].rearrange("(m p) -> p m", p=P)).then_inc(l0_in, 16)
                    for r in range(2):
                        sp.dma_start(bqs[r:P:2, :], dram["L0_attn_bq"].rearrange("(m q r) -> r q m", m=KD, r=2)[1 - r]).then_inc(l0_in, 16)
                sp.dma_start(bkv[:, 0:D], dram["L0_attn_bk"].partition_broadcast(P)).then_inc(l0_in, 16)
                sp.dma_start(bkv[:, D:2 * D], dram["L0_attn_bv"].partition_broadcast(P)).then_inc(l0_in, 16)
                sp.dma_start(bo0[:, :], dram["L0_attn_bo"].partition_broadcast(P)).then_inc(l0_in, 16)
                sp.dma_start(clsb[:, :], dram["cls_tok"].rearrange("a b d -> (a b d)").partition_broadcast(B)).then_inc(l0_in, 16)
                sp.dma_start(emb[0:BUCKETS, :], dram["L1_attn_rel_emb"]).then_inc(bias["emb_in"], 16)
                sp.dma_start(emb[BUCKETS:BUCKETS + 1, :], dram["c_masked"]).then_inc(bias["emb_in"], 16)
                sp.dma_start(hot[:, :], dram["c_buckets"]).then_inc(bias["emb_in"], 16)

            @block.gpsimd
            def _(pool):
                pool.wait_ge(img_in[1], 16)
                split(nc.gpsimd, 1, 1)
                nc.gpsimd.memset(nh16[:, :], -0.5).then_inc(c["nh"], 1)
                pool.wait_ge(l0_in, l0_all)
                nc.gpsimd.tensor_copy(wqs0[:, :, 0::2], wq0[:, :, 1::2]).then_inc(c["swapped"], 1)
                nc.gpsimd.tensor_copy(wqs0[:, :, 1::2], wq0[:, :, 0::2]).then_inc(c["swapped"], 1)
                pool.wait_ge(c["aggr"], 1)
                pool.wait_ge(c["nh"], 1)
                nc.gpsimd.tensor_scalar(varc[:, :], mvc[:, 1:2], EPS, None, ALU.add).then_inc(c["var"], 1)
                pool.wait_ge(c["var"], 1)
                nc.gpsimd.tensor_tensor(rstdc[:, :], varc[:, :], nh16[0:B, 0:1], ALU.pow).then_inc(c["rstd"], 1)
                pool.wait_ge(s["w_done"], 7)
                nc.gpsimd.tensor_tensor(d1[:, :, 0, :], d1[:, :, 0, :], rep(f1[:, 0, :, 0], 2, P), ALU.mult).then_inc(s["scaled"], 1)
                pool.wait_ge(s["a1_new"], 6)
                merge(nc.gpsimd, 1, 1)

            @block.vector
            def _(dve):
                nc.vector.memset(dots[:, :], 0.0).then_inc(s["tok_zero"], 1)
                nc.vector.memset(wd2[0:64, 0, :], 0.0).then_inc(s["tok_zero"], 1)
                nc.vector.memset(wd1[0:32, 0, :], 0.0).then_inc(s["tok_zero"], 1)
                for half, hi in ((0, 0), (0, 1), (1, 0)):
                    dve.wait_ge(img_in[half], 16)
                    split(nc.vector, half, hi)
                dve.wait_ge(s["lo_done"], 4)
                nc.vector.tensor_tensor(a1[:, :, :], lohi[:, :, 0, 0, :], lohi[:, :, 0, 1, :], ALU.add).then_inc(s["a1_done"], 1)
                nc.vector.tensor_tensor(d1[:, :, 0, :], lohi[:, :, 0, 0, :], lohi[:, :, 0, 1, :], ALU.subtract).then_inc(s["d1_done"], 1)
                nc.vector.tensor_tensor(d1[:, :, 1, :], lohi[:, :, 1, 0, :], lohi[:, :, 1, 1, :], ALU.add).then_inc(s["d1_done"], 1)
                nc.vector.tensor_tensor(d1[:, :, 2, :], lohi[:, :, 1, 0, :], lohi[:, :, 1, 1, :], ALU.subtract).then_inc(s["d1_done"], 1)
                dve.wait_ge(s["a1_done"], 1)
                nc.vector.tensor_tensor(lh2[:, 0, :, :], a1[:, :, 0::2], a1[:, :, 1::2], ALU.add).then_inc(s["lh2_done"], 1)
                nc.vector.tensor_tensor(lh2[:, 1, :, :], a1[:, :, 0::2], a1[:, :, 1::2], ALU.subtract).then_inc(s["lh2_done"], 1)
                dve.wait_ge(s["tok_w_in"], 16 * 12)
                dve.wait_ge(s["tok_zero"], 3)
                dve.wait_ge(s["d1_done"], 3)
                n_dots = 0

                def products():
                    nonlocal n_dots
                    n_dots += 1
                    if n_dots > 2:
                        dve.wait_ge(s["dots_done"], n_dots - 2)
                    return junk[:, n_dots % 2, :, :]

                w3v = wd3[:, :, :].rearrange("p c (j k) -> p c j k", k=3)
                for b in range(B):
                    for k in range(3):
                        nc.vector.tensor_tensor_reduce(products(), d1[:, b, :, :], w3v[:, :, :, k], 1.0, 0.0, ALU.mult,
                                                       ALU.add, dots[:, 3 * b + k:3 * b + k + 1]).then_inc(s["dots_done"], 1)
                dve.wait_ge(s["c2_done"], 2)
                nc.vector.tensor_tensor(lh3[:, 0, :, :], c2[0:64, 0, :, 0::2], c2[0:64, 0, :, 1::2], ALU.add).then_inc(s["lh3_done"], 1)
                nc.vector.tensor_tensor(lh3[:, 1, :, :], c2[0:64, 0, :, 0::2], c2[0:64, 0, :, 1::2], ALU.subtract).then_inc(s["lh3_done"], 1)
                w2v = wd2[:, :, :].rearrange("p c (j k) -> p c j k", k=3)
                for b in range(B):
                    for k in range(3):
                        nc.vector.tensor_tensor_reduce(products()[:, 0:2, 0:64], c2[:, :, b, :], w2v[:, :, :, k], 1.0, 0.0, ALU.mult,
                                                       ALU.add, dots[:, 24 + 3 * b + k:24 + 3 * b + k + 1]).then_inc(s["dots_done"], 1)
                dve.wait_ge(l0_in, l0_all)
                nc.vector.bn_stats(statc[:, :], clsb[:, :]).then_inc(c["stat"], 1)
                dve.wait_ge(c["stat"], 1)
                nc.vector.bn_aggr(mvc[:, :], statc[:, :]).then_inc(c["aggr"], 1)
                dve.wait_ge(s["c3_done"], 1)
                w1v = wd1[:, :, :].rearrange("p c (j k) -> p c j k", k=3)
                for b in range(B):
                    for k in range(3):
                        nc.vector.tensor_tensor_reduce(products()[0:64, 0:2, 0:32], c3[:, :, b, :], w1v[:, :, :, k], 1.0, 0.0, ALU.mult,
                                                       ALU.add, dots[0:64, 48 + 3 * b + k:48 + 3 * b + k + 1]).then_inc(s["dots_done"], 1)
                    nc.vector.tensor_tensor_reduce(products()[0:32, 0, 0:32], c3[0:32, 0, b, :], wa[:, :], 1.0, 0.0, ALU.mult,
                                                   ALU.add, dots[0:32, 72 + b:73 + b]).then_inc(s["dots_done"], 1)
                dve.wait_ge(c["rstd"], 1)
                dve.wait_ge(c["aggr"], 1)
                nc.vector.tensor_scalar(xc0[:, :], clsb[:, :], mvc[:, 0:1], rstdc[:, 0:1], ALU.subtract, ALU.mult).then_inc(c["xc0"], 1)
                dve.wait_ge(s["dots_ps"], 1)
                for i in range(3):
                    nc.vector.scalar_tensor_tensor(lev[:, 0, 24 * i:24 * i + 24].rearrange("p (b k) -> p b k", k=3),
                                                   bank[1][:, 24 * i:24 * i + 24].rearrange("p (b k) -> p b k", k=3),
                                                   0.5 ** (i + 1), rep(tokb[:, 3 * i:3 * i + 3], 1, B), ALU.mult,
                                                   ALU.add).then_inc(s["w_step"], 1)
                nc.vector.tensor_scalar(asig[:, 0, :], bank[1][:, 72:80], 0.125, tokb[:, 9:10], ALU.mult, ALU.add).then_inc(s["w_step"], 1)
                dve.wait_ge(s["w_step"], 4)
                z = lev[:, 0, :].rearrange("p (n k) -> p n k", k=3)
                nc.vector.tensor_reduce(red[:, 0, :], z, AX.X, ALU.max).then_inc(s["w_step"], 1)
                dve.wait_ge(s["w_step"], 5)
                nc.vector.tensor_tensor(lev[:, 1, :].rearrange("p (n k) -> p n k", k=3), z, rep(red[:, 0, :], 2, 3), ALU.subtract).then_inc(s["logit_done"], 1)
                dve.wait_ge(s["exp_done"], 2)
                ez = lev[:, 2, :].rearrange("p (n k) -> p n k", k=3)
                nc.vector.tensor_reduce(red[:, 1, :], ez, AX.X, ALU.add).then_inc(s["w_step"], 1)
                nc.vector.tensor_scalar(asig[:, 2, :], asig[:, 1, :], 1.0, None, ALU.add).then_inc(s["w_step"], 1)
                dve.wait_ge(s["w_step"], 7)
                nc.vector.reciprocal(red[:, 2, :], red[:, 1, :]).then_inc(s["w_step"], 1)
                nc.vector.reciprocal(asig[:, 0, :], asig[:, 2, :]).then_inc(s["w_step"], 1)
                dve.wait_ge(s["w_step"], 9)
                nc.vector.tensor_tensor(lev[:, 3, :].rearrange("p (n k) -> p n k", k=3), ez, rep(red[:, 2, :], 2, 3), ALU.mult).then_inc(s["w_step"], 1)
                dve.wait_ge(s["w_step"], 10)
                wv = lev[:, 3, :].rearrange("p (l b k) -> p l k b", l=3, k=3)
                nc.vector.tensor_copy(f3[0:32, 0, :], asig[0:32, 0, :]).then_inc(s["w_done"], 1)
                nc.vector.tensor_copy(f3[0:32, 1, :], wv[0:32, 2, 1, :]).then_inc(s["w_done"], 1)
                nc.vector.tensor_copy(f3[32:64, :, :], wv[32:64, 2, 0::2, :]).then_inc(s["w_done"], 1)
                nc.vector.memset(f2[0:64, 0, :], 1.0).then_inc(s["w_done"], 1)
                nc.vector.tensor_copy(f2[0:64, 1, :], wv[0:64, 1, 1, :]).then_inc(s["w_done"], 1)
                nc.vector.tensor_copy(f2[64:P, :, :], wv[64:P, 1, 0::2, :]).then_inc(s["w_done"], 1)
                nc.vector.tensor_scalar(f1[:, 0, :, :], lev[:, 3, 0:24].rearrange("p (b k) -> p b k", k=3), 0.25, None, ALU.mult).then_inc(s["w_done"], 1)
                dve.wait_ge(s["w_done"], 7)
                nc.vector.tensor_tensor(c3[:, :, :, :], c3[:, :, :, :], rep(f3[:, :, :], 3, 32), ALU.mult).then_inc(s["c3_scaled"], 1)
                for k in range(1, 3):
                    nc.vector.tensor_tensor(d1[:, :, k, :], d1[:, :, k, :], rep(f1[:, 0, :, k], 2, P), ALU.mult).then_inc(s["scaled"], 1)
                dve.wait_ge(s["un3_done"], 1)
                u3 = lh3
                nc.vector.tensor_tensor(c2[0:64, 0, :, 0::2], u3[:, 0, :, :], u3[:, 1, :, :], ALU.add).then_inc(s["a2_done"], 1)
                nc.vector.tensor_tensor(c2[0:64, 0, :, 1::2], u3[:, 0, :, :], u3[:, 1, :, :], ALU.subtract).then_inc(s["a2_done"], 1)
                dve.wait_ge(s["a2_done"], 2)
                nc.vector.tensor_tensor(c2[:, :, :, :], c2[:, :, :, :], rep(f2[:, :, :], 3, 64), ALU.mult).then_inc(s["c2_scaled"], 1)
                dve.wait_ge(s["scaled"], 3)
                dve.wait_ge(c["qc_ps"], 1)
                for m in range(KD):
                    nc.vector.tensor_scalar(qc0[:, m, :], bank[4][:, B * m:B * m + B], bqm[:, m:m + 1], None, ALU.add).then_inc(c["qc"], 1)
                dve.wait_ge(c["kvc_ps"], 1)
                nc.vector.tensor_tensor(kvc[:, :], bank[5][0:1, :], bkv[0:1, :], ALU.add).then_inc(c["kvc"], 1)
                nc.vector.tensor_tensor(lohi[:, :, 1, 0, :], d1[:, :, 1, :], d1[:, :, 2, :], ALU.add).then_inc(s["a1_new"], 1)
                nc.vector.tensor_tensor(lohi[:, :, 1, 1, :], d1[:, :, 1, :], d1[:, :, 2, :], ALU.subtract).then_inc(s["a1_new"], 1)
                dve.wait_ge(s["un2_done"], 2)
                nc.vector.tensor_tensor(a1[:, :, 0::2], lh2[:, 0, :, :], lh2[:, 1, :, :], ALU.add).then_inc(s["a1_new"], 1)
                nc.vector.tensor_tensor(a1[:, :, 1::2], lh2[:, 0, :, :], lh2[:, 1, :, :], ALU.subtract).then_inc(s["a1_new"], 1)
                dve.wait_ge(s["a1_new"], 4)
                nc.vector.tensor_tensor(lohi[:, :, 0, 0, :], a1[:, :, :], d1[:, :, 0, :], ALU.add).then_inc(s["a1_new"], 1)
                nc.vector.tensor_tensor(lohi[:, :, 0, 1, :], a1[:, :, :], d1[:, :, 0, :], ALU.subtract).then_inc(s["a1_new"], 1)
                dve.wait_ge(s["a1_new"], 6)
                for half, hi in ((0, 0), (0, 1), (1, 0)):
                    merge(nc.vector, half, hi)

            @block.tensor
            def _(pe):
                pe.wait_ge(mats_in, 16)
                for g in range(2):
                    pe.wait_ge(s["lh2_done"], g + 1)
                    nc.tensor.matmul(kvbank[:, g, :], mat("haar2"), lh2[:, g, :, :], start=True, stop=True).then_inc(s["c2_ps"], 1)
                pe.wait_ge(s["lh3_done"], 2)
                nc.tensor.matmul(bank[0][0:64, :], mat("haar3", 64), lh3[:, :, :, :], start=True, stop=True).then_inc(s["c3_ps"], 1)
                pe.wait_ge(s["dots_done"], 24 + 24 + 32)
                nc.tensor.matmul(bank[1][:, 0:80], ones, dots[:, :], start=True, stop=True).then_inc(s["dots_ps"], 1)
                pe.wait_ge(l0_in, l0_all)
                pe.wait_ge(c["xc0"], 1)
                for k in range(KD):
                    ins = nc.tensor.transpose(bank[3][:, B * k:B * k + B], xc0[:, P * k:P * k + P], mat("ident", B)[:, 0:B])
                ins.then_inc(c["xct_ps"], 1)
                pe.wait_ge(c["xct"], 1)
                for m in range(KD):
                    for k in range(KD):
                        ins = nc.tensor.matmul(bank[4][:, B * m:B * m + B], wq0[:, k, P * m:P * m + P], xct0[:, k, :], start=(k == 0), stop=(k == KD - 1))
                ins.then_inc(c["qc_ps"], 1)
                for k in range(KD):
                    ins = nc.tensor.matmul(bank[5][0:1, :], xct0[:, k, 0:1], wkv0[:, k, :], start=(k == 0), stop=(k == KD - 1))
                ins.then_inc(c["kvc_ps"], 1)
                pe.wait_ge(s["c3_scaled"], 1)
                nc.tensor.matmul(bank[0][0:64, :], mat("unhaar3", 64), c3[:, :, :, :], start=True, stop=True).then_inc(s["un3_ps"], 1)
                pe.wait_ge(s["c2_scaled"], 1)
                for g in range(2):
                    nc.tensor.matmul(kvbank[:, g, :], mat("unhaar2"), c2[:, g, :, :], start=True, stop=True).then_inc(s["un2_ps"], 1)

            @block.scalar
            def _(act):
                for g in range(2):
                    act.wait_ge(s["c2_ps"], g + 1)
                    nc.scalar.copy(c2[:, g, :, :], kvbank[:, g, :].rearrange("p (b j) -> p b j", b=B)).then_inc(s["c2_done"], 1)
                act.wait_ge(s["c3_ps"], 1)
                nc.scalar.copy(c3[:, :, :, :].rearrange("p c b j -> p (c b j)"), bank[0][0:64, :]).then_inc(s["c3_done"], 1)
                act.wait_ge(s["logit_done"], 1)
                nc.scalar.activation(lev[:, 2, :], lev[:, 1, :], ACT.Exp).then_inc(s["exp_done"], 1)
                nc.scalar.activation(asig[:, 1, :], asig[:, 0, :], ACT.Exp, scale=-1.0).then_inc(s["exp_done"], 1)
                act.wait_ge(c["xct_ps"], 1)
                nc.scalar.copy(xct0[:, :, :], bank[3][:, 0:KD * B].rearrange("p (k b) -> p k b", k=KD)).then_inc(c["xct"], 1)
                act.wait_ge(s["un3_ps"], 1)
                nc.scalar.copy(lh3[:, :, :, :].rearrange("p c b j -> p (c b j)"), bank[0][0:64, :]).then_inc(s["un3_done"], 1)
                for g in range(2):
                    act.wait_ge(s["un2_ps"], g + 1)
                    nc.scalar.mul(lh2[:, g, :, :].rearrange("p b j -> p (b j)"), kvbank[:, g, :], 0.25).then_inc(s["un2_done"], 1)
        tok.close()
        brev = sb("brev", [H1, 2 * ROWS], scope=attn0)
        scope = ExitStack()
        stat0 = sb("stat0", [P, NT, 6], scope=scope)
        mv0 = sb("mv0", [P, NT, 2], scope=scope)
        var0 = sb("var0", [P, NT], scope=scope)
        rstd0 = sb("rstd0", [P, NT], scope=scope)
        xn0 = [sb(f"xn0_{i}", [P, TPB, D], scope=scope) for i in range(2)]
        xt0 = [sb(f"xt0_{i}", [P, KD, ROWS], scope=scope) for i in range(2)]
        t1 = sb("t1", [P, KD, ROWS], scope=scope)
        t2 = sb("t2", [P, KD, ROWS], scope=scope)
        qt0 = [sb(f"qt0_{i}", [P, KD, ROWS], scope=scope) for i in range(2)]
        kvb = [sb(f"kvb_{i}", [P, TPB, 2 * D], scope=scope) for i in range(2)]
        kt1 = sb("kt1", [P, TPB, D], scope=scope)
        kt2 = sb("kt2", [P, TPB, D], scope=scope)
        kr = sb("kr", [P, TPB, D], scope=scope)
        vtkm = sb("vtkm", [P, KD, P], scope=scope)
        gs = sb("gs", [P, KD, D], scope=scope)
        xn1 = [sb(f"xn1_{i}", [P, TPB, D], scope=scope) for i in range(2)]
        zrow = sb("zrow", [P, 2, D], scope=scope)
        x1t = sb("x1t", [P, KD, ROWS], scope=scope)
        stat1 = sb("stat1", [P, TPB, 6], scope=scope)
        mv1 = sb("mv1", [P, TPB, 2], scope=scope)
        var1 = sb("var1", [P, TPB], scope=scope)
        rstd1 = sb("rstd1", [P, TPB], scope=scope)
        clsrow = sb("clsrow", [1, B, D], scope=scope)
        clsatt = sb("clsatt", [B, D], scope=scope)
        logits = sb("logits", [P, NTC, E], scope=scope)

        names = ("stat0 aggr0 var0 rstd0 swapped xc0 xct_ps xct qc_ps qc kvc_ps kvc xn_ready xt_ps xt_ready q_ps q_used "
                 "kv_ps kvb_ready kt1 kt2 qr_ready kr_ready vtk_ps vtk_ready g_ps g_ready out_ps hb_done h_done cls_copied "
                 "stat1 aggr1 var1 rstd1 xn1_ready x1t_ps x1t_ready lg_ps lg_done nh xrow_done cls_ps").split()
        s = {n: early_sem("a_" + n) for n in names}

        def per_image(eng, body):
            body(0, 0, True, False)
            with eng.Fori(0, B // 2 - 1) as pair:
                body(pair * 2 + 1, 1, False, False)
                body(pair * 2 + 2, 0, False, False)
            body(B - 1, (B - 1) % 2, False, True)

        def tiles(b):
            return bass.ds(b * TPB, TPB)

        with nc.Block() as block:
            @block.sync
            def _(sp):
                sp.dma_start(w1[:, :, :], dram["L0_ffn_W1"][0].rearrange("(k p) f -> p k f", p=P)).then_inc(w1_in, 16)
                sp.dma_start(w2[:, :, :], dram["L0_ffn_W2"][0].rearrange("(k p) d -> p k d", p=P)).then_inc(w2_in, 16)
                for src, dst in (("L1_attn_Wq", wq1), ("L1_attn_Wkv", wkv1), ("L1_attn_Wo", wo1)):
                    sp.dma_start(dst[:, :, :], dram[src].rearrange("(k p) n -> p k n", p=P)).then_inc(l1_in, 16)
                sp.dma_start(bo1[:, :], dram["L1_attn_bo"].partition_broadcast(P)).then_inc(l1_in, 16)
                sp.wait_ge(bias["brev"], 1)
                sp.dma_start(bias_rev, brev[:, :]).then_inc(bias["brev_out"], 16)
                sp.wait_ge(bias["brev_out"], 16)
                for t in range(TPB):
                    n, at = 1 + P * (t + 1), (1 + P) * t
                    rows = bass.AP(tensor=bias_rev.tensor, offset=ROWS - P * t - P, ap=[[1, P], [2 * ROWS, H1], [1, n]])
                    sp.dma_start(toeplitz[:, :, at:at + n], rows).then_inc(bias["rev_in"], 16)
                sp.wait_ge(s["nh"], 1)
                for c in range(0, buf.shape[0], 256):
                    n = min(256, buf.shape[0] - c)
                    sp.dma_start(buf[c:c + n, :], zrow[0:n // 2, :, :]).then_inc(buf_zeroed, 16)
                sp.wait_ge(buf_zeroed, 16 * -(-buf.shape[0] // 256))

            @block.gpsimd
            def _(pool):
                nc.gpsimd.memset(zrow[:, :, :], 0.0).then_inc(s["nh"], 1)
                nc.gpsimd.memset(logits[:, :, :], 0.0).then_inc(s["nh"], 1)

                def deviations0(n, t0, t1):
                    pool.wait_ge(s["aggr0"], t1)
                    nc.gpsimd.tensor_scalar(var0[:, t0:t1], mv0[:, t0:t1, 1], EPS, None, ALU.add).then_inc(s["var0"], 1)
                    pool.wait_ge(s["var0"], n)
                    nc.gpsimd.tensor_tensor(rstd0[:, t0:t1], var0[:, t0:t1], nh16[:, t0:t1], ALU.pow).then_inc(s["rstd0"], 1)

                deviations0(1, 0, TPB)
                deviations0(2, TPB, NT // 2)

                def turn_qk(b, slot, first):
                    pool.wait_ge(s["q_used"], b + 1)
                    if not first:
                        pool.wait_ge(s["out_ps"], b)
                    nc.gpsimd.tensor_tensor(qt0[slot][:, :, :], t1[:, :, :], t2[:, :, :], ALU.add).then_inc(s["qr_ready"], 1)
                    pool.wait_ge(s["kvb_ready"], b + 1)
                    if not first:
                        pool.wait_ge(s["kr_ready"], b)
                    nc.gpsimd.tensor_tensor(kt1[:, :, :], kvb[slot][:, :, 0:D], ropek[:, 0, :, :], ALU.mult).then_inc(s["kt1"], 1)
                    pool.wait_ge(s["kt1"], b + 1)
                    pool.wait_ge(s["kt2"], 2 * b + 2)
                    if not first:
                        pool.wait_ge(s["vtk_ps"], b + 1)
                    nc.gpsimd.tensor_tensor(kr[:, :, :], kt1[:, :, :], kt2[:, :, :], ALU.add).then_inc(s["kr_ready"], 1)

                def deviations(b):
                    waits_apart(pool, (s["aggr1"], 2 * b + 2))
                    nc.gpsimd.tensor_scalar(var1[:, :], mv1[:, :, 1], EPS, None, ALU.add).then_inc(s["var1"], 1)
                    pool.wait_ge(s["var1"], b + 1)
                    nc.gpsimd.tensor_tensor(rstd1[:, :], var1[:, :], nh16[:, 0:TPB], ALU.pow).then_inc(s["rstd1"], 1)

                def keep_rows(b, slot):
                    pool.wait_ge(s["xn1_ready"], b + 1)
                    nc.gpsimd.tensor_copy(xrow[:, tiles(b), :], xn1[slot][:, :, :]).then_inc(s["xrow_done"], 1)

                turn_qk(0, 0, True)
                deviations0(3, NT // 2, NT)

                def image(b, slot, first, last):
                    if not first:
                        deviations(b - 1)
                    pool.wait_ge(s["xn_ready"], b + 1)
                    nc.gpsimd.tensor_tensor(hrow[:, tiles(b), :], hrow[:, tiles(b), :], rep(bo0[:, :], 1, TPB), ALU.add).then_inc(s["hb_done"], 1)
                    if not last:
                        turn_qk(b + 1, 1 - slot, False)
                    if not first:
                        keep_rows(b - 1, 1 - slot)

                pool.sem_inc(s["xrow_done"], 1)
                per_image(pool, image)
                deviations(B - 1)
                keep_rows(B - 1, (B - 1) % 2)

            @block.vector
            def _(dve):
                dve.wait_ge(bias["emb_in"], 16 * 3)
                nc.vector.tensor_scalar(emb[0:BUCKETS, :], emb[0:BUCKETS, :], 64.0, None, ALU.mult).then_inc(bias["emb"], 1)

                def statistics(t0, t1):
                    for t in range(t0, t1):
                        nc.vector.bn_stats(stat0[:, t, :], hrow[:, t, :]).then_inc(s["stat0"], 1)
                    for t in range(t0, t1):
                        dve.wait_ge(s["stat0"], t + 1)
                        nc.vector.bn_aggr(mv0[:, t, :], stat0[:, t, :]).then_inc(s["aggr0"], 1)

                statistics(0, TPB)
                dve.wait_ge(bias["brev_ps"], 1)
                nc.vector.tensor_copy(brev[:, :], bank[1][0:H1, :]).then_inc(bias["brev"], 1)

                def norm0(b, slot):
                    for t in range(TPB):
                        at = bass.ds(b * TPB + t, 1)
                        ins = nc.vector.tensor_scalar(xn0[slot][:, t, :], hrow[:, at, :].rearrange("p o d -> p (o d)"),
                                                      mv0[:, at, 0:1].rearrange("p o d -> p (o d)"), rstd0[:, at], ALU.subtract, ALU.mult)
                    ins.then_inc(s["xn_ready"], 1)

                dve.wait_ge(s["rstd0"], 1)
                dve.wait_ge(s["aggr0"], TPB)
                norm0(0, 0)
                statistics(TPB, NT // 2)

                def rotate(b, slot, first):
                    dve.wait_ge(s["q_ps"], b + 1)
                    if not first:
                        dve.wait_ge(s["qr_ready"], b)
                    for m in range(KD):
                        cols = slice(ROWS * m, ROWS * m + ROWS)
                        nc.vector.scalar_tensor_tensor(t1[:, m, :], bank[1][:, cols], bqm[:, m:m + 1], ropeq[:, 0, m, :], ALU.add, ALU.mult)
                        ins = nc.vector.scalar_tensor_tensor(t2[:, m, :], bank[2][:, cols], bqs[:, m:m + 1], ropeq[:, 1, m, :], ALU.add, ALU.mult)
                    ins.then_inc(s["q_used"], 1)
                    dve.wait_ge(s["kv_ps"], b + 1)
                    if not first:
                        dve.wait_ge(s["vtk_ps"], b)
                        dve.wait_ge(s["kr_ready"], b)
                    nc.vector.tensor_tensor(kvb[slot][:, :, :], kvbank[:, :, :], rep(bkv[:, :], 1, TPB), ALU.add).then_inc(s["kvb_ready"], 1)
                    dve.wait_ge(s["kvb_ready"], b + 1)
                    nc.vector.tensor_tensor(kt2[:, :, 0::2], kvb[slot][:, :, 1:D:2], ropek[:, 1, :, 0::2], ALU.mult).then_inc(s["kt2"], 1)
                    nc.vector.tensor_tensor(kt2[:, :, 1::2], kvb[slot][:, :, 0:D:2], ropek[:, 1, :, 1::2], ALU.mult).then_inc(s["kt2"], 1)

                def residual(b, slot):
                    dve.wait_ge(s["out_ps"], b + 2)
                    dve.wait_ge(s["hb_done"], b + 1)
                    nc.vector.tensor_tensor(hrow[:, tiles(b), :], bank[5][:, :].rearrange("p (t d) -> p t d", t=TPB),
                                            hrow[:, tiles(b), :], ALU.add).then_inc(s["h_done"], 1)
                    waits_apart(dve, (s["h_done"], b + 1))
                    for t in range(TPB):
                        ins = nc.vector.bn_stats(stat1[:, t, :], hrow[:, bass.ds(b * TPB + t, 1), :].rearrange("p o d -> p (o d)"))
                    ins.then_inc(s["stat1"], 1)
                    waits_apart(dve, (s["stat1"], b + 1))
                    for t in range(TPB):
                        nc.vector.bn_aggr(mv1[:, t, :], stat1[:, t, :]).then_inc(s["aggr1"], 1)
                    dve.wait_ge(s["rstd1"], b + 1)
                    dve.wait_ge(s["x1t_ps"], b + 1)
                    dve.wait_ge(s["xrow_done"], b + 1)
                    dve.wait_ge(s["aggr1"], 2 * b + 2)
                    for t in range(TPB):
                        at = bass.ds(b * TPB + t, 1)
                        ins = nc.vector.tensor_scalar(xn1[slot][:, t, :], hrow[:, at, :].rearrange("p o d -> p (o d)"),
                                                      mv1[:, t, 0:1], rstd1[:, t:t + 1], ALU.subtract, ALU.mult)
                    ins.then_inc(s["xn1_ready"], 1)

                rotate(0, 0, True)
                statistics(NT // 2, NT)
                dve.wait_ge(s["rstd0"], 3)
                dve.wait_ge(s["aggr0"], NT)

                def image(b, slot, first, last):
                    if not last:
                        if not first:
                            dve.wait_ge(s["xt_ps"], b)
                        norm0(b + 1, 1 - slot)
                    dve.wait_ge(s["vtk_ps"], b + 2)
                    if not first:
                        dve.wait_ge(s["g_ps"], b)
                    nc.vector.tensor_tensor(vtkm[:, :, :], bank[3][:, 0:D].rearrange("p (g n) -> p g n", g=KD),
                                            mat("blocks").rearrange("p (g n) -> p g n", g=KD), ALU.mult).then_inc(s["vtk_ready"], 1)
                    if not first:
                        residual(b - 1, 1 - slot)
                    if not last:
                        rotate(b + 1, 1 - slot, False)

                per_image(dve, image)
                residual(B - 1, (B - 1) % 2)

            @block.scalar
            def _(act):
                def evac_xt(b, slot, early):
                    act.wait_ge(s["xt_ps"], b + 1)
                    if not early:
                        act.wait_ge(s["kv_ps"], b - 1)
                    nc.scalar.copy(xt0[slot][:, :, :], bank[0][:, :].rearrange("p (k n) -> p k n", k=KD)).then_inc(s["xt_ready"], 1)

                def evac_expert_rows(b):
                    act.wait_ge(s["x1t_ps"], b + 2)
                    nc.scalar.copy(x1t[:, :, :], bank[0][:, :].rearrange("p (k n) -> p k n", k=KD)).then_inc(s["x1t_ready"], 1)
                    act.wait_ge(s["lg_ps"], b + 1)
                    nc.scalar.copy(logits[:, tiles(b), :], bank[0][:, 0:TPB * E].rearrange("p (t e) -> p t e", t=TPB)).then_inc(s["lg_done"], 1)

                evac_xt(0, 0, True)
                act.wait_ge(s["nh"], 2)

                def image(b, slot, first, last):
                    if not last:
                        evac_xt(b + 1, 1 - slot, first)
                    act.wait_ge(s["g_ps"], b + 1)
                    if not first:
                        act.wait_ge(s["out_ps"], b + 1)
                    nc.scalar.copy(gs[:, :, :], bank[4][:, :].rearrange("p (g n) -> p g n", g=KD)).then_inc(s["g_ready"], 1)
                    if not first:
                        evac_expert_rows(b - 1)
                    act.wait_ge(s["cls_ps"], b + 1)
                    nc.scalar.copy(clsrow[0:1, bass.ds(b, 1), :].rearrange("p o d -> p (o d)"), bank[3][0:1, D:2 * D]).then_inc(s["cls_copied"], 1)

                per_image(act, image)
                evac_expert_rows(B - 1)

            @block.tensor
            def _(pe):
                pe.sem_inc(s["out_ps"], 1)
                pe.sem_inc(s["vtk_ps"], 1)
                pe.sem_inc(s["x1t_ps"], 1)
                pe.sem_inc(s["lg_done"], 1)
                pe.wait_ge(mats_in, 16)
                pe.wait_ge(l0_in, l0_all)
                pe.wait_ge(bias["emb"], 1)
                nc.tensor.matmul(bank[1][0:H1, :], emb[:, :], hot[:, :], start=True, stop=True).then_inc(bias["brev_ps"], 1)

                def turn(src, done):
                    for k in range(KD):
                        for t in range(TPB):
                            ins = nc.tensor.transpose(bank[0][:, ROWS * k + P * t:ROWS * k + P * t + P], src(t)[:, P * k:P * k + P], ident)
                    ins.then_inc(done, 1)

                def expert_rows_t(b, slot):
                    pe.wait_ge(s["xn1_ready"], b + 1)
                    for k in range(KD):
                        for t in range(TPB):
                            ins = nc.tensor.transpose(bank[0][:, ROWS * k + P * t:ROWS * k + P * t + P], xn1[slot][:, t, P * k:P * k + P], ident)
                    ins.then_inc(s["x1t_ps"], 1)

                def logits_of(b):
                    pe.wait_ge(s["x1t_ready"], b + 1)
                    for t in range(TPB):
                        for k in range(KD):
                            ins = nc.tensor.matmul(bank[0][:, E * t:E * t + E], x1t[:, k, P * t:P * t + P], wg[:, k, :], start=(k == 0), stop=(k == KD - 1))
                    ins.then_inc(s["lg_ps"], 1)

                pe.wait_ge(s["xn_ready"], 1)
                turn(lambda t: xn0[0][:, t, :], s["xt_ps"])
                pe.wait_ge(bias["brev"], 1)

                def project_q(b, slot):
                    pe.wait_ge(s["xt_ready"], b + 1)
                    for w, o in ((wq0, bank[1]), (wqs0, bank[2])):
                        for m in range(KD):
                            for k in range(KD):
                                ins = nc.tensor.matmul(o[:, ROWS * m:ROWS * m + ROWS], w[:, k, P * m:P * m + P], xt0[slot][:, k, :],
                                                       start=(k == 0), stop=(k == KD - 1))
                    ins.then_inc(s["q_ps"], 1)

                def project_kv(b, slot):
                    for t in range(TPB):
                        for k in range(KD):
                            ins = nc.tensor.matmul(kvbank[:, t, :], xt0[slot][:, k, P * t:P * t + P], wkv0[:, k, :], start=(k == 0), stop=(k == KD - 1))
                    ins.then_inc(s["kv_ps"], 1)

                project_q(0, 0)
                project_kv(0, 0)

                def image(b, slot, first, last):
                    pe.wait_ge(s["kr_ready"], b + 1)
                    if not first:
                        pe.wait_ge(s["vtk_ready"], b)
                        pe.wait_ge(s["cls_copied"], b)
                    for g in range(KD):
                        for t in range(TPB):
                            nc.tensor.matmul(bank[3][:, P * g:P * g + P], kvb[slot][:, t, D + P * g:D + P * g + P], kr[:, t, P * g:P * g + P],
                                             start=(t == 0), stop=False)
                        ins = nc.tensor.matmul(bank[3][:, P * g:P * g + P], kvc[0:1, D + P * g:D + P * g + P], kvc[0:1, P * g:P * g + P],
                                               start=False, stop=True)
                    ins.then_inc(s["vtk_ps"], 1)
                    if not first:
                        pe.wait_ge(s["lg_done"], b)
                    if not last:
                        pe.wait_ge(s["xn_ready"], b + 2)
                        turn(lambda t: xn0[1 - slot][:, t, :], s["xt_ps"])
                    pe.wait_ge(s["vtk_ready"], b + 1)
                    if not first:
                        pe.wait_ge(s["g_ready"], b)
                    for g in range(KD):
                        ins = nc.tensor.matmul(bank[4][:, D * g:D * g + D], vtkm[:, g, :], wo0[:, g, :], start=True, stop=True)
                    ins.then_inc(s["g_ps"], 1)
                    if not last:
                        pe.wait_ge(s["q_used"], b + 1)
                        project_q(b + 1, 1 - slot)
                    if not first:
                        expert_rows_t(b - 1, 1 - slot)
                    if not last:
                        pe.wait_ge(s["kvb_ready"], b + 1)
                        project_kv(b + 1, 1 - slot)
                    if not first:
                        logits_of(b - 1)
                    pe.wait_ge(s["g_ready"], b + 1)
                    pe.wait_ge(s["qr_ready"], b + 1)
                    if not first:
                        pe.wait_ge(s["h_done"], b)
                    for g in range(KD):
                        ins = nc.tensor.matmul(bank[3][0:1, D:2 * D], qc0[:, g, 0:1], gs[:, g, :], start=(g == 0), stop=(g == KD - 1))
                    ins.then_inc(s["cls_ps"], 1)
                    for t in range(TPB):
                        for g in range(KD):
                            ins = nc.tensor.matmul(bank[5][:, D * t:D * t + D], qt0[slot][:, g, P * t:P * t + P], gs[:, g, :],
                                                   start=(g == 0), stop=(g == KD - 1))
                    ins.then_inc(s["out_ps"], 1)

                per_image(pe, image)
                pe.wait_ge(s["lg_done"], B)
                expert_rows_t(B - 1, (B - 1) % 2)
                logits_of(B - 1)

        names = ("cls_in hcb hcls stat aggr var rstd xcls xct_ps xct lg_ps lg mx cw_d cw_e best_d oh_w best oh cls_m rank_ps "
                 "rk_zero rk step idx scattered").split()
        s = {n: early_sem("r_" + n) for n in names}
        hcb = sb("hcb", [B, D], scope=scope)
        x1ct = sb("x1ct", [P, KD, B], scope=scope)
        route = sb("route", [P, 6, NTC], scope=scope)
        oh = sb("oh", [P, NTC, E], scope=scope)
        wt = sb("wt", [P, NTC, E], scope=scope)
        wt2 = sb("wt2", [P, NTC, E], scope=scope)
        rk = sb("rk", [P, NTC, E], scope=scope)
        ohcm = sb("ohcm", [B, NT, E], scope=scope)
        with nc.Block() as block:
            @block.sync
            def _(sp):
                for b in range(B):
                    sp.dma_start(clsatt[b:b + 1, :], clsrow[0:1, b, :]).then_inc(s["cls_in"], 16)
                sp.wait_ge(s["cls_in"], 16 * B)

            @block.gpsimd
            def _(pool):
                nc.gpsimd.tensor_tensor(hcb[:, :], clsb[:, :], bo0[0:B, :], ALU.add).then_inc(s["hcb"], 1)
                pool.wait_ge(s["aggr"], 1)
                nc.gpsimd.tensor_scalar(varc[:, :], mvc[:, 1:2], EPS, None, ALU.add).then_inc(s["var"], 1)
                pool.wait_ge(s["var"], 1)
                nc.gpsimd.tensor_tensor(rstdc[:, :], varc[:, :], nh16[0:B, 0:1], ALU.pow).then_inc(s["rstd"], 1)
                pool.wait_ge(s["idx"], 1)
                for t in range(NT):
                    nc.gpsimd.indirect_dma_start(buf[0:SLOTS, :], bass.IndirectOffsetOnAxis(to_slot[:, t:t + 1], 0), xrow[:, t, :], None,
                                                 bounds_check=SLOTS - 1, oob_is_err=False).then_inc(s["scattered"], 16)
                nc.gpsimd.indirect_dma_start(buf[0:SLOTS, :], bass.IndirectOffsetOnAxis(to_slot[0:B, NT:NTC], 0), xcls[:, :], None,
                                             bounds_check=SLOTS - 1, oob_is_err=False).then_inc(s["scattered"], 16)
                pool.wait_ge(s["scattered"], 16 * NTC)

            @block.vector
            def _(dve):
                dve.wait_ge(s["cls_in"], 16 * B)
                dve.wait_ge(s["hcb"], 1)
                nc.vector.tensor_tensor(hcls[:, :], clsatt[:, :], hcb[:, :], ALU.add).then_inc(s["hcls"], 1)
                dve.wait_ge(s["hcls"], 1)
                nc.vector.bn_stats(statc[:, :], hcls[:, :]).then_inc(s["stat"], 1)
                dve.wait_ge(s["stat"], 1)
                nc.vector.bn_aggr(mvc[:, :], statc[:, :]).then_inc(s["aggr"], 1)
                nc.vector.memset(rk[:, :, :], 0.0).then_inc(s["rk_zero"], 1)
                dve.wait_ge(s["rstd"], 1)
                dve.wait_ge(s["aggr"], 1)
                nc.vector.tensor_scalar(xcls[:, :], hcls[:, :], mvc[:, 0:1], rstdc[:, 0:1], ALU.subtract, ALU.mult).then_inc(s["xcls"], 1)
                dve.wait_ge(s["lg"], 1)
                lg = logits[:, :, :]
                mx, total, prob, rank, slot, valid = (route[:, i, :] for i in range(6))
                nc.vector.tensor_reduce(mx, lg, AX.X, ALU.max).then_inc(s["mx"], 1)
                dve.wait_ge(s["mx"], 1)
                nc.vector.tensor_tensor(wt[:, :, :], lg, rep(mx, 2, E), ALU.subtract).then_inc(s["cw_d"], 1)
                nc.vector.tensor_tensor(oh[:, :, :], lg, rep(mx, 2, E), ALU.is_equal).then_inc(s["best_d"], 1)
                dve.wait_ge(s["best_d"], 1)
                nc.vector.tensor_tensor(wt2[:, :, :], oh[:, :, :], mat("order").rearrange("p (t e) -> p t e", e=E), ALU.mult).then_inc(s["oh_w"], 1)
                dve.wait_ge(s["oh_w"], 1)
                nc.vector.tensor_reduce(rank, wt2[:, :, :], AX.X, ALU.max).then_inc(s["best"], 1)
                dve.wait_ge(s["best"], 1)
                nc.vector.tensor_tensor(oh[:, :, :], wt2[:, :, :], rep(rank, 2, E), ALU.is_equal).then_inc(s["oh"], 1)
                dve.wait_ge(s["oh"], 1)
                nc.vector.tensor_tensor(ohcm[:, :, :], rep(oh[0:B, NT, :], 1, NT), mat("before", B).rearrange("p (t e) -> p t e", e=E), ALU.mult).then_inc(s["cls_m"], 1)
                dve.wait_ge(s["cw_e"], 1)
                nc.vector.tensor_reduce(total, wt[:, :, :], AX.X, ALU.add).then_inc(s["step"], 1)
                dve.wait_ge(s["step"], 1)
                nc.vector.reciprocal(prob, total).then_inc(s["step"], 1)
                dve.wait_ge(s["rank_ps"], 2)
                dve.wait_ge(s["rk_zero"], 1)
                nc.vector.tensor_copy(rk[:, 0:NT, :], bank[2][:, 0:NT * E].rearrange("p (t e) -> p t e", e=E)).then_inc(s["rk"], 1)
                nc.vector.tensor_copy(rk[0:B, NT, :], bank[3][0:B, 0:E]).then_inc(s["rk"], 1)
                dve.wait_ge(s["rk"], 2)
                nc.vector.tensor_tensor(wt2[:, :, :], rk[:, :, :], oh[:, :, :], ALU.mult).then_inc(s["step"], 1)
                nc.vector.tensor_tensor(rk[:, :, :], rk[:, :, :], mat("first_slot").rearrange("p (t e) -> p t e", e=E), ALU.add).then_inc(s["step"], 1)
                dve.wait_ge(s["step"], 4)
                nc.vector.tensor_reduce(rank, wt2[:, :, :], AX.X, ALU.add).then_inc(s["step"], 1)
                nc.vector.tensor_tensor(rk[:, :, :], rk[:, :, :], oh[:, :, :], ALU.mult).then_inc(s["step"], 1)
                dve.wait_ge(s["step"], 6)
                nc.vector.tensor_reduce(slot, rk[:, :, :], AX.X, ALU.add).then_inc(s["step"], 1)
                nc.vector.tensor_scalar(valid, rank, float(CAP), None, ALU.is_le).then_inc(s["step"], 1)
                dve.wait_ge(s["step"], 8)
                nc.vector.tensor_scalar(mx, valid, -float(FAR), float(FAR), ALU.mult, ALU.add).then_inc(s["step"], 1)
                dve.wait_ge(s["step"], 9)
                nc.vector.tensor_tensor(total, mx, slot, ALU.add).then_inc(s["step"], 1)
                dve.wait_ge(s["step"], 10)
                nc.vector.tensor_scalar(to_slot[:, :], total, 0.0, None, ALU.max).then_inc(s["idx"], 1)
                by_tile = lambda a: a[:, 0:NT].rearrange("p (b r) -> p r b", r=TPB)
                nc.vector.tensor_scalar(back_pairs[:, :, 0, :].bitcast(U32), by_tile(slot), float(SLOTS - 1), 0.0, ALU.min, ALU.max).then_inc(s["idx"], 1)
                nc.vector.tensor_tensor(back_pairs[:, :, 1, :], by_tile(prob), by_tile(valid), ALU.mult).then_inc(s["idx"], 1)
                nc.vector.tensor_scalar(back_cls[:, 0:1].bitcast(U32), slot[0:B, NT:NTC], float(SLOTS - 1), 0.0, ALU.min, ALU.max).then_inc(s["idx"], 1)
                nc.vector.tensor_tensor(back_cls[:, 1:2], prob[0:B, NT:NTC], valid[0:B, NT:NTC], ALU.mult).then_inc(s["idx"], 1)
                dve.wait_ge(w1_high, 1)
                low_part(nc.vector, w1[:, :, :], w1h[0][:, :, :], w1l[0][:, :, :]).then_inc(w1_low, 1)
                dve.wait_ge(w2_high, 1)
                low_part(nc.vector, w2[:, :, :], w2h[0][:, :, :], w2l[0][:, :, :]).then_inc(w2_low, 1)

            @block.scalar
            def _(act):
                for h in range(H1):
                    act.wait_ge(bias["flip_ps"], h + 1)
                    nc.scalar.copy(toeplitz[:, h, :], bank[4 + h % 2][:, 0:SCOLS]).then_inc(bias["flip_out"], 1)
                act.wait_ge(s["xct_ps"], 1)
                nc.scalar.copy(x1ct[:, :, :], bank[0][:, 0:KD * B].rearrange("p (k b) -> p k b", k=KD)).then_inc(s["xct"], 1)
                act.wait_ge(s["lg_ps"], 1)
                nc.scalar.copy(logits[0:B, NT, :], bank[1][0:B, 0:E]).then_inc(s["lg"], 1)
                act.wait_ge(s["cw_d"], 1)
                nc.scalar.activation(wt[:, :, :], wt[:, :, :], ACT.Exp).then_inc(s["cw_e"], 1)
                act.wait_ge(w1_in, 16)
                high(nc.scalar, w1[:, :, :], w1h[0][:, :, :]).then_inc(w1_high, 1)
                act.wait_ge(w2_in, 16)
                high(nc.scalar, w2[:, :, :], w2h[0][:, :, :]).then_inc(w2_high, 1)

            @block.tensor
            def _(pe):
                pe.wait_ge(bias["rev_in"], 16 * TPB)
                for h in range(H1):
                    if h >= 2:
                        pe.wait_ge(bias["flip_out"], h - 1)
                    nc.tensor.matmul(bank[4 + h % 2][:, 0:SCOLS], mat("flip"), toeplitz[:, h, :], start=True, stop=True).then_inc(bias["flip_ps"], 1)
                pe.wait_ge(s["xcls"], 1)
                for k in range(KD):
                    ins = nc.tensor.transpose(bank[0][:, B * k:B * k + B], xcls[:, P * k:P * k + P], mat("ident", B)[:, 0:B])
                ins.then_inc(s["xct_ps"], 1)
                pe.wait_ge(s["xct"], 1)
                for k in range(KD):
                    ins = nc.tensor.matmul(bank[1][0:B, 0:E], x1ct[:, k, :], wg[:, k, :], start=(k == 0), stop=(k == KD - 1))
                ins.then_inc(s["lg_ps"], 1)
                pe.wait_ge(s["cls_m"], 1)
                ranks = bank[2][:, 0:NT * E]
                nc.tensor.matmul(ranks, mat("tri"), oh[:, 0:NT, :], start=True, stop=False)
                of_pair = ranks.rearrange("p (b r e) -> p b r e", r=2, e=E)
                nc.tensor.matmul(of_pair[:, :, 1, :], mat("tri"), oh[:, 0:NT:2, :], start=False, stop=False)
                nc.tensor.matmul(of_pair[:, :, 0, :], mat("above"), oh[:, 1:NT:2, :], start=False, stop=False)
                for t in range(NT - TPB):
                    done = t // TPB * TPB + TPB
                    nc.tensor.matmul(bank[2][:, E * done:E * NT], ones, rep(oh[:, t, :], 1, NT - done), start=False, stop=False)
                nc.tensor.matmul(ranks, mat("ones", B), ohcm[:, :, :], start=False, stop=True).then_inc(s["rank_ps"], 1)
                nc.tensor.matmul(bank[3][0:B, 0:E], mat("tri8", B), oh[0:B, NT, :], start=True, stop=False)
                after = mat("after").rearrange("p (j b) -> p j b", b=B)
                for t in range(NT):
                    ins = nc.tensor.matmul(bank[3][0:B, 0:E], after[:, t // TPB, :], oh[:, t, :], start=False, stop=(t == NT - 1))
                ins.then_inc(s["rank_ps"], 1)
        scope.close()
        attn0.close()
        nc.clear_and_free_semaphores(early)
        nc.all_engine_barrier()
        hpairs, hrow = hrow, xrow
        yrow = hpairs
        in_order = sem("in_order")
        scope = ExitStack()
        b1rows = sb("b1rows", [E * KF, P], scope=scope)
        b1t = sb("b1t", [P, E * KF], scope=scope)
        b2b = sb("b2b", [P, E, D], scope=scope)
        xe = [sb(f"xe_{i}", [MR, MT, D], scope=scope) for i in range(2)]
        w1h.append(sb("w1h1", [P, KD, F], F32R, scope=scope))
        w1l.append(sb("w1l1", [P, KD, F], F32R, scope=scope))
        w2h.append(sb("w2h1", [P, KF, D], F32R, scope=scope))
        w2l.append(sb("w2l1", [P, KF, D], F32R, scope=scope))
        xeh = sb("xeh", [P, KD, MT * MR], F32R, scope=scope)
        xel = sb("xel", [P, KD, MT * MR], F32R, scope=scope)
        RING = 4
        hraw = sb("hraw", [P, RING, MT * MR], scope=scope)
        hth = sb("hth", [P, KF, MT * MR], F32R, scope=scope)
        htl = sb("htl", [P, KF, MT * MR], F32R, scope=scope)
        ys = [sb(f"ys_{i}", [MR, MT, D], scope=scope) for i in range(2)]
        names = "b_in b1_ps b1t xet_ps xeh xel h_ps gelu hth htl y_ps y_ready".split()
        s = {n: sem("e_" + n) for n in names}
        xe_in = [sem(f"xe_in{i}") for i in range(2)]
        y_out = [sem(f"y_out{i}") for i in range(2)]
        last_rows = CAP - (MT - 1) * MR
        spare = [(w1h[0], w2h[0]), (w1l[0], w2l[0])]
        wq = [a[:, :, 0:INNER] for a, _ in spare]
        wo = [a[:, :, INNER:2 * INNER] for a, _ in spare]
        wkv = [a[:, :, :].rearrange("p (k a) d -> p k (a d)", k=KD) for _, a in spare]
        attn1_weights = [(wkv1[:, :, :], wkv), (wq1[:, :, :], wq), (wo1[:, :, :].rearrange("p (k a) d -> p k (a d)", k=KD), wo)]
        l1_high, l1_low = sem("l1_high"), sem("l1_low")

        def per_expert(eng, body):
            body(0, 0, 1, True, False)
            with eng.Fori(0, E // 2 - 1) as pair:
                body(pair * 2 + 1, 1, pair + 1, False, False)
                body(pair * 2 + 2, 0, pair + 2, False, False)
            body(E - 1, (E - 1) % 2, E // 2, False, True)

        with nc.Block() as block:
            @block.sync
            def _(sp):
                def load_rows(e, slot):
                    sp.dma_start(xe[slot][:, :, :], buf[bass.ds(e * CAP, MT * MR), :].rearrange("(t p) d -> p t d", p=MR)).then_inc(xe_in[slot], 16)

                load_rows(0, 0)
                sp.dma_start(b1rows[:, :], dram["L0_ffn_b1"].rearrange("e (m p) -> (e m) p", p=P)).then_inc(s["b_in"], 16)
                sp.dma_start(b2b[:, :, :], dram["L0_ffn_b2"].partition_broadcast(P)).then_inc(s["b_in"], 16)

                def rows_in_order():
                    with nc.allow_non_contiguous_dma(reason="a row is a kilobyte"):
                        for t in range(TPB):
                            for r in range(2):
                                some = slice(P // 2 * t, P // 2 * t + P // 2)
                                sp.dma_start(hrow[r:P:2, t:NT:TPB, :], hpairs[some, r:NT:TPB, :]).then_inc(in_order, 16)
                                sp.dma_start(back[r:P:2, t, :, :], back_pairs[some, r, :, :]).then_inc(in_order, 16)

                def expert(e, slot, use, first, last):
                    if not last:
                        if not first:
                            sp.wait_ge(s["xet_ps"], e)
                        load_rows(e + 1, 1 - slot)
                        for n, w, w_in, w_low in (("L0_ffn_W1", w1, w1_in, w1_low), ("L0_ffn_W2", w2, w2_in, w2_low)):
                            sp.wait_ge(w_low, e + 1)
                            row = dram[n][bass.ds(e + 1, 1)].rearrange("o (k p) n -> p (o k) n", p=P)
                            sp.dma_start(w[:, :, :], row).then_inc(w_in, 16)
                    if first:
                        rows_in_order()
                    if last:
                        sp.wait_ge(w1_low, E)
                        sp.dma_start(w1[:, :, :], dram["L1_ffn_w1"].rearrange("(k p) f -> p k f", p=P)).then_inc(w1_in, 16)
                        sp.wait_ge(w2_low, E)
                        sp.dma_start(w2[:, :, :], dram["L1_ffn_w2"].rearrange("(k p) d -> p k d", p=P)).then_inc(w2_in, 16)
                    sp.wait_ge(s["y_ready"], 2 * e + 2)
                    whole = (MT - 1) * MR
                    sp.dma_start(ybuf[bass.ds(e * CAP, whole), :].rearrange("(t p) d -> p t d", p=MR), ys[slot][:, 0:MT - 1, :]).then_inc(y_out[slot], 16)
                    sp.dma_start(ybuf[bass.ds(e * CAP + whole, last_rows), :], ys[slot][0:last_rows, MT - 1, :]).then_inc(y_out[slot], 16)

                per_expert(sp, expert)
                for slot in range(2):
                    sp.wait_ge(y_out[slot], 32 * (E // 2 + 1))
                sp.wait_ge(in_order, 16 * 4 * TPB)

            @block.gpsimd
            def _(pool):
                def expert(e, slot, use, first, last):
                    if not last:
                        for w, wh, wl, w_high, w_low in ((w1, w1h, w1l, w1_high, w1_low), (w2, w2h, w2l, w2_high, w2_low)):
                            pool.wait_ge(w_high, e + 2)
                            low_part(nc.gpsimd, w[:, :, :], wh[1 - slot][:, :, :], wl[1 - slot][:, :, :]).then_inc(w_low, 1)
                    else:
                        w, parts = attn1_weights[0]
                        pool.wait_ge(l1_high, 1)
                        low_part(nc.gpsimd, w, parts[0], parts[1]).then_inc(l1_low, 1)

                per_expert(pool, expert)

            @block.vector
            def _(dve):
                for slot in range(2):
                    dve.sem_inc(y_out[slot], 32)
                dve.wait_ge(s["b1_ps"], 1)
                nc.vector.tensor_copy(b1t[:, :], bank[5][:, 0:E * KF]).then_inc(s["b1t"], 1)
                dve.wait_ge(s["b_in"], 32)

                def rows_low(e):
                    dve.wait_ge(s["xeh"], e + 1)
                    for k in range(KD):
                        ins = low_part(nc.vector, bank[k][:, 0:MT * MR], xeh[:, k, :], xel[:, k, :])
                    ins.then_inc(s["xel"], 1)

                rows_low(0)

                def expert(e, slot, use, first, last):
                    for m in range(KF + 1):
                        if m < KF:
                            dve.wait_ge(s["gelu"], e * KF + m + 1)
                            high(nc.vector, hraw[:, m % RING, :], hth[:, m, :]).then_inc(s["hth"], 1)
                        if m:
                            dve.wait_ge(s["hth"], e * KF + m)
                            low_part(nc.vector, hraw[:, (m - 1) % RING, :], hth[:, m - 1, :], htl[:, m - 1, :]).then_inc(s["htl"], 1)
                    if not last:
                        rows_low(e + 1)
                    else:
                        for i in (1, 2):
                            w, parts = attn1_weights[i]
                            dve.wait_ge(l1_high, i + 1)
                            low_part(nc.vector, w, parts[0], parts[1]).then_inc(l1_low, 1)
                    dve.wait_ge(s["y_ps"], e + 1)
                    dve.wait_ge(y_out[slot], use * 32)
                    bias = b2b[0:MR, bass.ds(e, 1), :]
                    nc.vector.tensor_tensor(ys[slot][:, 0:2, :], bank[3][0:MR, :].rearrange("p (t d) -> p t d", t=2),
                                            rep(bias.rearrange("p o d -> p (o d)"), 1, 2), ALU.add).then_inc(s["y_ready"], 1)
                    nc.vector.tensor_tensor(ys[slot][:, 2, :], bank[4][0:MR, 0:D], bias.rearrange("p o d -> p (o d)"), ALU.add).then_inc(s["y_ready"], 1)

                per_expert(dve, expert)

            @block.scalar
            def _(act):
                def rows_high(e):
                    act.wait_ge(s["xet_ps"], e + 1)
                    for k in range(KD):
                        ins = high(nc.scalar, bank[k][:, 0:MT * MR], xeh[:, k, :])
                    ins.then_inc(s["xeh"], 1)

                rows_high(0)
                act.wait_ge(s["b1t"], 1)

                def expert(e, slot, use, first, last):
                    for m in range(KF):
                        act.wait_ge(s["h_ps"], e * KF + m + 1)
                        if not (first and m < RING):
                            act.wait_ge(s["htl"], e * KF + m + 1 - RING)
                        nc.scalar.activation(hraw[:, m % RING, :], kvbank[:, m % 2, 0:MT * MR], ACT.Gelu, bias=b1t[:, bass.ds(e * KF + m, 1)]).then_inc(s["gelu"], 1)
                    if not last:
                        rows_high(e + 1)
                        for w, wh, w_in, w_high in ((w1, w1h, w1_in, w1_high), (w2, w2h, w2_in, w2_high)):
                            act.wait_ge(w_in, 16 * e + 32)
                            high(nc.scalar, w[:, :, :], wh[1 - slot][:, :, :]).then_inc(w_high, 1)
                    else:
                        act.wait_ge(l1_in, 16 * 4)
                        act.wait_ge(s["y_ps"], E - 1)
                        for w, parts in attn1_weights:
                            high(nc.scalar, w, parts[0]).then_inc(l1_high, 1)

                per_expert(act, expert)

            @block.tensor
            def _(pe):
                def turn_rows(e, slot, use):
                    pe.wait_ge(xe_in[slot], use * 16)
                    for k in range(KD):
                        for t in range(MT):
                            ins = nc.tensor.transpose(bank[k][:, MR * t:MR * t + MR], xe[slot][:, t, P * k:P * k + P], mat("ident", MR)[:, 0:MR])
                    ins.then_inc(s["xet_ps"], 1)

                pe.wait_ge(s["b_in"], 32)
                nc.tensor.transpose(bank[5][:, 0:E * KF], b1rows[:, :], mat("ident", E * KF)[:, 0:E * KF]).then_inc(s["b1_ps"], 1)
                turn_rows(0, 0, 1)

                def expert(e, slot, use, first, last):
                    pe.wait_ge(w1_low, e + 1)
                    pe.wait_ge(s["xel"], e + 1)
                    for m in range(KF):
                        if not (first and m < 2):
                            pe.wait_ge(s["gelu"], e * KF + m - 1)
                        for k in range(KD):
                            cols = slice(P * m, P * m + P)
                            ins = product(kvbank[:, m % 2, 0:MT * MR], (w1h[slot][:, k, cols], w1l[slot][:, k, cols]), (xeh[:, k, :], xel[:, k, :]),
                                          k == 0, k == KD - 1)
                        ins.then_inc(s["h_ps"], 1)
                    if not last:
                        turn_rows(e + 1, 1 - slot, use + slot)
                    pe.wait_ge(w2_low, e + 1)
                    if not first:
                        pe.wait_ge(s["y_ready"], 2 * e)
                    for t in range(MT):
                        o = bank[3][0:MR, D * t:D * t + D] if t < 2 else bank[4][0:MR, 0:D]
                        rows = slice(MR * t, MR * t + MR)
                        for m in range(KF):
                            if t == 0:
                                pe.wait_ge(s["htl"], e * KF + m + 1)
                            ins = product(o, (hth[:, m, rows], htl[:, m, rows]), (w2h[slot][:, m, :], w2l[slot][:, m, :]), m == 0, m == KF - 1)
                    ins.then_inc(s["y_ps"], 1)

                per_expert(pe, expert)
        scope.close()

        NP = B // 2
        TP = 2 * TPB
        W = TP * P
        b1q = sb("b1q", [P, KF])
        b1r = sb("b1r", [KF, P])
        b2q = sb("b2q", [P, D])
        stat3 = sb("stat3", [P, TP, 6])
        mv3 = sb("mv3", [P, TP, 2])
        var3 = sb("var3", [P, TP])
        rstd3 = sb("rstd3", [P, TP])
        nh3 = sb("nh3", [P, TP])
        statc3 = sb("statc3", [B, 6])
        mvc3 = sb("mvc3", [B, 2])
        varc3 = sb("varc3", [B, 1])
        rstdc3 = sb("rstdc3", [B, 1])
        xc3 = sb("xc3", [B, D])
        x3ch = sb("x3ch", [P, KD, B], F32R)
        x3cl = sb("x3cl", [P, KD, B], F32R)
        shift = sb("shift", [P, 2])
        xn3 = wq1[:, :, :].rearrange("p k n -> p (k n)").rearrange("p (t d) -> p t d", t=TP)
        x3h, x3l = [wq[0]], [wq[1]]
        up_w = [a[:, :, :].rearrange("p (k a) d -> p k (a d)", k=KD) for a in (w2h[0], w2l[0])]
        f = {n: sem("f_" + n) for n in ("w_in b1_ps b1 shift stat aggr var rstd xn x_ps xh xl h_ps hq knot gl frac rise y0 y1 y z_ps z zr h_out "
                                        "statc aggrc varc rstdc xc xc_ps xch xcl w_high w_low zc_ps zc hc_ps").split()}
        STEP = 0.25

        def statistics3(dve, p):
            for t in range(TP):
                nc.vector.bn_stats(stat3[:, t, :], hrow[:, TP * p + t, :]).then_inc(f["stat"], 1)
            for t in range(TP):
                dve.wait_ge(f["stat"], TP * p + t + 1)
                nc.vector.bn_aggr(mv3[:, t, :], stat3[:, t, :]).then_inc(f["aggr"], 1)

        def deviations3(pool, p):
            pool.wait_ge(f["aggr"], TP * p + TP)
            nc.gpsimd.tensor_scalar(var3[:, :], mv3[:, :, 1], EPS, None, ALU.add).then_inc(f["var"], 1)
            pool.wait_ge(f["var"], p + 1)
            nc.gpsimd.tensor_tensor(rstd3[:, :], var3[:, :], nh3[:, :], ALU.pow).then_inc(f["rstd"], 1)

        def normalise3(dve, p):
            dve.wait_ge(f["rstd"], p + 1)
            dve.wait_ge(f["aggr"], TP * p + TP)
            if p:
                dve.wait_ge(f["x_ps"], p)
            for t in range(TP):
                ins = nc.vector.tensor_scalar(xn3[:, t, :], hrow[:, TP * p + t, :], mv3[:, t, 0:1], rstd3[:, t:t + 1], ALU.subtract, ALU.mult)
            ins.then_inc(f["xn"], 1)

        def turned3(p, k):
            return bank[k][:, :] if p else kvbank[:, k, :]

        def turn_rows3(pe, p):
            pe.wait_ge(f["xn"], p + 1)
            if p:
                pe.wait_ge(f["xl"], p)
            for k in range(KD):
                for t in range(TP):
                    ins = nc.tensor.transpose(turned3(p, k)[:, P * t:P * t + P], xn3[:, t, P * k:P * k + P], ident)
            ins.then_inc(f["x_ps"], 1)

        def rows_high3(act, p):
            act.wait_ge(f["x_ps"], p + 1)
            for k in range(KD):
                ins = high(nc.scalar, turned3(p, k), x3h[p % 2][:, k, :])
            ins.then_inc(f["xh"], 1)

        def rows_low3(dve, p):
            dve.wait_ge(f["xh"], p + 1)
            for k in range(KD):
                ins = low_part(nc.vector, turned3(p, k), x3h[p % 2][:, k, :], x3l[p % 2][:, k, :])
            ins.then_inc(f["xl"], 1)

        gath = [sem(f"gathered{t}") for t in range(NTC)]
        scope = ExitStack()
        stat2 = sb("stat2", [P, NTC, 6], scope=scope)
        mv2 = sb("mv2", [P, NT, 2], scope=scope)
        var2 = sb("var2", [P, NT], scope=scope)
        rstd2 = sb("rstd2", [P, NT], scope=scope)
        nh2 = sb("nh2", [P, NT], scope=scope)
        mvc2 = sb("mvc2", [B, 2], scope=scope)
        varc2 = sb("varc2", [B, 1], scope=scope)
        rstdc2 = sb("rstdc2", [B, 1], scope=scope)
        xc2 = sb("xc2", [B, D], scope=scope)
        x2cth = sb("x2cth", [P, KD, B], F32R, scope=scope)
        x2ctl = sb("x2ctl", [P, KD, B], F32R, scope=scope)
        oc = sb("oc", [B, INNER], scope=scope)
        och = sb("och", [B, INNER], F32R, scope=scope)
        ocl = sb("ocl", [B, INNER], F32R, scope=scope)
        oct_ = sb("oct", [P, KI, B], scope=scope)
        hcb2 = sb("hcb2", [B, D], scope=scope)
        g = {n: sem("g_" + n) for n in "h2 h2c stat statc aggr aggrc var rstd nh xc xct_ps xct xctl oc_ps oc och ocl oct_ps oct oo_ps hcb hcls".split()}
        xn2 = [sb(f"xn2_{i}", [P, TPB, D], scope=scope) for i in range(2)]
        x2h = [sb(f"x2h_{i}", [P, KD, EVEN], F32R, scope=scope) for i in range(2)]
        x2l = [sb(f"x2l_{i}", [P, KD, EVEN], F32R, scope=scope) for i in range(2)]
        qk = [sb(f"qk_{i}", [P, 2 * KI, POS], scope=scope) for i in range(2)]
        vrow = [sb(f"vrow_{i}", [P, TPB, INNER], scope=scope) for i in range(2)]
        vcls = [sb(f"vcls_{i}", [P, INNER], scope=scope) for i in range(2)]
        sx = [sb(f"sx_{i}", [P, SCOLS], scope=scope) for i in range(2)]
        low = sb("low", [P, 2, TPB], scope=scope)
        prob = sb("prob", [P, H1, SCOLS], scope=scope)
        total = [sb(f"total_{i}", [P, TPB, H1], scope=scope) for i in range(2)]
        inv = sb("inv", [P, TPB, H1], scope=scope)
        pt = [sb(f"pt_{i}", [P, 3 * P], scope=scope) for i in range(2)]
        osb = sb("osb", [P, TPB, INNER], scope=scope)
        oth = sb("oth", [P, KI, ROWS], F32R, scope=scope)
        otl = sb("otl", [P, KI, ROWS], F32R, scope=scope)
        pick = [sb(f"pick_{i}", [B, P], F32R, scope=scope) for i in range(2)]
        names = ("xn2 x2t_ps x2h x2l x2c pick qk_ps even_out odd_out vc_ps vc s_ps smax p_done pt_ps pt pv inv o_tmp o_add o_fin "
                 "ot_ps oth ot wo_ps hb h_done").split()
        s = {n: sem("b_" + n) for n in names}
        UNITS = 2 * KI + TPB
        HALF = UNITS // 2
        tile_at = (0, 1 + P)

        def both(parts, *at):
            return [p[at] for p in parts]

        with nc.Block() as block:
            @block.sync
            def _(sp):
                sp.dma_start(b1r[:, :], dram["L1_ffn_b1"].rearrange("(m p) -> m p", p=P)).then_inc(f["w_in"], 16)
                sp.dma_start(b2q[:, :], dram["L1_ffn_b2"].partition_broadcast(P)).then_inc(f["w_in"], 16)

            @block.gpsimd
            def _(pool):
                def fetch(t):
                    b, half = divmod(t, TPB)
                    at = back[:, half, 0, b:b + 1].bitcast(U32)
                    nc.gpsimd.indirect_dma_start(yrow[:, t, :], None, ybuf[:, :], bass.IndirectOffsetOnAxis(at, 0)).then_inc(gath[t], 16)

                nc.gpsimd.indirect_dma_start(xcls[:, :], None, ybuf[:, :], bass.IndirectOffsetOnAxis(back_cls[:, 0:1].bitcast(U32), 0)).then_inc(gath[NT], 16)
                for t in range(2 * TPB):
                    fetch(t)
                nc.gpsimd.memset(nh2[:, :], -0.5).then_inc(g["nh"], 1)
                pool.wait_ge(g["nh"], 1)
                pool.wait_ge(g["aggrc"], 1)
                nc.gpsimd.tensor_scalar(varc2[:, :], mvc2[:, 1:2], EPS, None, ALU.add).then_inc(g["var"], 1)
                pool.wait_ge(g["var"], 1)
                nc.gpsimd.tensor_tensor(rstdc2[:, :], varc2[:, :], nh2[0:B, 0:1], ALU.pow).then_inc(g["rstd"], 1)

                def deviations(n, t0, t1):
                    pool.wait_ge(g["aggr"], t1)
                    nc.gpsimd.tensor_scalar(var2[:, t0:t1], mv2[:, t0:t1, 1], EPS, None, ALU.add).then_inc(g["var"], 1)
                    pool.wait_ge(g["var"], n)
                    nc.gpsimd.tensor_tensor(rstd2[:, t0:t1], var2[:, t0:t1], nh2[:, t0:t1], ALU.pow).then_inc(g["rstd"], 1)

                nc.gpsimd.tensor_copy(pick[0][:, :], mat("ident", B)[:, 0:1].broadcast_to([B, P])).then_inc(s["pick"], 1)
                deviations(2, 0, TPB)
                for t in range(2 * TPB, NT):
                    fetch(t)
                nc.gpsimd.tensor_tensor(hcb2[:, :], hcls[:, :], bo1[0:B, :], ALU.add).then_inc(g["hcb"], 1)
                deviations(3, TPB, 2 * TPB)
                pool.wait_ge(g["xctl"], 2)
                nc.gpsimd.tensor_copy(x2h[1][:, :, POS:EVEN], x2cth[:, :, 0:1])
                nc.gpsimd.tensor_copy(x2l[1][:, :, POS:EVEN], x2ctl[:, :, 0:1])

                def cls_column(b, slot):
                    nc.gpsimd.tensor_copy(x2h[slot][:, :, 0:1], x2cth[:, :, bass.ds(b, 1)])
                    nc.gpsimd.tensor_copy(x2l[slot][:, :, 0:1], x2ctl[:, :, bass.ds(b, 1)]).then_inc(s["x2c"], 1)
                    nc.gpsimd.tensor_copy(pick[slot][:, :], mat("ident", B)[:, bass.ds(b, 1)].broadcast_to([B, P])).then_inc(s["pick"], 1)

                def image(b, slot, first, last):
                    if not last:
                        if not first:
                            pool.wait_ge(s["vc_ps"], b)
                        cls_column(b + 1, 1 - slot)
                    pool.wait_ge(s["xn2"], b + 1)
                    nc.gpsimd.tensor_tensor(hrow[:, tiles(b), :], hrow[:, tiles(b), :], rep(bo1[:, :], 1, TPB), ALU.add).then_inc(s["hb"], 1)
                    if first:
                        deviations(4, 2 * TPB, NT)
                    if last:
                        nc.gpsimd.memset(nh3[:, :], -0.5).then_inc(f["shift"], 1)
                        nc.gpsimd.memset(shift[:, 0:1], -ROUND).then_inc(f["shift"], 1)
                        nc.gpsimd.memset(shift[:, 1:2], STEP - ROUND).then_inc(f["shift"], 1)
                        pool.wait_ge(f["shift"], 3)
                        deviations3(pool, 0)
                        pool.wait_ge(f["aggrc"], 1)
                        nc.gpsimd.tensor_scalar(varc3[:, :], mvc3[:, 1:2], EPS, None, ALU.add).then_inc(f["varc"], 1)
                        pool.wait_ge(f["varc"], 1)
                        nc.gpsimd.tensor_tensor(rstdc3[:, :], varc3[:, :], nh3[0:B, 0:1], ALU.pow).then_inc(f["rstdc"], 1)
                        pool.wait_ge(f["w_high"], 2)
                        low_part(nc.gpsimd, w1[:, :, :], up_w[0], up_w[1]).then_inc(f["w_low"], 1)
                        deviations3(pool, 1)
                    pool.wait_ge(s["p_done"], H1 * b + H1)
                    pool.wait_ge(s["vc"], b + 1)
                    if not first:
                        pool.wait_ge(s["ot_ps"], TPB * b)
                    for t in range(TPB):
                        nc.gpsimd.tensor_tensor(osb[:, t, :].rearrange("p (h d) -> p h d", h=H1), vcls[slot][:, :].rearrange("p (h d) -> p h d", h=H1),
                                                rep(prob[:, :, tile_at[t]], 2, HD1), ALU.mult).then_inc(s["o_tmp"], 1)
                    pool.wait_ge(s["inv"], b + 1)
                    for t in range(TPB):
                        pool.wait_ge(s["o_add"], TPB * b + t + 1)
                        o = osb[:, t, :].rearrange("p (h d) -> p h d", h=H1)
                        nc.gpsimd.tensor_tensor(o, o, rep(inv[:, t, :], 2, HD1), ALU.mult).then_inc(s["o_fin"], 1)

                per_image(pool, image)

            @block.vector
            def _(dve):
                def norm2(b, slot):
                    for t in range(TPB):
                        at = bass.ds(b * TPB + t, 1)
                        ins = nc.vector.tensor_scalar(xn2[slot][:, t, :], hrow[:, at, :].rearrange("p o d -> p (o d)"),
                                                      mv2[:, at, 0:1].rearrange("p o d -> p (o d)"), rstd2[:, at], ALU.subtract, ALU.mult)
                    ins.then_inc(s["xn2"], 1)

                def rows_low(b, slot):
                    dve.wait_ge(s["x2h"], b + 1)
                    low_part(nc.vector, bank[0][:, :].rearrange("p (k n) -> p k n", k=KD), x2h[slot][:, :, 1:POS], x2l[slot][:, :, 1:POS]).then_inc(s["x2l"], 1)

                def out_low(b, t):
                    dve.wait_ge(s["oth"], TPB * b + t + 1)
                    low_part(nc.vector, bank[0][:, :].rearrange("p (c n) -> p c n", c=KI), oth[:, :, P * t:P * t + P], otl[:, :, P * t:P * t + P]).then_inc(s["ot"], 1)

                def even_unit(b, slot, u):
                    dve.wait_ge(s["qk_ps"], UNITS * b + u + 1)
                    if u < 2 * KI:
                        nc.vector.tensor_copy(qk[slot][:, u, :], kvbank[:, 0, 0:POS]).then_inc(s["even_out"], 1)
                    else:
                        nc.vector.tensor_copy(vrow[slot][:, u - 2 * KI, :], kvbank[:, 0, :]).then_inc(s["even_out"], 1)

                def scores(b, h, first):
                    used = [] if first and h < 2 else [(s["p_done"], H1 * b + h - 1)]
                    waits_apart(dve, (s["s_ps"], H1 * b + h + 1), *used)
                    for t in range(TPB):
                        at, n = tile_at[t], 1 + P * (t + 1)
                        ins = nc.vector.tensor_tensor_reduce(sx[h % 2][:, at:at + n], bank[1 + h % 2][:, at:at + n], toeplitz[:, h, at:at + n],
                                                             -0.125, 3e38, ALU.add, ALU.min, low[:, h % 2, t:t + 1])
                    ins.then_inc(s["smax"], 1)

                def take(t):
                    dve.wait_ge(gath[t], 16)
                    nc.vector.scalar_tensor_tensor(hrow[:, t, :], yrow[:, t, :], back[:, t % TPB, 1, t // TPB:t // TPB + 1], hrow[:, t, :], ALU.mult, ALU.add).then_inc(g["h2"], 1)
                    dve.wait_ge(g["h2"], t + 1)
                    nc.vector.bn_stats(stat2[:, t, :], hrow[:, t, :]).then_inc(g["stat"], 1)
                    dve.wait_ge(g["stat"], t + 1)
                    nc.vector.bn_aggr(mv2[:, t, :], stat2[:, t, :]).then_inc(g["aggr"], 1)

                dve.wait_ge(gath[NT], 16)
                nc.vector.scalar_tensor_tensor(hcls[:, :], xcls[:, :], back_cls[:, 1:2], hcls[:, :], ALU.mult, ALU.add).then_inc(g["h2c"], 1)
                dve.wait_ge(g["h2c"], 1)
                nc.vector.bn_stats(stat2[0:B, NT, :], hcls[:, :]).then_inc(g["statc"], 1)
                dve.wait_ge(g["statc"], 1)
                nc.vector.bn_aggr(mvc2[:, :], stat2[0:B, NT, :]).then_inc(g["aggrc"], 1)
                for t in range(TPB):
                    take(t)
                dve.wait_ge(g["rstd"], 1)
                dve.wait_ge(g["aggrc"], 1)
                nc.vector.tensor_scalar(xc2[:, :], hcls[:, :], mvc2[:, 0:1], rstdc2[:, 0:1], ALU.subtract, ALU.mult).then_inc(g["xc"], 1)
                dve.wait_ge(g["rstd"], 2)
                dve.wait_ge(g["aggr"], TPB)
                norm2(0, 0)
                dve.wait_ge(g["xct"], 2)
                turned = bank[1][:, 0:KD * B].rearrange("p (k b) -> p k b", k=KD)
                low_part(nc.vector, turned, x2cth[:, :, :], x2ctl[:, :, :]).then_inc(g["xctl"], 1)
                for at in (POS, 0):
                    ins = low_part(nc.vector, turned[:, :, 0:1], x2h[0][:, :, at:at + 1], x2l[0][:, :, at:at + 1])
                ins.then_inc(g["xctl"], 1)
                rows_low(0, 0)
                for u in range(0, H1, 2):
                    if u < 4:
                        take(TPB + u // 2)
                    even_unit(0, 0, u)
                    if u == 2:
                        dve.wait_ge(g["och"], 1)
                        low_part(nc.vector, oc[:, :], och[:, :], ocl[:, :]).then_inc(g["ocl"], 1)
                dve.wait_ge(g["oo_ps"], 1)
                dve.wait_ge(g["hcb"], 1)
                dve.wait_ge(g["xc"], 1)
                nc.vector.tensor_tensor(hcls[:, :], bank[5][0:B, 0:D], hcb2[:, :], ALU.add).then_inc(g["hcls"], 1)
                dve.wait_ge(g["rstd"], 3)
                dve.wait_ge(g["aggr"], 2 * TPB)

                def beside_last(h):
                    if h == 0:
                        statistics3(dve, 0)
                        nc.vector.bn_stats(statc3[:, :], hcls[:, :]).then_inc(f["statc"], 1)
                        dve.wait_ge(f["statc"], 1)
                        nc.vector.bn_aggr(mvc3[:, :], statc3[:, :]).then_inc(f["aggrc"], 1)
                    elif h == 2:
                        normalise3(dve, 0)
                        dve.wait_ge(f["rstdc"], 1)
                        dve.wait_ge(f["aggrc"], 1)
                        nc.vector.tensor_scalar(xc3[:, :], hcls[:, :], mvc3[:, 0:1], rstdc3[:, 0:1], ALU.subtract, ALU.mult).then_inc(f["xc"], 1)
                    elif h == 4:
                        statistics3(dve, 1)
                    elif h == 5:
                        rows_low3(dve, 0)
                    elif h == 6:
                        normalise3(dve, 1)
                    elif h == 7:
                        dve.wait_ge(f["b1_ps"], 1)
                        nc.vector.tensor_copy(b1q[:, :], kvbank[:, 1, 0:KF]).then_inc(f["b1"], 1)
                        dve.wait_ge(f["xch"], 1)
                        low_part(nc.vector, kvbank[:, 0, 0:KD * B].rearrange("p (k b) -> p k b", k=KD), x3ch[:, :, :], x3cl[:, :, :]).then_inc(f["xcl"], 1)

                def image(b, slot, first, last):
                    if not first and not last:
                        dve.wait_ge(s["x2t_ps"], b)
                    scores(b, 0, first)
                    if not last:
                        norm2(b + 1, 1 - slot)
                    scores(b, 1, first)
                    even_unit(b, slot, H1)
                    if not last:
                        rows_low(b + 1, 1 - slot)
                    for h in range(H1):
                        if h + 2 < H1:
                            scores(b, h + 2, first)
                        if h % 2 == 0 and not last:
                            even_unit(b + 1, 1 - slot, h)
                        if last:
                            beside_last(h)
                        if first:
                            for t in range(2 * TPB + 2 * h, min(2 * TPB + 2 * h + 2, NT)):
                                take(t)
                        if h < TPB and not first:
                            out_low(b - 1, h)
                        dve.wait_ge(s["pt_ps"], H1 * b + h + 1)
                        if not (first and h < 2):
                            dve.wait_ge(s["pv"], H1 * b + h - 1)
                        nc.vector.tensor_copy(pt[h % 2][:, :], bank[3][:, 0:3 * P]).then_inc(s["pt"], 1)
                        if h == 3 and not first:
                            dve.wait_ge(s["wo_ps"], b)
                            dve.wait_ge(s["hb"], b)
                            nc.vector.tensor_tensor(hrow[:, tiles(b - 1), :], bank[0][:, :].rearrange("p (t d) -> p t d", t=TPB),
                                                    hrow[:, tiles(b - 1), :], ALU.add).then_inc(s["h_done"], 1)
                    dve.wait_ge(s["p_done"], H1 * b + H1)
                    if not first:
                        dve.wait_ge(s["o_fin"], TPB * b)
                    nc.vector.reciprocal(inv[:, :, :], total[slot][:, :, :]).then_inc(s["inv"], 1)
                    if first:
                        dve.wait_ge(g["rstd"], 4)
                        dve.wait_ge(g["aggr"], NT)
                    dve.wait_ge(s["pv"], H1 * b + H1)
                    for t in range(TPB):
                        dve.wait_ge(s["o_tmp"], TPB * b + t + 1)
                        nc.vector.tensor_tensor(osb[:, t, :], bank[4 + t][:, :], osb[:, t, :], ALU.add).then_inc(s["o_add"], 1)

                per_image(dve, image)
                for t in range(TPB):
                    out_low(B - 1, t)
                dve.wait_ge(s["wo_ps"], B)
                dve.wait_ge(s["hb"], B)
                nc.vector.tensor_tensor(hrow[:, tiles(B - 1), :], bank[0][:, :].rearrange("p (t d) -> p t d", t=TPB),
                                        hrow[:, tiles(B - 1), :], ALU.add).then_inc(s["h_done"], 1)

            @block.scalar
            def _(act):
                def rows_t(b, slot, early):
                    act.wait_ge(s["x2t_ps"], b + 1)
                    if not early:
                        act.wait_ge(s["vc_ps"], b - 1)
                    nc.scalar.copy(x2h[slot][:, :, 1:POS], bank[0][:, :].rearrange("p (k n) -> p k n", k=KD)).then_inc(s["x2h"], 1)

                def odd_unit(b, slot, u):
                    act.wait_ge(s["qk_ps"], UNITS * b + u + 1)
                    if u < 2 * KI:
                        nc.scalar.copy(qk[slot][:, u, :], kvbank[:, 1, 0:POS]).then_inc(s["odd_out"], 1)
                    else:
                        nc.scalar.copy(vrow[slot][:, u - 2 * KI, :], kvbank[:, 1, :]).then_inc(s["odd_out"], 1)

                def cls_v(b, slot):
                    act.wait_ge(s["vc_ps"], b + 1)
                    nc.scalar.copy(vcls[slot][:, :], bank[0][:, :]).then_inc(s["vc"], 1)

                def out_t(b, t):
                    act.wait_ge(s["ot_ps"], TPB * b + t + 1)
                    nc.scalar.copy(oth[:, :, P * t:P * t + P], bank[0][:, :].rearrange("p (c n) -> p c n", c=KI)).then_inc(s["oth"], 1)

                act.wait_ge(g["xct_ps"], 1)
                turned = bank[1][:, 0:KD * B].rearrange("p (k b) -> p k b", k=KD)
                high(nc.scalar, turned, x2cth[:, :, :]).then_inc(g["xct"], 1)
                for at in (POS, 0):
                    ins = high(nc.scalar, turned[:, :, 0:1], x2h[0][:, :, at:at + 1])
                ins.then_inc(g["xct"], 1)
                rows_t(0, 0, True)
                odd_unit(0, 0, 1)
                odd_unit(0, 0, 3)
                act.wait_ge(g["oc_ps"], 1)
                nc.scalar.copy(oc[:, :], bank[3][0:B, :]).then_inc(g["oc"], 1)
                high(nc.scalar, bank[3][0:B, :], och[:, :]).then_inc(g["och"], 1)
                odd_unit(0, 0, 5)
                act.wait_ge(g["oct_ps"], 1)
                nc.scalar.copy(oct_[:, :, :], bank[4][:, 0:KI * B].rearrange("p (k b) -> p k b", k=KI)).then_inc(g["oct"], 1)
                odd_unit(0, 0, 7)
                cls_v(0, 0)

                def image(b, slot, first, last):
                    for h in range(H1):
                        act.wait_ge(s["smax"], H1 * b + h + 1)
                        if h == 0 and not first:
                            act.wait_ge(s["pt_ps"], H1 * b)
                            act.wait_ge(s["o_tmp"], TPB * b)
                            act.wait_ge(s["inv"], b)
                        for t in range(TPB):
                            at, n = tile_at[t], 1 + P * (t + 1)
                            ins = nc.scalar.activation(prob[:, h, at:at + n], sx[h % 2][:, at:at + n], ACT.Exp, bias=low[:, h % 2, t:t + 1],
                                                       scale=-1.0, accum_out=total[slot][:, t, h:h + 1])
                        ins.then_inc(s["p_done"], 1)
                        if h == 0:
                            odd_unit(b, slot, H1 + 1)
                            if not last:
                                rows_t(b + 1, 1 - slot, first)
                        if h < TPB and not first:
                            out_t(b - 1, h)
                        if h % 2 == 1 and not last:
                            odd_unit(b + 1, 1 - slot, h)
                        if last and h in (1, 2):
                            act.wait_ge(w1_in, 16 * (E + 1))
                            high(nc.scalar, w1[:, h - 1, :], up_w[0][:, h - 1, :]).then_inc(f["w_high"], 1)
                        if last and h == 4:
                            rows_high3(act, 0)
                        if last and h == 6:
                            act.wait_ge(f["xc_ps"], 1)
                            high(nc.scalar, kvbank[:, 0, 0:KD * B].rearrange("p (k b) -> p k b", k=KD), x3ch[:, :, :]).then_inc(f["xch"], 1)
                    if not last:
                        cls_v(b + 1, 1 - slot)

                per_image(act, image)
                for t in range(TPB):
                    out_t(B - 1, t)

            @block.tensor
            def _(pe):
                def turn_rows(b, slot):
                    pe.wait_ge(s["xn2"], b + 1)
                    for k in range(KD):
                        for t in range(TPB):
                            ins = nc.tensor.transpose(bank[0][:, ROWS * k + P * t:ROWS * k + P * t + P], xn2[slot][:, t, P * k:P * k + P], ident)
                    ins.then_inc(s["x2t_ps"], 1)

                def unit(b, slot, u, early):
                    if not (early and u < 2):
                        pe.wait_ge(s["odd_out" if u % 2 else "even_out"], HALF * b + u // 2)
                    for k in range(KD):
                        x = (x2h[slot], x2l[slot])
                        if u < 2 * KI:
                            m = u % KI
                            w = both(wq if u < KI else wkv, slice(0, P), k, slice(P * m, P * m + P))
                            ins = product(kvbank[:, u % 2, 0:EVEN], w, both(x, slice(0, P), k, slice(0, EVEN)), k == 0, k == KD - 1)
                        else:
                            at = 1 + P * (u - 2 * KI)
                            ins = product(kvbank[:, u % 2, :], both(x, slice(0, P), k, slice(at, at + P)),
                                          both(wkv, slice(0, P), k, slice(INNER, 2 * INNER)), k == 0, k == KD - 1)
                    ins.then_inc(s["qk_ps"], 1)

                def cls_v(b, slot):
                    nc.tensor.matmul(bank[0][:, :], pick[slot][:, :], ocl[:, :], start=True, stop=False)
                    nc.tensor.matmul(bank[0][:, :], pick[slot][:, :], och[:, :], start=False, stop=True).then_inc(s["vc_ps"], 1)

                def scores(b, slot, h, first):
                    if not (first and h < 2):
                        pe.wait_ge(s["smax"], H1 * b + h - 1)
                    rows = slice(HD1 * (h % 2), HD1 * (h % 2) + HD1)
                    for t in range(TPB):
                        at, n = tile_at[t], 1 + P * (t + 1)
                        ins = nc.tensor.matmul(bank[1 + h % 2][:, at:at + n], qk[slot][rows, h // 2, 1 + P * t:1 + P * t + P],
                                               qk[slot][rows, KI + h // 2, 0:n], start=True, stop=True)
                    ins.then_inc(s["s_ps"], 1)

                def turn_probs(b, h, first):
                    pe.wait_ge(s["p_done"], H1 * b + h + 1)
                    if not (first and h == 0):
                        pe.wait_ge(s["pt"], H1 * b + h)
                    for i, at in enumerate((1, 2 + P, 2 + 2 * P)):
                        ins = nc.tensor.transpose(bank[3][:, P * i:P * i + P], prob[:, h, at:at + P], ident)
                    ins.then_inc(s["pt_ps"], 1)

                def weighted(b, slot, h):
                    pe.wait_ge(s["pt"], H1 * b + h + 1)
                    cols = slice(HD1 * h, HD1 * h + HD1)
                    nc.tensor.matmul(bank[4][:, cols], pt[h % 2][:, 0:P], vrow[slot][:, 0, cols], start=True, stop=True)
                    nc.tensor.matmul(bank[5][:, cols], pt[h % 2][:, P:2 * P], vrow[slot][:, 0, cols], start=True, stop=False)
                    nc.tensor.matmul(bank[5][:, cols], pt[h % 2][:, 2 * P:3 * P], vrow[slot][:, 1, cols], start=False, stop=True).then_inc(s["pv"], 1)

                def turn_out(b, t):
                    pe.wait_ge(s["o_fin"], TPB * b + t + 1)
                    for c in range(KI):
                        ins = nc.tensor.transpose(bank[0][:, P * c:P * c + P], osb[:, t, P * c:P * c + P], ident)
                    ins.then_inc(s["ot_ps"], 1)

                def project(b):
                    pe.wait_ge(s["ot"], TPB * b + TPB)
                    for t in range(TPB):
                        for c in range(KI):
                            cols = slice(INNER // 2 * (c % 2), INNER // 2 * (c % 2) + D)
                            ins = product(bank[0][:, D * t:D * t + D], both((oth, otl), slice(0, P), c, slice(P * t, P * t + P)),
                                          both(wo, slice(0, P), c // 2, cols), c == 0, c == KI - 1)
                    ins.then_inc(s["wo_ps"], 1)

                pe.wait_ge(g["xc"], 1)
                for k in range(KD):
                    ins = nc.tensor.transpose(bank[1][:, B * k:B * k + B], xc2[:, P * k:P * k + P], mat("ident", B)[:, 0:B])
                ins.then_inc(g["xct_ps"], 1)
                turn_rows(0, 0)
                pe.wait_ge(l1_in, 16 * 4)
                pe.wait_ge(l1_low, 3)
                pe.wait_ge(g["xctl"], 2)
                pe.wait_ge(s["x2l"], 1)
                for u in range(H1):
                    unit(0, 0, u, True)
                    if u == 2:
                        for k in range(KD):
                            ins = product(bank[3][0:B, :], both((x2cth, x2ctl), slice(0, P), k, slice(0, B)),
                                          both(wkv, slice(0, P), k, slice(INNER, 2 * INNER)), k == 0, k == KD - 1)
                        ins.then_inc(g["oc_ps"], 1)
                    if u == 5:
                        pe.wait_ge(g["oc"], 1)
                        for k in range(KI):
                            ins = nc.tensor.transpose(bank[4][:, B * k:B * k + B], oc[:, P * k:P * k + P], mat("ident", B)[:, 0:B])
                        ins.then_inc(g["oct_ps"], 1)
                pe.wait_ge(g["oct"], 1)
                for k in range(KI):
                    ins = nc.tensor.matmul(bank[5][0:B, 0:D], oct_[:, k, :], wo1[:, k, :], start=(k == 0), stop=(k == KI - 1))
                ins.then_inc(g["oo_ps"], 1)
                pe.wait_ge(g["ocl"], 1)
                pe.wait_ge(s["pick"], 1)
                cls_v(0, 0)

                def image(b, slot, first, last):
                    pe.wait_ge(s["even_out"], HALF * b + KI)
                    pe.wait_ge(s["odd_out"], HALF * b + KI)
                    scores(b, slot, 0, first)
                    scores(b, slot, 1, first)
                    for u in range(H1, UNITS):
                        unit(b, slot, u, False)
                    if not last:
                        pe.wait_ge(s["vc"], b + 1)
                        turn_rows(b + 1, 1 - slot)
                    for h in range(H1):
                        if h + 2 < H1:
                            scores(b, slot, h + 2, first)
                        if not last:
                            if h == 0:
                                pe.wait_ge(s["x2l"], b + 2)
                                pe.wait_ge(s["x2c"], b + 1)
                            unit(b + 1, 1 - slot, h, False)
                        if h < TPB and not first:
                            if h > 0 or last:
                                pe.wait_ge(s["ot" if h else "vc"], TPB * b - TPB + 1 if h else b + 1)
                            turn_out(b - 1, h)
                        turn_probs(b, h, first)
                        if h == 0:
                            pe.wait_ge(s["even_out"], HALF * b + HALF)
                            pe.wait_ge(s["odd_out"], HALF * b + HALF)
                            if not first:
                                pe.wait_ge(s["o_add"], TPB * b)
                        else:
                            weighted(b, slot, h - 1)
                        if h == 2 and not first:
                            project(b - 1)
                        if last and h == 3:
                            turn_rows3(pe, 0)
                        if last and h == 6:
                            pe.wait_ge(f["xl"], 1)
                            pe.wait_ge(f["w_in"], 32)
                            nc.tensor.transpose(kvbank[:, 1, 0:KF], b1r[:, :], mat("ident", KF)[:, 0:KF]).then_inc(f["b1_ps"], 1)
                            pe.wait_ge(f["xc"], 1)
                            for k in range(KD):
                                ins = nc.tensor.transpose(kvbank[:, 0, B * k:B * k + B], xc3[:, P * k:P * k + P], mat("ident", B)[:, 0:B])
                            ins.then_inc(f["xc_ps"], 1)
                    if not last:
                        if not first:
                            pe.wait_ge(s["h_done"], b)
                        pe.wait_ge(s["pick"], b + 2)
                        cls_v(b + 1, 1 - slot)
                    weighted(b, slot, H1 - 1)

                per_image(pe, image)
                pe.wait_ge(s["h_done"], B - 1)
                for t in range(TPB):
                    if t:
                        pe.wait_ge(s["ot"], TPB * B - 1)
                    turn_out(B - 1, t)
                project(B - 1)
        scope.close()

        scope = ExitStack()
        x3h.append(sb("x3h_1", [P, KD, W], F32R, scope=scope))
        x3l.append(sb("x3l_1", [P, KD, W], F32R, scope=scope))
        SLOT = 3
        hq = [sb(f"hq_{i}", [P, W], scope=scope) for i in range(SLOT)]
        knot = [sb(f"knot_{i}", [P, W], scope=scope) for i in range(SLOT)]
        gl = [sb(f"gl_{i}", [P, W], scope=scope) for i in range(SLOT)]
        gr = [sb(f"gr_{i}", [P, W], scope=scope) for i in range(SLOT)]
        frac = [sb(f"frac_{i}", [P, W], scope=scope) for i in range(SLOT)]
        yt = [sb(f"yt_{i}", [P, KF, W], scope=scope) for i in range(2)]
        ytc = sb("ytc", [P, KF, B], scope=scope)
        z = [sb(f"z_{i}", [P, TPB, D], scope=scope) for i in range(2)]
        zc = sb("zc", [B, D], scope=scope)
        s = f
        N_CHUNK = NP * KF + 1

        CLS_AT = 3
        LAG = 6

        def chunk_cols(c):
            return slice(0, W) if c < NP * KF else slice(0, KF * B)

        with nc.Block() as block:
            @block.sync
            def _(sp):
                for p in range(NP):
                    for i in range(2):
                        sp.wait_ge(s["h_out"], 2 * p + i + 1)
                        b = 2 * p + i
                        sp.dma_start(out[b, 1:POS, :].rearrange("(t p) d -> p t d", p=P), hrow[:, TPB * b:TPB * b + TPB, :]).then_inc(out_stored, 16)
                sp.wait_ge(s["h_out"], B + 1)
                sp.dma_start(out[:, 0, :], hcls[:, :]).then_inc(out_stored, 16)
                sp.wait_ge(out_stored, 16 * (B + 1))

            @block.gpsimd
            def _(pool):
                def chunk(c):
                    i, n = c % SLOT, chunk_cols(c)
                    pool.wait_ge(s["knot"], c + 1)
                    nc.gpsimd.tensor_tensor(frac[i][:, n], hq[i][:, n], knot[i][:, n], ALU.subtract).then_inc(s["frac"], 1)
                    pool.wait_ge(s["gl"], 2 * c + 2)
                    nc.gpsimd.tensor_tensor(gr[i][:, n], gr[i][:, n], gl[i][:, n], ALU.subtract).then_inc(s["rise"], 1)

                for p in range(NP):
                    for m in range(KF):
                        chunk(p * KF + m)
                        if m == 2 and p + 2 < NP:
                            deviations3(pool, p + 2)
                chunk(NP * KF)

            @block.vector
            def _(dve):
                def round_in(c):
                    i, n = c % SLOT, chunk_cols(c)
                    if c < NP * KF:
                        dve.wait_ge(s["h_ps"], c + 1)
                    if c >= SLOT:
                        dve.wait_ge(s["frac"], c + 1 - SLOT)
                    if c < NP * KF:
                        nc.vector.tensor_scalar(hq[i][:, n], kvbank[:, c % 2, :], b1q[:, c % KF:c % KF + 1], ROUND, ALU.add, ALU.add).then_inc(s["hq"], 1)
                    else:
                        dve.wait_ge(s["zc"], 1)
                        nc.vector.tensor_scalar(hq[i][:, n], ytc[:, :, :].rearrange("p m b -> p (m b)"), ROUND, None, ALU.add).then_inc(s["hq"], 1)

                def knots(c):
                    i, n = c % SLOT, chunk_cols(c)
                    dve.wait_ge(s["hq"], c + 1)
                    if c >= SLOT:
                        dve.wait_ge(s["gl"], 2 * (c + 1 - SLOT))
                    nc.vector.tensor_scalar(knot[i][:, n].bitcast(I32), hq[i][:, n].bitcast(I32), -64, None, ALU.bitwise_and).then_inc(s["knot"], 1)

                def slope(c):
                    i, n = c % SLOT, chunk_cols(c)
                    dve.wait_ge(s["frac"], c + 1)
                    dve.wait_ge(s["rise"], c + 1)
                    nc.vector.tensor_tensor(frac[i][:, n], frac[i][:, n], gr[i][:, n], ALU.mult).then_inc(s["y0"], 1)

                def interpolate(c):
                    i, n = c % SLOT, chunk_cols(c)
                    dve.wait_ge(s["y0"], c + 1)
                    nc.vector.scalar_tensor_tensor(gl[i][:, n], frac[i][:, n], 1.0 / STEP, gl[i][:, n], ALU.mult, ALU.add).then_inc(s["y1"], 1)

                def round_out(c):
                    i, n = c % SLOT, chunk_cols(c)
                    dve.wait_ge(s["y1"], c + 1)
                    if c < NP * KF:
                        p, m = divmod(c, KF)
                        if p >= 2 and m == 0:
                            dve.wait_ge(s["z_ps"], 2 * (p - 1))
                        to = yt[p % 2][:, m, :]
                    else:
                        to = ytc[:, :, :].rearrange("p m b -> p (m b)")
                    nc.vector.tensor_scalar(to, gl[i][:, n], ROUND, -ROUND, ALU.add, ALU.add).then_inc(s["y"], 1)

                def take_down(p):
                    for i in range(2):
                        n = 2 * p + i
                        dve.wait_ge(s["z_ps"], n + 1)
                        if n >= 2:
                            dve.wait_ge(s["h_out"], n - 1)
                        for t in range(TPB):
                            ins = nc.vector.tensor_tensor(z[i][:, t, :], bank[2 + TPB * i + t][:, 0:D], b2q[:, :], ALU.add)
                        ins.then_inc(s["z"], 1)

                def store(p, i):
                    at = TPB * (2 * p + i)
                    n = 2 * p + i
                    dve.wait_ge(s["z"], n + 1)
                    nc.vector.tensor_scalar(z[i][:, :, :], z[i][:, :, :], ROUND, -ROUND, ALU.add, ALU.add).then_inc(s["zr"], 1)
                    dve.wait_ge(s["zr"], n + 1)
                    nc.vector.tensor_tensor(hrow[:, at:at + TPB, :], hrow[:, at:at + TPB, :], z[i][:, :, :], ALU.add).then_inc(s["h_out"], 1)

                TAKE = 4
                for c in range(N_CHUNK + SLOT):
                    if c < N_CHUNK:
                        round_in(c)
                    if c >= SLOT:
                        round_out(c - SLOT)
                    if 2 <= c < N_CHUNK + 2:
                        slope(c - 2)
                    if c < N_CHUNK:
                        knots(c)
                    if 2 <= c < N_CHUNK + 2:
                        interpolate(c - 2)
                    if c == CLS_AT + 1:
                        dve.wait_ge(s["hc_ps"], 1)
                        nc.vector.tensor_tensor(ytc[:, :, :], bank[5][:, 0:KF * B].rearrange("p (m b) -> p m b", b=B), rep(b1q[:, :], 2, B), ALU.add).then_inc(s["zc"], 1)
                    if c < NP * KF:
                        p, m = divmod(c, KF)
                        if m == 1 and p + 1 < NP:
                            rows_low3(dve, p + 1)
                        if m == 2 and p + 2 < NP:
                            statistics3(dve, p + 2)
                        if m == TAKE and p:
                            take_down(p - 1)
                        if m in (TAKE + 1, TAKE + 2) and p:
                            store(p - 1, m - TAKE - 1)
                        if m == 5 and p + 2 < NP:
                            normalise3(dve, p + 2)
                take_down(NP - 1)
                for i in range(2):
                    store(NP - 1, i)
                dve.wait_ge(s["zc_ps"], 1)
                nc.vector.tensor_tensor(zc[:, :], bank[0][0:B, 0:D], b2q[0:B, :], ALU.add).then_inc(s["zc"], 1)
                dve.wait_ge(s["zc"], 2)
                nc.vector.tensor_scalar(zc[:, :], zc[:, :], ROUND, -ROUND, ALU.add, ALU.add).then_inc(s["zc"], 1)
                dve.wait_ge(s["zc"], 3)
                nc.vector.tensor_tensor(hcls[:, :], hcls[:, :], zc[:, :], ALU.add).then_inc(s["h_out"], 1)

            @block.scalar
            def _(act):
                for c in range(N_CHUNK):
                    i, n = c % SLOT, chunk_cols(c)
                    act.wait_ge(s["knot"], c + 1)
                    if c >= SLOT:
                        act.wait_ge(s["y"], c + 1 - SLOT)
                    nc.scalar.activation(gl[i][:, n], knot[i][:, n], ACT.Gelu, bias=shift[:, 0:1]).then_inc(s["gl"], 1)
                    nc.scalar.activation(gr[i][:, n], knot[i][:, n], ACT.Gelu, bias=shift[:, 1:2]).then_inc(s["gl"], 1)
                    if c % KF == 0 and c // KF + 1 < NP:
                        rows_high3(act, c // KF + 1)

            @block.tensor
            def _(pe):
                def up(c):
                    p, m = divmod(c, KF)
                    if m == 0:
                        pe.wait_ge(s["xl"], p + 1)
                    if c >= 2:
                        pe.wait_ge(s["hq"], c - 1)
                    for k in range(KD):
                        ins = product(kvbank[:, c % 2, :], both(up_w, slice(0, P), k, slice(P * m, P * m + P)),
                                      both((x3h[p % 2], x3l[p % 2]), slice(0, P), k, slice(0, W)), k == 0, k == KD - 1)
                    ins.then_inc(s["h_ps"], 1)

                def up_cls():
                    for m in range(KF):
                        for k in range(KD):
                            ins = product(bank[5][:, B * m:B * m + B], both(up_w, slice(0, P), k, slice(P * m, P * m + P)),
                                          both((x3ch, x3cl), slice(0, P), k, slice(0, B)), k == 0, k == KD - 1)
                    ins.then_inc(s["hc_ps"], 1)

                def down(c):
                    p, m = divmod(c, KF)
                    if m == 0 and p:
                        pe.wait_ge(s["z"], 2 * p)
                    if c == 0:
                        pe.wait_ge(s["zc"], 1)
                    pe.wait_ge(s["y"], c + 1)
                    for t in range(TP):
                        ins = nc.tensor.matmul(bank[2 + t][:, 0:D], yt[p % 2][:, m, P * t:P * t + P], w2[:, m, :], start=(m == 0), stop=(m == KF - 1))
                        if m == KF - 1 and t % TPB == TPB - 1:
                            ins.then_inc(s["z_ps"], 1)

                pe.wait_ge(w2_in, 16 * (E + 1))
                for c in range(NP * KF + LAG):
                    if c < NP * KF:
                        up(c)
                        if c % KF == 0 and c // KF + 1 < NP:
                            turn_rows3(pe, c // KF + 1)
                    if c == CLS_AT:
                        up_cls()
                    if c >= LAG:
                        down(c - LAG)
                pe.wait_ge(s["y"], N_CHUNK)
                for m in range(KF):
                    ins = nc.tensor.matmul(bank[0][0:B, 0:D], ytc[:, m, :], w2[:, m, :], start=(m == 0), stop=(m == KF - 1))
                ins.then_inc(s["zc_ps"], 1)
        scope.close()


_OUT = (B, POS, D)


def kernel(**inputs):
    import numpy as _np
    import concourse.bacc as _bacc
    from concourse import mybir as _mybir
    from concourse.bass_utils import run_bass_kernel_spmd as _run

    nc = _bacc.Bacc("TRN2", target_bir_lowering=False, num_devices=1)
    arrays, dram = {}, {}
    for name, a in [*inputs.items(), *_shape_constants().items()]:
        a = _np.ascontiguousarray(a)
        arrays[f"in_{name}"] = a
        dram[name] = nc.dram_tensor(f"in_{name}", a.shape, _mybir.dt.from_np(a.dtype), kind="ExternalInput").ap()
    out = nc.dram_tensor("out_0", _OUT, _mybir.dt.float32, kind="ExternalOutput").ap()
    vit_tower_kernel(nc, dram, out)
    r = _run(nc, [arrays], core_ids=[0])
    return r.results[0]["out_0"]
```
